# Optimizing a Trainium2 kernel written in Bass

```python
import numpy as np
import jax
import jax.numpy as jnp

def _softmax(x, axis=-1):
    return jax.nn.softmax(x, axis=axis)

def _gelu(x):
    return jax.nn.gelu(x, approximate=True)

def _silu(x):
    return jax.nn.silu(x)

def _sigmoid(x):
    return jax.nn.sigmoid(x)

def _layernorm(x, axis=-1, eps=1e-05):
    m = jnp.mean(x, axis=axis, keepdims=True)
    v = jnp.var(x, axis=axis, keepdims=True)
    return (x - m) / jnp.sqrt(v + eps)

def _scatter_add(tgt, idx, src, axis=0):
    return tgt.at[idx].add(src)

def _segment_sum(src, seg, n):
    return jax.ops.segment_sum(src, seg, n)
kernel_name = 'mk_xattn_seq_d2_seqx_r4_08a0d3'

def setup_inputs(seed: int=0):
    np.random.seed(seed)
    _w = jnp.asarray

    def _rec_inputs():
        import jax
        import jax.numpy as jnp
        _rk = jax.random.key(seed)
        x = -0.0002928 + 1 * jax.random.normal(jax.random.fold_in(_rk, 1), (16, 512, 256), jnp.float32)
        _lenS = 512 - jax.random.randint(jax.random.fold_in(_rk, 7), (16,), 0, max(1, 512 // 4) + 1, jnp.int32)
        _lenS2 = 64 - jax.random.randint(jax.random.fold_in(_rk, 8), (16,), 0, max(1, 64 // 4) + 1, jnp.int32)
        _ctx_768P = jax.random.normal(jax.random.fold_in(_rk, 11), (16, 16, 192), jnp.float32)
        _ctx_768c = jax.random.dirichlet(jax.random.fold_in(_rk, 511), 0.3 * jnp.ones((16,), jnp.float32), (16, 64))
        _ctx_768t = jnp.einsum('bsk,bkd->bsd', _ctx_768c, _ctx_768P)
        _ctx_768t = _ctx_768t * jax.lax.rsqrt(jnp.mean(jnp.square(_ctx_768t)) + 1e-12) * 0.953939
        ctx_768 = -0.00423632 + 0.9977 * (_ctx_768t + 0.3 * jax.random.normal(jax.random.fold_in(_rk, 611), (16, 64, 192), jnp.float32))
        return (x, ctx_768)
    x, ctx_768 = _rec_inputs()

    def _L0_xattn_setup():
        import jax, jax.numpy as jnp
        import numpy as np
        D, H, DFF, DC = (256, 16, 1024, 192)
        DH = D // H
        EPS = 1e-05

        def layer_norm(x, g, b):
            m = jnp.mean(x, axis=-1, keepdims=True)
            v = jnp.mean(jnp.square(x - m), axis=-1, keepdims=True)
            return (x - m) * jax.lax.rsqrt(v + EPS) * g + b

        def _self_attn(x, Wqkv, Wproj, bproj):
            B, T, _ = x.shape
            qkv = x @ Wqkv
            qkv = qkv.reshape(B, T, 3, H, DH)
            q, k, v = (qkv[:, :, i].transpose(0, 2, 1, 3) for i in range(3))
            scale = DH ** (-0.5)
            attn = jnp.einsum('bhtd,bhsd->bhts', q, k) * scale
            causal = jnp.triu(jnp.ones((T, T), bool), k=1)
            attn = jnp.where(causal, -jnp.inf, attn)
            attn = jax.nn.softmax(attn, axis=-1)
            out = jnp.einsum('bhts,bhsd->bhtd', attn, v)
            out = out.transpose(0, 2, 1, 3).reshape(B, T, D)
            return out @ Wproj + bproj

        def _cross_attn(x, cond, Wq, Wkv, Wproj, bproj):
            B, T, _ = x.shape
            C = cond.shape[1]
            q = (x @ Wq).reshape(B, T, H, DH).transpose(0, 2, 1, 3)
            kv = (cond @ Wkv).reshape(B, C, 2, H, DH)
            k = kv[:, :, 0].transpose(0, 2, 1, 3)
            v = kv[:, :, 1].transpose(0, 2, 1, 3)
            scale = DH ** (-0.5)
            attn = jax.nn.softmax(jnp.einsum('bhtd,bhcd->bhtc', q, k) * scale, axis=-1)
            out = jnp.einsum('bhtc,bhcd->bhtd', attn, v)
            out = out.transpose(0, 2, 1, 3).reshape(B, T, D)
            return out @ Wproj + bproj
        key = jax.random.key(seed)
        ks = jax.random.split(key, 20)
        s = 0.02
        return {'x': jax.random.normal(ks[0], (2, 512, D), jnp.float32), 'cond': jax.random.normal(ks[1], (2, 77, DC), jnp.float32), 'Wqkv': jax.random.normal(ks[2], (D, 3 * D), jnp.float32) * s, 'Wproj_sa': jax.random.normal(ks[3], (D, D), jnp.float32) * s, 'bproj_sa': jnp.zeros((D,), jnp.float32), 'g1': jnp.ones((D,), jnp.float32), 'b1': jnp.zeros((D,), jnp.float32), 'Wq_ca': jax.random.normal(ks[4], (D, D), jnp.float32) * s, 'Wkv_ca': jax.random.normal(ks[5], (DC, 2 * D), jnp.float32) * s, 'Wproj_ca': jax.random.normal(ks[6], (D, D), jnp.float32) * s, 'bproj_ca': jnp.zeros((D,), jnp.float32), 'g2': jnp.ones((D,), jnp.float32), 'b2': jnp.zeros((D,), jnp.float32), 'Wff1': jax.random.normal(ks[7], (D, DFF), jnp.float32) * s, 'bff1': jnp.zeros((DFF,), jnp.float32), 'Wff2': jax.random.normal(ks[8], (DFF, D), jnp.float32) * s, 'bff2': jnp.zeros((D,), jnp.float32), 'g3': jnp.ones((D,), jnp.float32), 'b3': jnp.zeros((D,), jnp.float32)}
    _L0_xattn_all = _L0_xattn_setup()
    _L0_xattn_in = {k: v for k, v in _L0_xattn_all.items() if k in ('Wqkv', 'Wproj_sa', 'bproj_sa', 'g1', 'b1', 'Wq_ca', 'Wkv_ca', 'Wproj_ca', 'bproj_ca', 'g2', 'b2', 'Wff1', 'bff1', 'Wff2', 'bff2', 'g3', 'b3')}
    del _L0_xattn_all

    def _L1_xattn_setup():
        import jax, jax.numpy as jnp
        import numpy as np
        LN_EPS = 1e-05

        def _ln(x, g, b):
            m = jnp.mean(x, axis=-1, keepdims=True)
            v = jnp.mean((x - m) ** 2, axis=-1, keepdims=True)
            return (x - m) / jnp.sqrt(v + LN_EPS) * g + b
        key = jax.random.key(seed)
        ks = jax.random.split(key, 8)
        B, N, S, D, T = (16, 64, 512, 256, 192)

        def xavier(k, shape):
            fan_in, fan_out = shape
            lim = (6.0 / (fan_in + fan_out)) ** 0.5
            return jax.random.uniform(k, shape, minval=-lim, maxval=lim, dtype=jnp.float32)
        return {'prev_states': jax.random.normal(ks[0], (B, N, D), dtype=jnp.float32), 'input_tokens': jax.random.normal(ks[1], (B, S, T), dtype=jnp.float32), 'W_proj': xavier(ks[2], (T, D)), 'b_proj': jnp.zeros((D,), jnp.float32), 'g_state': jnp.ones((D,), jnp.float32), 'beta_state': jnp.zeros((D,), jnp.float32), 'g_input': jnp.ones((D,), jnp.float32), 'beta_input': jnp.zeros((D,), jnp.float32), 'g_out': jnp.ones((D,), jnp.float32), 'beta_out': jnp.zeros((D,), jnp.float32), 'W_u': xavier(ks[3], (2 * D, D)), 'b_u': jnp.full((D,), -1.0, jnp.float32), 'W_r': xavier(ks[4], (2 * D, D)), 'b_r': jnp.zeros((D,), jnp.float32), 'W_n': xavier(ks[5], (2 * D, D)), 'b_n': jnp.zeros((D,), jnp.float32)}
    _L1_xattn_all = _L1_xattn_setup()
    _L1_xattn_in = {k: v for k, v in _L1_xattn_all.items() if k in ('W_proj', 'b_proj', 'g_state', 'beta_state', 'g_input', 'beta_input', 'g_out', 'beta_out', 'W_u', 'b_u', 'W_r', 'b_r', 'W_n', 'b_n')}
    del _L1_xattn_all
    return {'x': x, 'ctx_768': ctx_768, 'L0_xattn_Wqkv': _L0_xattn_in['Wqkv'], 'L0_xattn_Wproj_sa': _L0_xattn_in['Wproj_sa'], 'L0_xattn_bproj_sa': _L0_xattn_in['bproj_sa'], 'L0_xattn_g1': _L0_xattn_in['g1'], 'L0_xattn_b1': _L0_xattn_in['b1'], 'L0_xattn_Wq_ca': _L0_xattn_in['Wq_ca'], 'L0_xattn_Wkv_ca': _L0_xattn_in['Wkv_ca'], 'L0_xattn_Wproj_ca': _L0_xattn_in['Wproj_ca'], 'L0_xattn_bproj_ca': _L0_xattn_in['bproj_ca'], 'L0_xattn_g2': _L0_xattn_in['g2'], 'L0_xattn_b2': _L0_xattn_in['b2'], 'L0_xattn_Wff1': _L0_xattn_in['Wff1'], 'L0_xattn_bff1': _L0_xattn_in['bff1'], 'L0_xattn_Wff2': _L0_xattn_in['Wff2'], 'L0_xattn_bff2': _L0_xattn_in['bff2'], 'L0_xattn_g3': _L0_xattn_in['g3'], 'L0_xattn_b3': _L0_xattn_in['b3'], 'L1_xattn_W_proj': _L1_xattn_in['W_proj'], 'L1_xattn_b_proj': _L1_xattn_in['b_proj'], 'L1_xattn_g_state': _L1_xattn_in['g_state'], 'L1_xattn_beta_state': _L1_xattn_in['beta_state'], 'L1_xattn_g_input': _L1_xattn_in['g_input'], 'L1_xattn_beta_input': _L1_xattn_in['beta_input'], 'L1_xattn_g_out': _L1_xattn_in['g_out'], 'L1_xattn_beta_out': _L1_xattn_in['beta_out'], 'L1_xattn_W_u': _L1_xattn_in['W_u'], 'L1_xattn_b_u': _L1_xattn_in['b_u'], 'L1_xattn_W_r': _L1_xattn_in['W_r'], 'L1_xattn_b_r': _L1_xattn_in['b_r'], 'L1_xattn_W_n': _L1_xattn_in['W_n'], 'L1_xattn_b_n': _L1_xattn_in['b_n']}

def reference(x, ctx_768, L0_xattn_Wqkv, L0_xattn_Wproj_sa, L0_xattn_bproj_sa, L0_xattn_g1, L0_xattn_b1, L0_xattn_Wq_ca, L0_xattn_Wkv_ca, L0_xattn_Wproj_ca, L0_xattn_bproj_ca, L0_xattn_g2, L0_xattn_b2, L0_xattn_Wff1, L0_xattn_bff1, L0_xattn_Wff2, L0_xattn_bff2, L0_xattn_g3, L0_xattn_b3, L1_xattn_W_proj, L1_xattn_b_proj, L1_xattn_g_state, L1_xattn_beta_state, L1_xattn_g_input, L1_xattn_beta_input, L1_xattn_g_out, L1_xattn_beta_out, L1_xattn_W_u, L1_xattn_b_u, L1_xattn_W_r, L1_xattn_b_r, L1_xattn_W_n, L1_xattn_b_n):
    import jax
    import jax.numpy as jnp

    def _L0_xattn_ref(x, cond, Wqkv, Wproj_sa, bproj_sa, g1, b1, Wq_ca, Wkv_ca, Wproj_ca, bproj_ca, g2, b2, Wff1, bff1, Wff2, bff2, g3, b3):
        import jax, jax.numpy as jnp
        import numpy as np
        D, H, DFF, DC = (256, 16, 1024, 192)
        DH = D // H
        EPS = 1e-05

        def layer_norm(x, g, b):
            m = jnp.mean(x, axis=-1, keepdims=True)
            v = jnp.mean(jnp.square(x - m), axis=-1, keepdims=True)
            return (x - m) * jax.lax.rsqrt(v + EPS) * g + b

        def _self_attn(x, Wqkv, Wproj, bproj):
            B, T, _ = x.shape
            qkv = x @ Wqkv
            qkv = qkv.reshape(B, T, 3, H, DH)
            q, k, v = (qkv[:, :, i].transpose(0, 2, 1, 3) for i in range(3))
            scale = DH ** (-0.5)
            attn = jnp.einsum('bhtd,bhsd->bhts', q, k) * scale
            causal = jnp.triu(jnp.ones((T, T), bool), k=1)
            attn = jnp.where(causal, -jnp.inf, attn)
            attn = jax.nn.softmax(attn, axis=-1)
            out = jnp.einsum('bhts,bhsd->bhtd', attn, v)
            out = out.transpose(0, 2, 1, 3).reshape(B, T, D)
            return out @ Wproj + bproj

        def _cross_attn(x, cond, Wq, Wkv, Wproj, bproj):
            B, T, _ = x.shape
            C = cond.shape[1]
            q = (x @ Wq).reshape(B, T, H, DH).transpose(0, 2, 1, 3)
            kv = (cond @ Wkv).reshape(B, C, 2, H, DH)
            k = kv[:, :, 0].transpose(0, 2, 1, 3)
            v = kv[:, :, 1].transpose(0, 2, 1, 3)
            scale = DH ** (-0.5)
            attn = jax.nn.softmax(jnp.einsum('bhtd,bhcd->bhtc', q, k) * scale, axis=-1)
            out = jnp.einsum('bhtc,bhcd->bhtd', attn, v)
            out = out.transpose(0, 2, 1, 3).reshape(B, T, D)
            return out @ Wproj + bproj
        x = x + _self_attn(layer_norm(x, g1, b1), Wqkv, Wproj_sa, bproj_sa)
        x = x + _cross_attn(layer_norm(x, g2, b2), cond, Wq_ca, Wkv_ca, Wproj_ca, bproj_ca)
        h = layer_norm(x, g3, b3)
        h = jax.nn.gelu(h @ Wff1 + bff1, approximate=False) @ Wff2 + bff2
        return x + h

    def _L1_xattn_ref(prev_states, input_tokens, W_proj, b_proj, g_state, beta_state, g_input, beta_input, g_out, beta_out, W_u, b_u, W_r, b_r, W_n, b_n):
        import jax, jax.numpy as jnp
        import numpy as np
        LN_EPS = 1e-05

        def _ln(x, g, b):
            m = jnp.mean(x, axis=-1, keepdims=True)
            v = jnp.mean((x - m) ** 2, axis=-1, keepdims=True)
            return (x - m) / jnp.sqrt(v + LN_EPS) * g + b
        D = prev_states.shape[-1]
        tok = input_tokens @ W_proj + b_proj
        scores = jnp.einsum('bnd,bsd->bns', prev_states, tok) / jnp.sqrt(jnp.float32(D))
        attn = jax.nn.softmax(scores, axis=-1)
        routed = jnp.einsum('bns,bsd->bnd', attn, tok)
        ps_n = _ln(prev_states, g_state, beta_state)
        in_n = _ln(routed, g_input, beta_input)
        concat = jnp.concatenate([ps_n, in_n], axis=-1)
        u = jax.nn.sigmoid(concat @ W_u + b_u)
        r = jax.nn.sigmoid(concat @ W_r + b_r)
        reset_in = jnp.concatenate([r * ps_n, in_n], axis=-1)
        cand = jnp.tanh(reset_in @ W_n + b_n)
        new_state = (1.0 - u) * prev_states + u * cand
        return _ln(new_state, g_out, beta_out)
    x = _L0_xattn_ref(x, ctx_768, L0_xattn_Wqkv, L0_xattn_Wproj_sa, L0_xattn_bproj_sa, L0_xattn_g1, L0_xattn_b1, L0_xattn_Wq_ca, L0_xattn_Wkv_ca, L0_xattn_Wproj_ca, L0_xattn_bproj_ca, L0_xattn_g2, L0_xattn_b2, L0_xattn_Wff1, L0_xattn_bff1, L0_xattn_Wff2, L0_xattn_bff2, L0_xattn_g3, L0_xattn_b3)
    x = _L1_xattn_ref(x, ctx_768, L1_xattn_W_proj, L1_xattn_b_proj, L1_xattn_g_state, L1_xattn_beta_state, L1_xattn_g_input, L1_xattn_beta_input, L1_xattn_g_out, L1_xattn_beta_out, L1_xattn_W_u, L1_xattn_b_u, L1_xattn_W_r, L1_xattn_b_r, L1_xattn_W_n, L1_xattn_b_n)
    return x

_drawn_inputs = setup_inputs


def setup_inputs(seed=0):
    import zlib

    import numpy as np

    out = dict(_drawn_inputs(seed))
    spreads = {'L0_xattn_bproj_sa': (0.0, 0.1),
     'L0_xattn_g1': (1.0, 0.6),
     'L0_xattn_b1': (0.0, 0.8),
     'L0_xattn_bproj_ca': (0.0, 0.1),
     'L0_xattn_g2': (1.0, 0.6),
     'L0_xattn_b2': (0.0, 2.0),
     'L0_xattn_bff1': (0.0, 0.383),
     'L0_xattn_bff2': (0.0, 0.1),
     'L0_xattn_g3': (1.0, 0.6),
     'L0_xattn_b3': (0.0, 0.665),
     'L1_xattn_b_proj': (0.0, 0.1),
     'L1_xattn_g_state': (1.0, 0.2),
     'L1_xattn_beta_state': (0.0, 0.287),
     'L1_xattn_g_input': (1.0, 0.2),
     'L1_xattn_beta_input': (0.0, 0.286),
     'L1_xattn_g_out': (1.0, 0.2),
     'L1_xattn_beta_out': (0.0, 0.1),
     'L1_xattn_b_u': (-1.0, 0.2),
     'L1_xattn_b_r': (0.0, 2.0),
     'L1_xattn_b_n': (0.0, 0.412)}
    factors = {'L0_xattn_Wqkv': 3.811, 'L0_xattn_Wproj_sa': 3.698, 'L0_xattn_Wq_ca': 34.87}
    for name, (base, spread) in spreads.items():
        noise = np.random.default_rng([zlib.crc32(name.encode()), seed]).standard_normal(out[name].shape)
        drawn = base * np.exp(spread * noise) if base else spread * noise
        out[name] = jnp.asarray(drawn.astype(out[name].dtype))
    for name, factor in factors.items():
        out[name] = (out[name] * factor).astype(out[name].dtype)
    return out
```

```python
import concourse.bass as bass
from concourse import mybir
from contextlib import ExitStack


def build(nc, x, ctx_768, l0_wqkv, l0_wproj_sa, l0_bproj_sa, l0_g1, l0_b1, l0_wq_ca, l0_wkv_ca, l0_wproj_ca,
          l0_bproj_ca, l0_g2, l0_b2, l0_wff1, l0_bff1, l0_wff2, l0_bff2, l0_g3, l0_b3, l1_w_proj, l1_b_proj,
          l1_g_state, l1_beta_state, l1_g_input, l1_beta_input, l1_g_out, l1_beta_out, l1_w_u, l1_b_u, l1_w_r,
          l1_b_r, l1_w_n, l1_b_n, out):
    f32 = mybir.dt.float32
    f32r = mybir.dt.float32r
    bf16 = mybir.dt.bfloat16
    ALU = mybir.AluOpType
    ACT = mybir.ActivationFunctionType
    AX = mybir.AxisListType

    B, T, D = x.shape
    C, DC = ctx_768.shape[1:]
    DFF = l0_wff1.shape[1]
    P = 128
    H = 16
    DH = D // H
    NT = T // P
    NF = D // P
    NFF = DFF // P
    NC = 2
    CK = [P, DC - P]
    HG = 4
    NG = H // HG
    NP = H // 2
    QW = 32
    EPS = 1e-5
    ATT_SCALE = float(DH) ** -0.5
    ROUTE_SCALE = float(D) ** -0.5
    MASKED = -1e30
    SA_K = 3 * DH
    SA_KM = SA_K + 2
    CA_K = 6 * DH
    CA_KM = CA_K + 4

    es = ExitStack()
    with es:
        def sb(name, shape, dt=f32):
            return es.enter_context(nc.sbuf_tensor(name, shape, dt))

        wqkv = sb("wqkv", [P, NF, 3 * D])
        wproj_sa = sb("wproj_sa", [P, NG, D])
        wproj_ca = sb("wproj_ca", [P, NG, D])
        wq_ca = sb("wq_ca", [P, NF, D])
        wkv_ca = sb("wkv_ca", [P, NC, 2 * D])
        wff1 = sb("wff1", [P, NF, DFF])
        wff2 = sb("wff2", [P, NFF, D])
        wtok = sb("wtok", [P, NC, D])
        w_u = sb("w_u", [P, 2 * NF, D])
        w_r = sb("w_r", [P, 2 * NF, D])
        w_n = sb("w_n", [P, 2 * NF, D])
        COLS = ["g1", "b1", "g2", "b2", "g3", "b3", "g_state", "beta_state", "g_input", "beta_input",
                "btok", "b_u", "b_r", "b_n"]
        cols_dram = [l0_g1, l0_b1, l0_g2, l0_b2, l0_g3, l0_b3, l1_g_state, l1_beta_state, l1_g_input,
                     l1_beta_input, l1_b_proj, l1_b_u, l1_b_r, l1_b_n]
        cols = sb("cols", [P, len(COLS), NF])
        bff1 = sb("bff1", [P, NFF])
        half_bias = sb("half_bias", [P, 2, NF])
        bff2_row = sb("bff2_row", [P, D])
        btok_row = sb("btok_row", [P, D])
        gout_row = sb("gout_row", [P, D])
        bout_row = sb("bout_row", [P, D])

        def col(name, f):
            return cols[:, COLS.index(name), f:f + 1]

        ident = sb("ident", [P, P])
        ident_bf = sb("ident_bf", [P, P], bf16)
        mask_bf = sb("mask_bf", [P, P], bf16)
        maskT_bf = sb("maskT_bf", [P, P], bf16)
        sel = sb("sel", [P, P])
        neg_half = sb("neg_half", [P, NT])

        x0 = sb("x0", [P, NT, D])
        x1 = sb("x1", [P, NT, D])
        x2 = x1
        x2b = sb("x2b", [P, NT, D])
        x3 = x2b
        stats = sb("stats", [P, NT, 6])
        mv = sb("mv", [P, NT, 2])
        ve = sb("ve", [P, NT])
        rstd = sb("rstd", [P, NT])
        xh = sb("xh", [P, NT, D])
        hT = sb("hT", [P, NF, T])
        psnT = sb("psnT", [P, NF, T])
        q_hi = sb("q_hi", [P, NF, T], f32r)
        q_lo = sb("q_lo", [P, NF, T], f32r)
        k_hi = sb("k_hi", [P, NF, T], f32r)
        k_lo = sb("k_lo", [P, NF, T], f32r)
        q_st = sb("q_st", [P, NP, T], f32r)
        k_st = sb("k_st", [P, NP, T], f32r)
        v_sa = sb("v_sa", [P, NT, H, QW])
        negm = sb("negm", [P, NT, H])
        nm2 = sb("nm2", [P, NT, 2, H], f32r)
        nmT = sb("nmT", [2 * H, T], f32r)
        gT = sb("gT", [P, NFF, T])
        probs = gT[:, :, :].rearrange("p (s h) t -> p s h t", s=2)
        pv_sb = sb("pv_sb", [P, 2, T])
        rsum = sb("rsum", [P, 2, T])
        routed = rsum[:, :, :].rearrange("p a (b d) -> p (a b) d", d=D)
        attT = sb("attT", [P, NG, T])
        q2_st = q_st
        ctx_sb = sb("ctx_sb", [P, DC])
        ctxT = sb("ctxT", [P, NC, P])
        k2_hi = sb("k2_hi", [P, NF, C], f32r)
        k2_lo = sb("k2_lo", [P, NF, C], f32r)
        k2_st = sb("k2_st", [P, NP, 2 * C], f32r)
        v_ca = sb("v_ca", [P, NP, 2 * QW])
        tokT = sb("tokT", [P, NF, C])
        tok = sb("tok", [P, D])
        xT = sb("xT", [P, NF, T])
        rmax = sb("rmax", [P, 2 * NT])
        rden = sb("rden", [P, 2 * NT])
        route = sb("route", [P, NT, C])
        routeT = sb("routeT", [P, 2, P])
        t_r = sb("t_r", [P, NF, T])
        t_u = sb("t_u", [P, NF, T])
        cand = sb("cand", [P, NF, T])
        y_out = sb("y_out", [P, NT, D])

        bank = [es.enter_context(nc.psum_tensor(f"bank{k}", [P, 512], f32)) for k in range(4)]
        wide = [es.enter_context(nc.psum_tensor(f"wide{k}", [P, 2, 512], f32)) for k in range(2)]

        MAX_UNITS = []
        for qb in range(NT):
            per = T // ((qb + 1) * P)
            MAX_UNITS += [(qb, h, per) for h in range(0, H, 2 * per)]
        ST_UNITS = [(g, kb, pr) for g in range(NG) for kb in range(NT) for pr in range(2)]

        PER, S = {}, {}

        def sem(name, per):
            PER[name] = per
            S[name] = es.enter_context(nc.semaphore(name))

        def n(name, b, c):
            return b * PER[name] + c

        for ln in ("ln1", "ln2", "ln3", "psn", "inn", "fin"):
            sem(f"{ln}_stat", NT)
            sem(f"{ln}_var", NT + 1)
            sem(f"{ln}_rstd", 1)
            sem(f"{ln}_norm", NT)
        for name, per in [
            ("x_in", 16), ("ctx_in", 32), ("y_stored", 16),
            ("h1", NF), ("h2", NF), ("h3", NF), ("psn_done", NF), ("inn_done", NF), ("xT_done", NF),
            ("q_hi_done", NF), ("k_hi_done", NF), ("q_lo_done", NF), ("k_lo_done", NF),
            ("q_stacked", 16 * 3 * H), ("k_stacked", 16 * 3 * H), ("v_done", 2),
            ("ctxT_done", 1), ("k2_hi_done", 1), ("k2_lo_done", 1), ("k2_stacked", 16 * 3 * H), ("v2_done", 2),
            ("tokT_done", NF), ("tok_done", 1),
            ("max_done", len(MAX_UNITS)), ("nm_hi_done", 1), ("nm_lo_done", 1), ("nmT_done", 1),
            ("max_stacked", 64),
            ("exp_done", len(ST_UNITS)), ("pv_used", NG * NT),
            ("pv_out", NG), ("rsum_done", NG), ("att_done", NG), ("x1_done", 2),
            ("q2_hi_done", NF), ("q2_lo_done", NF), ("q2_stacked", 16 * 3 * H),
            ("max2_done", NT), ("nm2_hi_done", 1), ("nm2_lo_done", 1), ("nmT2_done", 1), ("max2_stacked", 64),
            ("exp2_done", NP // 2), ("pv2_out", NG), ("rsum2_done", NG), ("att2_done", NG), ("x2_done", 2),
            ("x2b_done", 1), ("gelu_done", NFF), ("x3_done", 2),
            ("rmax_done", 1), ("rbias_done", 1), ("rexp_done", NT), ("rtotal_done", 1), ("rden_done", 1),
            ("routeT_done", 1), ("routed_done", NT), ("tr_done", NF), ("tu_done", NF), ("rp_done", NF),
            ("cand_done", NF), ("diff_done", NF), ("step_done", NF), ("new_done", NF), ("gained", 1),
            ("y_done", 1),
        ]:
            sem(name, per)

        BANK_USES = (
            [(("ln1T", f), ("h1", f + 1)) for f in range(NF)]
            + [(("q", f), ("q_lo_done", f + 1)) for f in range(NF)]
            + [(("k", f), ("k_lo_done", f + 1)) for f in range(NF)]
            + [(("v", i), ("v_done", i + 1)) for i in range(2)]
            + [(("ctxT", 0), ("ctxT_done", 1)), (("k2", 0), ("k2_lo_done", 1)), (("v2", 0), ("v2_done", 2)),
               (("tokT", 0), ("tokT_done", NF)), (("tok", 0), ("tok_done", 1)), (("negmT", 0), ("nmT_done", 1))]
            + [u for g in range(NG) for u in ((("pv", g), ("pv_out", g + 1)), (("sum", g), ("rsum_done", g + 1)))]
            + [(("proj", i), ("x1_done", i + 1)) for i in range(2)]
            + [(("ln2T", f), ("h2", f + 1)) for f in range(NF)]
            + [(("q2", f), ("q2_lo_done", f + 1)) for f in range(NF)]
            + [(("negm2T", 0), ("nmT2_done", 1))]
            + [u for g in range(NG) for u in ((("pv2", g), ("pv2_out", g + 1)), (("sum2", g), ("rsum2_done", g + 1)))]
            + [(("proj2", i), ("x2_done", i + 1)) for i in range(2)]
            + [(("ln3T", f), ("h3", f + 1)) for f in range(NF)]
            + [(("ff2", i), ("x3_done", i + 1)) for i in range(2)]
            + [(("xT", f), ("xT_done", f + 1)) for f in range(NF)]
            + [(("route", 0), ("rexp_done", NT))]
            + [(("psnT", f), ("psn_done", f + 1)) for f in range(NF)]
            + [(("routeT", 0), ("routeT_done", 1))]
            + [(("routed", i), ("routed_done", 2 * i + 2)) for i in range(2)]
            + [(("innT", f), ("inn_done", f + 1)) for f in range(NF)]
            + [(("r", f), ("tr_done", f + 1)) for f in range(NF)]
            + [(("u", f), ("tu_done", f + 1)) for f in range(NF)]
            + [(("n", f), ("cand_done", f + 1)) for f in range(NF)]
            + [(("new", i), ("fin_norm", 2 * i + 2)) for i in range(2)])
        WIDE_USES = ([(("max", u), ("max_done", u + 1)) for u in range(len(MAX_UNITS))]
                     + [(("st", u), ("exp_done", u + 1)) for u in range(len(ST_UNITS))]
                     + [(("max2", t), ("max2_done", t + 1)) for t in range(NT)]
                     + [(("st2", u), ("exp2_done", u + 1)) for u in range(NP // 2)]
                     + [(("ff1", u), ("gelu_done", 2 * u + 2)) for u in range(NFF // 2)])
        RINGS = {"bank": (bank, BANK_USES, {}), "wide": (wide, WIDE_USES, {})}
        FULL = {("pv", g): ("pv_used", NT * (g + 1)) for g in range(NG)}
        for ring, (tiles, uses, at) in RINGS.items():
            at.update({use: i for i, (use, _) in enumerate(uses)})
            for k in range(len(tiles)):
                turns = [use for use, _ in uses[k::len(tiles)] if use not in FULL]
                FULL.update({use: (f"{ring}_full{k}", c + 1) for c, use in enumerate(turns)})
                sem(f"{ring}_full{k}", len(turns))

        def free(pe, b, use, ring="bank"):
            tiles, uses, at = RINGS[ring]
            i = at[use]
            if i >= len(tiles):
                name, c = uses[i - len(tiles)][1]
                pe.wait_ge(S[name], n(name, b, c))
            else:
                last = len(uses) - len(tiles) + (i - len(uses)) % len(tiles)
                name = uses[last][1][0]
                pe.wait_ge(S[name], n(name, b, 0))
            return tiles[i % len(tiles)]

        def filled(use):
            return S[FULL[use][0]]

        def full(eng, b, use, ring="bank"):
            tiles, _, at = RINGS[ring]
            name, c = FULL[use]
            eng.wait_ge(S[name], n(name, b, c))
            return tiles[at[use] % len(tiles)]

        w_in = es.enter_context(nc.semaphore("w_in"))
        zeroed = es.enter_context(nc.semaphore("zeroed"))
        pads_in = es.enter_context(nc.semaphore("pads_in"))
        consts = es.enter_context(nc.semaphore("consts"))
        consts_dve = es.enter_context(nc.semaphore("consts_dve"))
        N_ZERO, N_CONST, N_CONST_DVE, N_PAD = 9, 6, 11, 16 * 2 * (HG + 1)
        N_LOAD = 16 * (len(COLS) + 1 + 4 + 7 + 2 * NC)

        block = es.enter_context(nc.Block())
        x_v = x.rearrange("b (t p) d -> b p t d", p=P)
        out_v = out.rearrange("b (t p) d -> b p t d", p=P)

        @block.sync
        def _(sp):
            loads = []

            def load(dst, src):
                loads.append(16)
                sp.dma_start(dst, src).then_inc(w_in, 16)

            with nc.allow_non_contiguous_dma(reason="vectors over features, once"):
                for i, v in enumerate(cols_dram):
                    load(cols[:, i, :], v.rearrange("(f p) -> p f", p=P))
                load(bff1[:, :], l0_bff1.rearrange("(f p) -> p f", p=P))
            for row, v in ((bff2_row, l0_bff2), (btok_row, l1_b_proj), (gout_row, l1_g_out),
                           (bout_row, l1_beta_out)):
                load(row[:, :], v.rearrange("(a n) -> a n", a=1).broadcast_to((P, D)))
            for dst, w in ((wqkv, l0_wqkv), (wq_ca, l0_wq_ca), (wff1, l0_wff1), (wff2, l0_wff2), (w_u, l1_w_u),
                           (w_r, l1_w_r), (w_n, l1_w_n)):
                load(dst[:, :, :], w.rearrange("(f p) n -> p f n", p=P))
            for c in range(NC):
                load(wkv_ca[0:CK[c], c, :], l0_wkv_ca[c * P:c * P + CK[c], :])
                load(wtok[0:CK[c], c, :], l1_w_proj[c * P:c * P + CK[c], :])
            assert sum(loads) == N_LOAD
            sp.wait_ge(zeroed, N_ZERO)
            for dst, w, bias in ((wproj_sa, l0_wproj_sa, l0_bproj_sa), (wproj_ca, l0_wproj_ca, l0_bproj_ca)):
                wv = w.rearrange("(g j d) n -> j d g n", j=HG, d=DH)
                for j in range(HG):
                    sp.dma_start(dst[j * QW:j * QW + DH, :, :], wv[j]).then_inc(pads_in, 16)
                sp.dma_start(dst[DH:DH + 1, 0, :], bias.rearrange("(a n) -> a n", a=1)).then_inc(pads_in, 16)

            with sp.Fori(0, B) as b:
                sp.wait_ge(S["x1_done"], n("x1_done", b, 0))
                sp.dma_start(x0[:, :, :], x_v[b]).then_inc(S["x_in"], 16)
                sp.wait_ge(S["ctxT_done"], n("ctxT_done", b, 0))
                for half in range(2):
                    sp.dma_start(ctx_sb[half * C:half * C + C, :], ctx_768[b]).then_inc(S["ctx_in"], 16)

                def stack(done, ready, src, slots, dst):
                    for f in range(NF):
                        sp.wait_ge(S[ready], n(ready, b, f + 1))
                        for at in slots:
                            for j in range(P // DH):
                                sp.dma_start(dst(f * (P // DH) + j, at), src[j * DH:j * DH + DH, f, :].bitcast(f32))\
                                  .then_inc(S[done], 16)

                def self_q(h, at):
                    return q_st[(h % 2) * 64 + at:(h % 2) * 64 + at + DH, h // 2, :].bitcast(f32)

                def self_k(h, at):
                    return k_st[(h % 2) * 64 + at:(h % 2) * 64 + at + DH, h // 2, :].bitcast(f32)

                def cross_q(h, at):
                    row = (h % 2) * 3 * DH + at
                    return q2_st[row:row + DH, h // 2, :].bitcast(f32)

                stack("q_stacked", "q_hi_done", q_hi, (0, DH), self_q)
                stack("k_stacked", "k_hi_done", k_hi, (0, 2 * DH), self_k)
                stack("q_stacked", "q_lo_done", q_lo, (2 * DH,), self_q)
                stack("k_stacked", "k_lo_done", k_lo, (DH,), self_k)
                for ready, src, slots in (("k2_hi_done", k2_hi, (0, 2 * DH)), ("k2_lo_done", k2_lo, (DH,))):
                    sp.wait_ge(S[ready], n(ready, b, 1))
                    for at in slots:
                        for h in range(H):
                            row = (h % 2) * 3 * DH + at
                            sp.dma_start(k2_st[row:row + DH, h // 2, (h % 2) * C:(h % 2) * C + C].bitcast(f32),
                                         src[(h % 8) * DH:(h % 8) * DH + DH, h // 8, :].bitcast(f32))\
                              .then_inc(S["k2_stacked"], 16)
                sp.wait_ge(S["nmT_done"], n("nmT_done", b, 1))
                for part in range(4):
                    row = (part // 2) * 64 + SA_K + part % 2
                    sp.dma_start(q_st[row:row + 1, :, :].bitcast(f32), nmT[part * NP:part * NP + NP, :].bitcast(f32))\
                      .then_inc(S["max_stacked"], 16)
                stack("q2_stacked", "q2_hi_done", q_hi, (0, DH), cross_q)
                stack("q2_stacked", "q2_lo_done", q_lo, (2 * DH,), cross_q)
                sp.wait_ge(S["nmT2_done"], n("nmT2_done", b, 1))
                for part in range(4):
                    sp.dma_start(q2_st[CA_K + part:CA_K + part + 1, :, :].bitcast(f32),
                                 nmT[part * NP:part * NP + NP, :].bitcast(f32))\
                      .then_inc(S["max2_stacked"], 16)
                sp.wait_ge(S["y_done"], n("y_done", b, 1))
                sp.dma_start(out_v[b], y_out[:, :, :]).then_inc(S["y_stored"], 16)
            sp.wait_ge(S["y_stored"], 16 * B)

        @block.gpsimd
        def _(pool):
            for tile in (wproj_sa, wproj_ca, v_sa):
                pool.memset(tile[:], 0.0).then_inc(zeroed, 1)
            for tile in (ident, ident_bf, sel, mask_bf, maskT_bf, v_ca):
                pool.memset(tile[:], 0.0).then_inc(zeroed, 1)
            pool.memset(neg_half[:, :], -0.5).then_inc(consts, 1)
            pool.wait_ge(zeroed, N_ZERO)
            pool.affine_select(out=ident[:, :], in_=ident[:, :], compare_op=ALU.not_equal, fill=1.0, base=0,
                               pattern=[[-1, P]], channel_multiplier=1).then_inc(consts, 1)
            pool.affine_select(out=ident_bf[:, :], in_=ident_bf[:, :], compare_op=ALU.not_equal, fill=1.0, base=0,
                               pattern=[[-1, P]], channel_multiplier=1).then_inc(consts, 1)
            sel_v = sel[:, :].rearrange("p (j c) -> p j c", j=HG)
            pool.affine_select(out=sel_v, in_=sel_v, compare_op=ALU.not_equal, fill=1.0, base=-DH,
                               pattern=[[-QW, HG], [0, QW]], channel_multiplier=1).then_inc(consts, 1)
            pool.affine_select(out=mask_bf[:, :], in_=mask_bf[:, :], compare_op=ALU.is_ge, fill=MASKED, base=0,
                               pattern=[[-1, P]], channel_multiplier=1).then_inc(consts, 1)
            pool.affine_select(out=maskT_bf[:, :], in_=maskT_bf[:, :], compare_op=ALU.is_ge, fill=MASKED, base=0,
                               pattern=[[1, P]], channel_multiplier=-1).then_inc(consts, 1)

            pool.wait_ge(consts, N_CONST)
            with pool.Fori(0, B) as b:
                def root(ln):
                    pool.wait_ge(S[f"{ln}_var"], n(f"{ln}_var", b, NT + 1))
                    pool.tensor_tensor(rstd[:, :], ve[:, :], neg_half[:, :], ALU.pow).then_inc(S[f"{ln}_rstd"], 1)

                root("ln1")
                root("ln2")
                pool.wait_ge(S["x2_done"], n("x2_done", b, 2))
                for t in range(NT):
                    last = pool.tensor_tensor(x2b[:, t, :], x2[:, t, :], bff2_row[:, :], ALU.add)
                last.then_inc(S["x2b_done"], 1)
                for ln in ("ln3", "psn", "inn", "fin"):
                    root(ln)
                pool.wait_ge(S["fin_norm"], n("fin_norm", b, NT))
                for t in range(NT):
                    last = pool.tensor_tensor(y_out[:, t, :], y_out[:, t, :], gout_row[:, :], ALU.mult)
                last.then_inc(S["gained"], 1)
                pool.wait_ge(S["gained"], n("gained", b, 1))
                for t in range(NT):
                    last = pool.tensor_tensor(y_out[:, t, :], y_out[:, t, :], bout_row[:, :], ALU.add)
                last.then_inc(S["y_done"], 1)

        @block.scalar
        def _(act):
            act.wait_ge(w_in, N_LOAD)
            act.wait_ge(consts_dve, N_CONST_DVE)
            act.wait_ge(consts, N_CONST)
            with act.Fori(0, B) as b:
                def turned(use, dst, done, gain, bias):
                    for f in range(NF):
                        ps = full(act, b, (use, f))
                        act.activation(dst[:, f, :], ps[:, :], ACT.Identity, scale=col(gain, f), bias=col(bias, f))\
                           .then_inc(S[done], 1)

                def high(use, f, dst, done):
                    ps = full(act, b, (use, f))
                    act.activation(dst[:, f, :], ps[:, :], ACT.Copy).then_inc(S[done], 1)

                turned("ln1T", hT, "h1", "g1", "b1")
                act.wait_ge(S["q2_stacked"], n("q2_stacked", b, 0))
                act.wait_ge(S["k_stacked"], n("k_stacked", b, 0))
                for f in range(NF):
                    high("q", f, q_hi, "q_hi_done")
                for f in range(NF):
                    high("k", f, k_hi, "k_hi_done")
                for i in range(2):
                    ps = full(act, b, ("v", i))
                    for t in range(2):
                        last = act.activation(v_sa[:, 2 * i + t, :, 0:DH],
                                              ps[:, t * D:t * D + D].rearrange("p (h d) -> p h d", h=H), ACT.Copy)
                    last.then_inc(S["v_done"], 1)
                ps = full(act, b, ("ctxT", 0))
                act.activation(ctxT[:, 0, :], ps[:, 0:P], ACT.Copy)
                act.activation(ctxT[0:CK[1], 1, :], ps[0:CK[1], P:2 * P], ACT.Copy).then_inc(S["ctxT_done"], 1)
                ps = full(act, b, ("k2", 0))
                act.wait_ge(S["k2_stacked"], n("k2_stacked", b, 0))
                act.activation(k2_hi[:, :, :], ps[:, 0:NF * C].rearrange("p (f c) -> p f c", f=NF), ACT.Copy)\
                   .then_inc(S["k2_hi_done"], 1)
                ps = full(act, b, ("v2", 0))
                for e in range(2):
                    rows = slice(e * C, e * C + C)
                    act.activation(v_ca[rows, :, e * QW:e * QW + DH],
                                   ps[rows, 0:D].rearrange("p (t e d) -> p e t d", e=2, d=DH)[:, e], ACT.Copy)\
                       .then_inc(S["v2_done"], 1)
                ps = full(act, b, ("tokT", 0))
                for f in range(NF):
                    act.activation(tokT[:, f, :], ps[:, f * C:f * C + C], ACT.Identity, bias=col("btok", f))\
                       .then_inc(S["tokT_done"], 1)

                def out_of(u_use, g, done, att):
                    ps = full(act, b, (u_use, g))
                    if g >= 2:
                        act.wait_ge(S[att], n(att, b, g - 1))
                    act.activation(pv_sb[:, g % 2, :], ps[:, :], ACT.Copy).then_inc(S[done], 1)

                def transposed_max(use, done):
                    ps = full(act, b, (use, 0))
                    act.activation(nmT[:, :], ps[0:2 * H, :], ACT.Copy).then_inc(S[done], 1)

                transposed_max("negmT", "nmT_done")
                for u, (g, kb, pr) in enumerate(ST_UNITS):
                    w = T - kb * P
                    ps = full(act, b, ("st", u), "wide")
                    if u // 2 >= 2:
                        act.wait_ge(S["pv_used"], n("pv_used", b, u // 2 - 1))
                    act.activation(probs[:, (u // 2) % 2, 2 * pr:2 * pr + 2, kb * P:T], ps[:, :, 0:w], ACT.Exp,
                                   scale=ATT_SCALE).then_inc(S["exp_done"], 1)
                    if g >= 1 and kb == 1 and pr == 0:
                        out_of("pv", g - 1, "pv_out", "att_done")
                out_of("pv", NG - 1, "pv_out", "att_done")
                turned("ln2T", hT, "h2", "g2", "b2")
                for f in range(NF):
                    high("q2", f, q_hi, "q2_hi_done")
                act.wait_ge(S["max_stacked"], n("max_stacked", b, 64))
                transposed_max("negm2T", "nmT2_done")
                for u in range(NP // 2):
                    ps = full(act, b, ("st2", u), "wide")
                    act.activation(probs[:, u // 2, 2 * (u % 2):2 * (u % 2) + 2, :], ps[:, :, :], ACT.Exp,
                                   scale=ATT_SCALE).then_inc(S["exp2_done"], 1)
                for g in range(NG):
                    out_of("pv2", g, "pv2_out", "att2_done")
                turned("ln3T", hT, "h3", "g3", "b3")
                for u in range(NFF // 2):
                    ps = full(act, b, ("ff1", u), "wide")
                    for i in range(2):
                        f = 2 * u + i
                        act.activation(gT[:, f, :], ps[:, i, :], ACT.Gelu, bias=bff1[:, f:f + 1])\
                           .then_inc(S["gelu_done"], 1)
                for f in range(NF):
                    high("xT", f, xT, "xT_done")
                ps = full(act, b, ("route", 0))
                act.wait_ge(S["rbias_done"], n("rbias_done", b, 1))
                for t in range(NT):
                    act.activation(route[:, t, :], ps[:, t * C:t * C + C], ACT.Exp, bias=rmax[:, NT + t:NT + t + 1],
                                   scale=ROUTE_SCALE).then_inc(S["rexp_done"], 1)
                turned("psnT", psnT, "psn_done", "g_state", "beta_state")
                ps = full(act, b, ("routeT", 0))
                act.activation(routeT[:, :, :], ps[:, 0:2 * P].rearrange("p (i c) -> p i c", i=2), ACT.Copy).then_inc(S["routeT_done"], 1)
                turned("innT", hT, "inn_done", "g_input", "beta_input")
                for i, (gate, dst, done) in enumerate((("r", t_r, "tr_done"), ("u", t_u, "tu_done"))):
                    for f in range(NF):
                        ps = full(act, b, (gate, f))
                        act.activation(dst[:, f, :], ps[:, :], ACT.Tanh, scale=0.5, bias=half_bias[:, i, f:f + 1])\
                           .then_inc(S[done], 1)
                for f in range(NF):
                    ps = full(act, b, ("n", f))
                    act.activation(cand[:, f, :], ps[:, :], ACT.Tanh, bias=col("b_n", f)).then_inc(S["cand_done"], 1)

        @block.vector
        def _(dve):
            dve.memset(k_st[:, :, :].bitcast(f32), 1.0).then_inc(consts_dve, 1)
            dve.memset(k2_st[:, :, :].bitcast(f32), 0.0).then_inc(consts_dve, 1)
            dve.wait_ge(consts_dve, 2)
            dve.memset(k2_st[CA_K:CA_K + 2, :, 0:C].bitcast(f32), 1.0).then_inc(consts_dve, 1)
            dve.memset(k2_st[CA_K:CA_KM, :, C:2 * C].bitcast(f32), 1.0).then_inc(consts_dve, 1)
            dve.wait_ge(consts_dve, 4)
            dve.memset(k2_st[CA_K:CA_K + 2, :, C:2 * C].bitcast(f32), 0.0).then_inc(consts_dve, 1)
            dve.wait_ge(zeroed, N_ZERO)
            dve.memset(v_sa[:, :, :, DH:DH + 1], 1.0).then_inc(consts_dve, 1)
            dve.memset(v_ca[0:C, :, DH:DH + 1], 1.0).then_inc(consts_dve, 1)
            dve.memset(v_ca[C:2 * C, :, QW + DH:QW + DH + 1], 1.0).then_inc(consts_dve, 1)
            dve.wait_ge(w_in, N_LOAD)
            dve.tensor_scalar(half_bias[:, 0, :], cols[:, COLS.index("b_r"), :], 0.5, None, ALU.mult)\
               .then_inc(consts_dve, 1)
            dve.tensor_scalar(half_bias[:, 1, :], cols[:, COLS.index("b_u"), :], 0.5, None, ALU.mult)\
               .then_inc(consts_dve, 1)
            dve.tensor_scalar(w_n[:, 0:NF, :], w_n[:, 0:NF, :], 0.5, None, ALU.mult).then_inc(consts_dve, 1)

            with dve.Fori(0, B) as b:
                def norm(ln, src, dst, before=None):
                    for t in range(NT):
                        if before is not None:
                            before(t)
                        dve.bn_stats(stats[:, t, :], src(t)).then_inc(S[f"{ln}_stat"], 1)
                    dve.drain()
                    for t in range(NT):
                        dve.bn_aggr(mv[:, t, :], stats[:, t, :]).then_inc(S[f"{ln}_var"], 1)
                    dve.wait_ge(S[f"{ln}_var"], n(f"{ln}_var", b, NT))
                    dve.tensor_scalar(ve[:, :], mv[:, :, 1], EPS, None, ALU.add).then_inc(S[f"{ln}_var"], 1)
                    dve.wait_ge(S[f"{ln}_rstd"], n(f"{ln}_rstd", b, 1))
                    for t in range(NT):
                        dve.tensor_scalar(dst(t), src(t), mv[:, t, 0:1], rstd[:, t:t + 1], ALU.subtract, ALU.mult)\
                           .then_inc(S[f"{ln}_norm"], 1)

                def to_xh(t):
                    return xh[:, t, :]

                def low(use, f, hi, dst, hi_done, done):
                    ps = full(dve, b, (use, f))
                    dve.wait_ge(S[hi_done], n(hi_done, b, f + 1))
                    dve.tensor_tensor(dst[:, f, :], ps[:, :], hi[:, f, :].bitcast(f32), ALU.subtract)\
                       .then_inc(S[done], 1)

                def split_max(hi_out, lo_out, src, hi_done, lo_done):
                    dve.tensor_copy(hi_out, src).then_inc(S[hi_done], 1)
                    dve.wait_ge(S[hi_done], n(hi_done, b, 1))
                    dve.tensor_tensor(lo_out, src, hi_out.bitcast(f32), ALU.subtract).then_inc(S[lo_done], 1)

                def normalise(use, g, rs_done, out_done, done):
                    ps = full(dve, b, (use, g))
                    dve.reciprocal(rsum[:, g % 2, :], ps[:, :]).then_inc(S[rs_done], 1)
                    dve.wait_ge(S[rs_done], n(rs_done, b, g + 1))
                    dve.wait_ge(S[out_done], n(out_done, b, g + 1))
                    dve.tensor_tensor(attT[:, g, :], pv_sb[:, g % 2, :], rsum[:, g % 2, :], ALU.mult)\
                       .then_inc(S[done], 1)

                def residual(use, i, dst, src, done):
                    ps = full(dve, b, (use, i))
                    dve.tensor_tensor(dst[:, 2 * i:2 * i + 2, :], ps[:, :].rearrange("p (t d) -> p t d", t=2),
                                      src[:, 2 * i:2 * i + 2, :], ALU.add).then_inc(S[done], 1)

                dve.wait_ge(S["x_in"], n("x_in", b, 16))
                norm("ln1", lambda t: x0[:, t, :], to_xh)
                for f in range(NF):
                    low("q", f, q_hi, q_lo, "q_hi_done", "q_lo_done")
                for f in range(NF):
                    low("k", f, k_hi, k_lo, "k_hi_done", "k_lo_done")
                ps = full(dve, b, ("k2", 0))
                dve.wait_ge(S["k2_hi_done"], n("k2_hi_done", b, 1))
                dve.tensor_tensor(k2_lo[:, :, :], ps[:, 0:NF * C].rearrange("p (f c) -> p f c", f=NF),
                                  k2_hi[:, :, :].bitcast(f32), ALU.subtract).then_inc(S["k2_lo_done"], 1)
                ps = full(dve, b, ("tok", 0))
                dve.tensor_tensor(tok[:, :], ps[:, 0:D], btok_row[:, :], ALU.add).then_inc(S["tok_done"], 1)
                for u, (qb, h, per) in enumerate(MAX_UNITS):
                    w = (qb + 1) * P
                    ps = full(dve, b, ("max", u), "wide")
                    dve.tensor_reduce(negm[:, qb, h:h + 2 * per].rearrange("p (m e) -> p e m", e=2),
                                      ps[:, :, 0:per * w].rearrange("p a (h w) -> p a h w", w=w), AX.X, ALU.max,
                                      negate=True).then_inc(S["max_done"], 1)
                dve.wait_ge(S["max_done"], n("max_done", b, len(MAX_UNITS)))
                by_head = nm2[:, :, :, :].rearrange("p t a (b m) -> p t a b m", b=2)
                split_max(by_head[:, :, :, 0, :], by_head[:, :, :, 1, :],
                          negm[:, :, :].rearrange("p t (m e) -> p t e m", e=2), "nm_hi_done", "nm_lo_done")
                for g in range(NG):
                    normalise("sum", g, "rsum_done", "pv_out", "att_done")
                for i in range(2):
                    residual("proj", i, x1, x0, "x1_done")
                dve.wait_ge(S["x1_done"], n("x1_done", b, 2))
                norm("ln2", lambda t: x1[:, t, :], to_xh)
                for f in range(NF):
                    low("q2", f, q_hi, q_lo, "q2_hi_done", "q2_lo_done")
                for t in range(NT):
                    ps = full(dve, b, ("max2", t), "wide")
                    dve.tensor_reduce(negm[:, t, :].rearrange("p (a h) -> p a h", a=2),
                                      ps[:, :, :].rearrange("p a (h c) -> p a h c", c=C), AX.X, ALU.max,
                                      negate=True).then_inc(S["max2_done"], 1)
                dve.wait_ge(S["max2_done"], n("max2_done", b, NT))
                split_max(by_head[:, :, :, 0, :], by_head[:, :, :, 1, :],
                          negm[:, :, :].rearrange("p t (m e) -> p t e m", e=2), "nm2_hi_done", "nm2_lo_done")
                for g in range(NG):
                    normalise("sum2", g, "rsum2_done", "pv2_out", "att2_done")
                for i in range(2):
                    residual("proj2", i, x2, x1, "x2_done")
                dve.wait_ge(S["x2_done"], n("x2_done", b, 2))
                norm("ln3", lambda t: x2[:, t, :], to_xh)
                dve.wait_ge(S["x2b_done"], n("x2b_done", b, 1))
                for i in range(2):
                    residual("ff2", i, x3, x2b, "x3_done")
                dve.wait_ge(S["x3_done"], n("x3_done", b, 2))
                norm("psn", lambda t: x3[:, t, :], to_xh)
                ps = full(dve, b, ("route", 0))
                scores = ps[:, 0:NT * C].rearrange("p (t c) -> p t c", t=NT)
                dve.tensor_reduce(rmax[:, 0:NT], scores, AX.X, ALU.max, negate=True).then_inc(S["rmax_done"], 1)
                dve.wait_ge(S["rmax_done"], n("rmax_done", b, 1))
                dve.tensor_scalar(rmax[:, NT:2 * NT], rmax[:, 0:NT], ROUTE_SCALE, None, ALU.mult)\
                   .then_inc(S["rbias_done"], 1)
                dve.wait_ge(S["rexp_done"], n("rexp_done", b, NT))
                dve.tensor_reduce(rden[:, 0:NT], route[:, :, :], AX.X, ALU.add).then_inc(S["rtotal_done"], 1)
                dve.wait_ge(S["rtotal_done"], n("rtotal_done", b, 1))
                dve.reciprocal(rden[:, NT:2 * NT], rden[:, 0:NT]).then_inc(S["rden_done"], 1)
                dve.wait_ge(S["rden_done"], n("rden_done", b, 1))
                for i in range(2):
                    ps = full(dve, b, ("routed", i))
                    for t in (i, i + 2):
                        dve.tensor_scalar(routed[:, t, :], ps[:, (t // 2) * D:(t // 2) * D + D],
                                          rden[:, NT + t:NT + t + 1], None, ALU.mult).then_inc(S["routed_done"], 1)
                dve.wait_ge(S["routed_done"], n("routed_done", b, NT))
                norm("inn", lambda t: routed[:, t, :], to_xh)
                for f in range(NF):
                    dve.wait_ge(S["tr_done"], n("tr_done", b, f + 1))
                    dve.scalar_tensor_tensor(out=t_r[:, f, :], in0=t_r[:, f, :], scalar=1.0, in1=psnT[:, f, :],
                                             op0=ALU.add, op1=ALU.mult).then_inc(S["rp_done"], 1)
                for f in range(NF):
                    dve.wait_ge(S["cand_done"], n("cand_done", b, f + 1))
                    dve.tensor_tensor(cand[:, f, :], cand[:, f, :], xT[:, f, :], ALU.subtract)\
                       .then_inc(S["diff_done"], 1)
                    dve.wait_ge(S["diff_done"], n("diff_done", b, f + 1))
                    dve.scalar_tensor_tensor(out=t_u[:, f, :], in0=t_u[:, f, :], scalar=1.0, in1=cand[:, f, :],
                                             op0=ALU.add, op1=ALU.mult).then_inc(S["step_done"], 1)
                    dve.wait_ge(S["step_done"], n("step_done", b, f + 1))
                    dve.scalar_tensor_tensor(out=cand[:, f, :], in0=t_u[:, f, :], scalar=0.5, in1=xT[:, f, :],
                                             op0=ALU.mult, op1=ALU.add).then_inc(S["new_done"], 1)

                def new_state(t):
                    k = RINGS["bank"][2][("new", t // 2)] % 4
                    return bank[k][:, (t % 2) * D:(t % 2) * D + D]

                dve.wait_ge(S["y_stored"], n("y_stored", b, 0))
                norm("fin", new_state, lambda t: y_out[:, t, :], before=lambda t: full(dve, b, ("new", t // 2)))

        @block.tensor
        def _(pe):
            pe.wait_ge(w_in, N_LOAD)
            pe.wait_ge(consts, N_CONST)
            pe.wait_ge(consts_dve, N_CONST_DVE)
            pe.wait_ge(pads_in, N_PAD)
            with pe.Fori(0, B) as b:
                def turn(ln, use, src=xh):
                    for f in range(NF):
                        ps = free(pe, b, (use, f))
                        for t in range(NT):
                            if ln is not None and f == 0:
                                pe.wait_ge(S[f"{ln}_norm"], n(f"{ln}_norm", b, t + 1))
                            last = pe.transpose(ps[:, t * P:t * P + P], src[:, t, f * P:f * P + P], ident[:, :])
                        last.then_inc(filled((use, f)), 1)

                def project_T(use, f, w, at, rhs, ready, count):
                    ps = free(pe, b, (use, f))
                    for kt in range(NF):
                        pe.wait_ge(S[ready], n(ready, b, kt + 1))
                        last = pe.matmul(ps[:, :], w[:, kt, at + f * P:at + f * P + P], rhs[:, kt, :],
                                         start=(kt == 0), stop=(kt == NF - 1))
                    last.then_inc(filled((use, f)), 1)

                turn("ln1", "ln1T")
                for f in range(NF):
                    project_T("q", f, wqkv, 0, hT, "h1", NF)
                for f in range(NF):
                    project_T("k", f, wqkv, D, hT, "h1", NF)
                for i in range(2):
                    ps = free(pe, b, ("v", i))
                    for t in (2 * i, 2 * i + 1):
                        for kt in range(NF):
                            last = pe.matmul(ps[:, (t % 2) * D:(t % 2) * D + D], hT[:, kt, t * P:t * P + P],
                                             wqkv[:, kt, 2 * D:3 * D], start=(kt == 0), stop=(kt == NF - 1))
                    last.then_inc(filled(("v", i)), 1)

                ps = free(pe, b, ("ctxT", 0))
                pe.wait_ge(S["ctx_in"], n("ctx_in", b, 32))
                for c in range(NC):
                    last = pe.transpose(ps[0:CK[c], c * P:c * P + P], ctx_sb[:, c * P:c * P + CK[c]], ident[:, :])
                last.then_inc(filled(("ctxT", 0)), 1)
                pe.wait_ge(S["ctxT_done"], n("ctxT_done", b, 1))
                ps = free(pe, b, ("k2", 0))
                for f in range(NF):
                    for c in range(NC):
                        last = pe.matmul(ps[:, f * C:f * C + C], wkv_ca[0:CK[c], c, f * P:f * P + P],
                                         ctxT[0:CK[c], c, 0:C], start=(c == 0), stop=(c == NC - 1))
                last.then_inc(filled(("k2", 0)), 1)
                ps = free(pe, b, ("v2", 0))
                for c in range(NC):
                    last = pe.matmul(ps[:, 0:D], ctxT[0:CK[c], c, :], wkv_ca[0:CK[c], c, D:2 * D],
                                     start=(c == 0), stop=(c == NC - 1))
                last.then_inc(filled(("v2", 0)), 1)
                ps = free(pe, b, ("tokT", 0))
                for f in range(NF):
                    for c in range(NC):
                        last = pe.matmul(ps[:, f * C:f * C + C], wtok[0:CK[c], c, f * P:f * P + P],
                                         ctxT[0:CK[c], c, 0:C], start=(c == 0), stop=(c == NC - 1))
                last.then_inc(filled(("tokT", 0)), 1)
                ps = free(pe, b, ("tok", 0))
                for c in range(NC):
                    last = pe.matmul(ps[:, 0:D], ctxT[0:CK[c], c, :], wtok[0:CK[c], c, :],
                                     start=(c == 0), stop=(c == NC - 1))
                last.then_inc(filled(("tok", 0)), 1)

                pe.wait_ge(S["q_stacked"], n("q_stacked", b, PER["q_stacked"]))
                pe.wait_ge(S["k_stacked"], n("k_stacked", b, PER["k_stacked"]))
                for u, (qb, h0, per) in enumerate(MAX_UNITS):
                    w = (qb + 1) * P
                    ps = free(pe, b, ("max", u), "wide")
                    for i in range(2 * per):
                        e, m, at = i % 2, (h0 + i) // 2, (i // 2) * w
                        pe.matmul(ps[:, e, at:at + w], q_st[64 * e:64 * e + SA_K, m, qb * P:qb * P + P],
                                  k_st[64 * e:64 * e + SA_K, m, 0:w], start=True, stop=False)
                        last = pe.matmul(ps[:, e, at + qb * P:at + w], ident_bf[:, :], mask_bf[:, :],
                                         start=False, stop=True)
                    last.then_inc(filled(("max", u)), 1)

                def turn_max(use, ready):
                    ps = free(pe, b, (use, 0))
                    pe.wait_ge(S[ready], n(ready, b, 1))
                    for t in range(NT):
                        last = pe.transpose(ps[0:2 * H, t * P:t * P + P],
                                            nm2[:, t, :, :].bitcast(f32).rearrange("p a h -> p (a h)"), ident[:, :])
                    last.then_inc(filled((use, 0)), 1)

                def spread(use, g, out_done):
                    ps = free(pe, b, (use, g))
                    pe.wait_ge(S[out_done], n(out_done, b, g + 1))
                    pe.matmul(ps[:, :], sel[:, :], pv_sb[:, g % 2, :], start=True, stop=True)\
                      .then_inc(filled((use, g)), 1)

                def project_out(use, w, done):
                    for i in range(2):
                        ps = free(pe, b, (use, i))
                        for t in (2 * i, 2 * i + 1):
                            for g in range(NG):
                                pe.wait_ge(S[done], n(done, b, g + 1))
                                last = pe.matmul(ps[:, (t % 2) * D:(t % 2) * D + D], attT[:, g, t * P:t * P + P],
                                                 w[:, g, :], start=(g == 0), stop=(g == NG - 1))
                        last.then_inc(filled((use, i)), 1)

                turn_max("negmT", "nm_lo_done")
                pe.wait_ge(S["max_stacked"], n("max_stacked", b, 64))

                def weigh(s):
                    g, kb = s // NT, s % NT
                    ps = free(pe, b, ("pv", g)) if kb == 0 else bank[RINGS["bank"][2][("pv", g)] % 4]
                    pe.wait_ge(S["exp_done"], n("exp_done", b, 2 * s + 2))
                    for j in range(HG):
                        last = pe.matmul(ps[j * QW:j * QW + QW, kb * P:T], v_sa[:, kb, HG * g + j, :],
                                         probs[:, s % 2, j, kb * P:T], start=(kb == 0), stop=(kb == NT - 1))
                    last.then_inc(S["pv_used"], 1)

                pe.wait_ge(S["v_done"], n("v_done", b, 2))
                for s in range(NG * NT):
                    g, kb = s // NT, s % NT
                    for pr in range(2):
                        u = 2 * s + pr
                        ps = free(pe, b, ("st", u), "wide")
                        for i in range(2):
                            m = (HG * g + 2 * pr) // 2
                            pe.matmul(ps[:, i, 0:T - kb * P],
                                      k_st[64 * i:64 * i + SA_KM, m, kb * P:kb * P + P],
                                      q_st[64 * i:64 * i + SA_KM, m, kb * P:T], start=True, stop=False)
                        for i in range(2):
                            last = pe.matmul(ps[:, i, 0:P], ident_bf[:, :], maskT_bf[:, :], start=False, stop=True)
                        last.then_inc(filled(("st", u)), 1)
                    if s >= 1:
                        weigh(s - 1)
                    if kb == 1 and g >= 1:
                        spread("sum", g - 1, "pv_out")
                weigh(NG * NT - 1)
                spread("sum", NG - 1, "pv_out")
                project_out("proj", wproj_sa, "att_done")

                turn("ln2", "ln2T")
                for f in range(NF):
                    project_T("q2", f, wq_ca, 0, hT, "h2", NF)
                pe.wait_ge(S["q2_stacked"], n("q2_stacked", b, PER["q2_stacked"]))
                pe.wait_ge(S["k2_stacked"], n("k2_stacked", b, PER["k2_stacked"]))
                for t in range(NT):
                    ps = free(pe, b, ("max2", t), "wide")
                    for m in range(NP):
                        at = (m % 4) * 2 * C
                        last = pe.matmul(ps[:, m // 4, at:at + 2 * C], q2_st[0:CA_K, m, t * P:t * P + P],
                                         k2_st[0:CA_K, m, :], start=True, stop=True)
                    last.then_inc(filled(("max2", t)), 1)
                turn_max("negm2T", "nm2_lo_done")
                pe.wait_ge(S["max2_stacked"], n("max2_stacked", b, 64))
                for u in range(NP // 2):
                    ps = free(pe, b, ("st2", u), "wide")
                    for i in range(2):
                        last = pe.matmul(ps[:, i, :], k2_st[0:CA_KM, 2 * u + i, :], q2_st[0:CA_KM, 2 * u + i, :],
                                         start=True, stop=True)
                    last.then_inc(filled(("st2", u)), 1)
                pe.wait_ge(S["v2_done"], n("v2_done", b, 2))
                for g in range(NG):
                    ps = free(pe, b, ("pv2", g))
                    pe.wait_ge(S["exp2_done"], n("exp2_done", b, g + 1))
                    for i in range(2):
                        last = pe.matmul(ps[i * 2 * QW:i * 2 * QW + 2 * QW, :], v_ca[:, 2 * g + i, :],
                                         probs[:, g // 2, 2 * (g % 2) + i, :],
                                         start=True, stop=True)
                    last.then_inc(filled(("pv2", g)), 1)
                    if g >= 1:
                        spread("sum2", g - 1, "pv2_out")
                spread("sum2", NG - 1, "pv2_out")
                project_out("proj2", wproj_ca, "att2_done")

                turn("ln3", "ln3T")
                for u in range(NFF // 2):
                    ps = free(pe, b, ("ff1", u), "wide")
                    for i in range(2):
                        for kt in range(NF):
                            pe.wait_ge(S["h3"], n("h3", b, kt + 1))
                            f = 2 * u + i
                            last = pe.matmul(ps[:, i, :], wff1[:, kt, f * P:f * P + P], hT[:, kt, :],
                                             start=(kt == 0), stop=(kt == NF - 1))
                    last.then_inc(filled(("ff1", u)), 1)
                for i in range(2):
                    ps = free(pe, b, ("ff2", i))
                    for t in (2 * i, 2 * i + 1):
                        for f in range(NFF):
                            pe.wait_ge(S["gelu_done"], n("gelu_done", b, f + 1))
                            last = pe.matmul(ps[:, (t % 2) * D:(t % 2) * D + D], gT[:, f, t * P:t * P + P],
                                             wff2[:, f, :], start=(f == 0), stop=(f == NFF - 1))
                    last.then_inc(filled(("ff2", i)), 1)

                pe.wait_ge(S["x3_done"], n("x3_done", b, 2))
                turn(None, "xT", x3)
                ps = free(pe, b, ("route", 0))
                pe.wait_ge(S["xT_done"], n("xT_done", b, NF))
                pe.wait_ge(S["tokT_done"], n("tokT_done", b, NF))
                for t in range(NT):
                    for kt in range(NF):
                        last = pe.matmul(ps[:, t * C:t * C + C], xT[:, kt, t * P:t * P + P], tokT[:, kt, :],
                                         start=(kt == 0), stop=(kt == NF - 1))
                last.then_inc(filled(("route", 0)), 1)
                turn("psn", "psnT")
                ps = free(pe, b, ("routeT", 0))
                pe.wait_ge(S["rexp_done"], n("rexp_done", b, NT))
                for i in range(2):
                    last = pe.transpose(ps[:, i * P:i * P + P],
                                        route[:, 2 * i:2 * i + 2, :].rearrange("p t c -> p (t c)"), ident[:, :])
                last.then_inc(filled(("routeT", 0)), 1)
                pe.wait_ge(S["routeT_done"], n("routeT_done", b, 1))
                pe.wait_ge(S["tok_done"], n("tok_done", b, 1))
                for i in range(2):
                    ps = free(pe, b, ("routed", i))
                    rows = slice(i * C, i * C + C)
                    for t in (i, i + 2):
                        last = pe.matmul(ps[:, (t // 2) * D:(t // 2) * D + D], routeT[rows, t // 2, :], tok[rows, :],
                                         start=True, stop=True)
                    last.then_inc(filled(("routed", i)), 1)
                turn("inn", "innT")

                def gate(use, w, first, first_ready):
                    for f in range(NF):
                        ps = free(pe, b, (use, f))
                        for kt in range(2 * NF):
                            rhs, ready, c = ((first, first_ready, kt + 1) if kt < NF
                                             else (hT, "inn_done", kt - NF + 1))
                            pe.wait_ge(S[ready], n(ready, b, c))
                            last = pe.matmul(ps[:, :], w[:, kt, f * P:f * P + P], rhs[:, kt % NF, :],
                                             start=(kt == 0), stop=(kt == 2 * NF - 1))
                        last.then_inc(filled((use, f)), 1)

                gate("r", w_r, psnT, "psn_done")
                gate("u", w_u, psnT, "psn_done")
                gate("n", w_n, t_r, "rp_done")
                for i in range(2):
                    ps = free(pe, b, ("new", i))
                    pe.wait_ge(S["new_done"], n("new_done", b, NF))
                    for t in (2 * i, 2 * i + 1):
                        for f in range(NF):
                            at = (t % 2) * D + f * P
                            last = pe.transpose(ps[:, at:at + P], cand[:, f, t * P:t * P + P], ident[:, :])
                    last.then_inc(filled(("new", i)), 1)


_OUTS = [((16, 512, 256), 'float32')]


def kernel(**inputs):
    import numpy as _np
    import concourse.bacc as _bacc
    from concourse import mybir as _mybir
    from concourse.bass_utils import run_bass_kernel_spmd as _run

    names = ["x", "ctx_768"] + [f"L0_xattn_{w}" for w in (
        "Wqkv", "Wproj_sa", "bproj_sa", "g1", "b1", "Wq_ca", "Wkv_ca", "Wproj_ca", "bproj_ca", "g2", "b2", "Wff1",
        "bff1", "Wff2", "bff2", "g3", "b3")] + [f"L1_xattn_{w}" for w in (
            "W_proj", "b_proj", "g_state", "beta_state", "g_input", "beta_input", "g_out", "beta_out", "W_u", "b_u",
            "W_r", "b_r", "W_n", "b_n")]
    nc = _bacc.Bacc("TRN2", target_bir_lowering=False, num_devices=1)
    arrays, args = {}, []
    for name in names:
        a = _np.ascontiguousarray(inputs[name])
        arrays[f"in_{name}_dram"] = a
        args.append(nc.dram_tensor(f"in_{name}_dram", a.shape, _mybir.dt.from_np(a.dtype), kind="ExternalInput").ap())
    for i, (shape, dtype) in enumerate(_OUTS):
        dt = _mybir.dt.from_np(_np.dtype(dtype))
        args.append(nc.dram_tensor(f"out_{i}_dram", shape, dt, kind="ExternalOutput").ap())
    build(nc, *args)
    r = _run(nc, [arrays], core_ids=[0])
    return r.results[0]["out_0_dram"]
```

```python
import concourse.bass as bass
from concourse import mybir
from contextlib import ExitStack


def build(nc, x, ctx_768, l0_wqkv, l0_wproj_sa, l0_bproj_sa, l0_g1, l0_b1, l0_wq_ca, l0_wkv_ca, l0_wproj_ca,
          l0_bproj_ca, l0_g2, l0_b2, l0_wff1, l0_bff1, l0_wff2, l0_bff2, l0_g3, l0_b3, l1_w_proj, l1_b_proj,
          l1_g_state, l1_beta_state, l1_g_input, l1_beta_input, l1_g_out, l1_beta_out, l1_w_u, l1_b_u, l1_w_r,
          l1_b_r, l1_w_n, l1_b_n, out):
    f32 = mybir.dt.float32
    f32r = mybir.dt.float32r
    bf16 = mybir.dt.bfloat16
    ALU = mybir.AluOpType
    ACT = mybir.ActivationFunctionType
    AX = mybir.AxisListType

    B, T, D = x.shape
    C, DC = ctx_768.shape[1:]
    DFF = l0_wff1.shape[1]
    P = 128
    H = 16
    DH = D // H
    NT = T // P
    NF = D // P
    NFF = DFF // P
    NC = 2
    CK = [P, DC - P]
    HG = 4
    NG = H // HG
    NP = H // 2
    QW = 32
    EPS = 1e-5
    ATT_SCALE = float(DH) ** -0.5
    ROUTE_SCALE = float(D) ** -0.5
    MASKED = -1e30
    SA_K = 3 * DH
    SA_KM = SA_K + 2
    CA_K = 6 * DH
    CA_KM = CA_K + 4

    es = ExitStack()
    with es:
        def sb(name, shape, dt=f32):
            return es.enter_context(nc.sbuf_tensor(name, shape, dt))

        wqkv = sb("wqkv", [P, NF, 3 * D])
        wproj_sa = sb("wproj_sa", [P, NG, D])
        wproj_ca = sb("wproj_ca", [P, NG, D])
        wq_ca = sb("wq_ca", [P, NF, D])
        wkv_ca = sb("wkv_ca", [P, NC, 2 * D])
        wff1 = sb("wff1", [P, NF, DFF])
        wff2 = sb("wff2", [P, NFF, D])
        wtok = sb("wtok", [P, NC, D])
        w_u = sb("w_u", [P, 2 * NF, D])
        w_r = sb("w_r", [P, 2 * NF, D])
        w_n = sb("w_n", [P, 2 * NF, D])
        COLS = ["g1", "b1", "g2", "b2", "g3", "b3", "g_state", "beta_state", "g_input", "beta_input",
                "btok", "b_u", "b_r", "b_n"]
        cols_dram = [l0_g1, l0_b1, l0_g2, l0_b2, l0_g3, l0_b3, l1_g_state, l1_beta_state, l1_g_input,
                     l1_beta_input, l1_b_proj, l1_b_u, l1_b_r, l1_b_n]
        cols = sb("cols", [P, len(COLS), NF])
        bff1 = sb("bff1", [P, NFF])
        half_bias = sb("half_bias", [P, 2, NF])
        bff2_row = sb("bff2_row", [P, D])
        btok_row = sb("btok_row", [P, D])
        gout_row = sb("gout_row", [P, D])
        bout_row = sb("bout_row", [P, D])

        def col(name, f):
            return cols[:, COLS.index(name), f:f + 1]

        ident = sb("ident", [P, P])
        ident_bf = sb("ident_bf", [P, P], bf16)
        mask_bf = sb("mask_bf", [P, P], bf16)
        maskT_bf = sb("maskT_bf", [P, P], bf16)
        sel = sb("sel", [P, P])
        neg_half = sb("neg_half", [P, NT])
        mark = sb("mark", [P, 1])

        x_ln = sb("x_ln", [P, NT, D])
        x_res = sb("x_res", [P, NT, D])
        xs = sb("xs", [P, NT, D])
        stats = sb("stats", [P, NT, 6])
        mv = sb("mv", [P, NT, 2])
        ve = sb("ve", [P, NT])
        rstd = sb("rstd", [P, NT])
        xh = sb("xh", [P, NT, D])
        hT_a = sb("hT_a", [P, NF, T])
        hT = sb("hT", [P, NF, T])
        psnT = sb("psnT", [P, NF, T])
        part_hi = sb("part_hi", [P, NF, T], f32r)
        part_lo = sb("part_lo", [P, NF, T], f32r)
        q_st = sb("q_st", [P, NP, T], f32r)
        k_st = sb("k_st", [P, NP, T], f32r)
        q2_st = sb("q2_st", [P, NP, T], f32r)
        v_sa = sb("v_sa", [P, NT, H, QW])
        negm = sb("negm", [P, NT, H])
        negm2 = sb("negm2", [P, NT, H])
        nm2 = sb("nm2", [P, NT, 2, H], f32r)
        nmT = sb("nmT", [2 * H, T], f32r)
        gT = sb("gT", [P, NFF, T])
        probs = gT[:, :, :].rearrange("p (s h) t -> p s h t", s=2)
        pv_sb = sb("pv_sb", [P, 2, T])
        attT = sb("attT", [P, NG, T])
        ctx_sb = sb("ctx_sb", [P, DC])
        ctxT = sb("ctxT", [P, NC, P])
        k2_hi = sb("k2_hi", [P, NF, C], f32r)
        k2_lo = sb("k2_lo", [P, NF, C], f32r)
        k2_st = sb("k2_st", [P, NP, 2 * C], f32r)
        v_ca = sb("v_ca", [P, NP, 2 * QW])
        tokT = sb("tokT", [P, NF, C])
        tok = sb("tok", [P, D])
        xT = sb("xT", [P, NF, T])
        rmax = sb("rmax", [P, 2 * NT])
        rden = sb("rden", [P, 2 * NT])
        route = sb("route", [P, NT, C])
        routeT = sb("routeT", [P, 2, P])
        t_r = sb("t_r", [P, NF, T])
        t_u = sb("t_u", [P, NF, T])
        cand = sb("cand", [P, NF, T])
        xh_a = t_r[:, :, :].rearrange("p a (b d) -> p (a b) d", d=D)
        routed = cand[:, :, :].rearrange("p a (b d) -> p (a b) d", d=D)
        d_q = nc.dram_tensor("d_q", [2, D, T], f32, kind="Internal").ap()
        d_k = nc.dram_tensor("d_k", [2, D, T], f32, kind="Internal").ap()
        d_q2 = nc.dram_tensor("d_q2", [2, D, T], f32, kind="Internal").ap()
        d_k2 = nc.dram_tensor("d_k2", [2, D, C], f32, kind="Internal").ap()

        bank = [es.enter_context(nc.psum_tensor(f"bank{k}", [P, 512], f32)) for k in range(3)]
        acc = [es.enter_context(nc.psum_tensor("acc0", [P, 512], f32))]
        wide = [es.enter_context(nc.psum_tensor(f"wide{k}", [P, 2, 512], f32)) for k in range(2)]

        MAX_UNITS = []
        for qb in range(NT):
            per = T // ((qb + 1) * P)
            MAX_UNITS += [(qb, h, per) for h in range(0, H, 2 * per)]
        ST_UNITS = [(g, kb, pr) for g in range(NG) for kb in range(NT) for pr in range(2)]

        def A(name, i=0):
            return ("A", name, i)

        def Bs(name, i=0):
            return ("B", name, i)

        def maxes(lo, hi):
            return [A("max", u) for u in range(lo, hi)]

        NMAX = len(MAX_UNITS)
        NS = NG * NT
        ORDER = (
            [A("load_a"), Bs("load_b"), A("ln1_stat"), A("ln1_norm"), Bs("proj", 0), Bs("proj", 1), Bs("ln2_stat"),
             A("ln1T"), A("q"), Bs("ln2_norm"), A("k"), Bs("ctxT"), Bs("k2"), Bs("ln2T"), Bs("q2"), Bs("v2"), A("stack"),
             Bs("stack2"), A("v"), Bs("tokT"), Bs("tok")]
            + maxes(0, 1) + [Bs("max2", 0)] + maxes(1, 2) + [Bs("max2", 1)] + maxes(2, 3) + [Bs("max2", 2)]
            + maxes(3, 4) + [Bs("max2", 3), Bs("negm2")] + maxes(4, 8)
            + [Bs("st2", 0), Bs("st2", 1), Bs("pv2", 0)] + maxes(8, 9) + [Bs("st2", 2), Bs("pv2", 1), Bs("norm2", 0)]
            + [Bs("st2", 3), Bs("pv2", 2), Bs("norm2", 1)] + maxes(9, 10) + [Bs("pv2", 3), Bs("norm2", 2)]
            + maxes(10, 11) + [Bs("norm2", 3), Bs("proj2", 0), Bs("proj2", 1), Bs("ln3_stat")] + maxes(11, 13)
            + [Bs("ln3_norm")] + maxes(13, 14) + [Bs("ln3T")])
        for f in range(NFF):
            ORDER += [Bs("ff1", f)] + maxes(14 + f, 15 + f)
        ORDER += [Bs("ff2", 0), A("negm"), Bs("ff2", 1), Bs("ff2", 2), Bs("ff2", 3)]
        assert 14 + NFF == NMAX
        AFTER = {
            0: ["psn_stat", "xT", "route"], 1: ["psn_norm"], 2: ["psnT"], 3: ["routeT"], 4: ["routed", "inn_stat"],
            5: ["inn_norm"], 6: ["innT"], 7: [("r", 0)], 8: [("r", 1)], 9: [("u", 0)], 10: [("u", 1)],
            11: [("n", 0)], 12: [("n", 1)], 14: ["new", "fin_stat"], 15: ["fin_norm"]}
        for st in range(NS):
            ORDER += [A("st", st)]
            if st:
                ORDER += [A("pv", st - 1)]
            if st and st % NT == 0:
                ORDER += [A("take", st // NT - 1)]
            if st % NT == 1 and st > 1:
                ORDER += [A("norm", st // NT - 1)]
            ORDER += [Bs(x) if isinstance(x, str) else Bs(*x) for x in AFTER.get(st, [])]
        ORDER += [A("pv", NS - 1), A("take", NG - 1), A("norm", NG - 1)]
        PHASES = {"first": [x for x in ORDER if x[0] == "A"], "loop": ORDER,
                  "last": [x for x in ORDER if x[0] == "B"]}

        PER, BASE, S = {}, {}, {}

        def sem(name, per, base=0):
            PER[name], BASE[name] = per, base
            S[name] = es.enter_context(nc.semaphore(name))

        def n(name, b, c):
            j, off = b
            assert off * PER[name] + BASE[name] + c > 0, "a wait for nothing"
            return j * PER[name] + (off * PER[name] + BASE[name] + c)

        for ln in ("ln1", "ln2", "ln3", "psn", "inn", "fin"):
            sem(f"{ln}_var", NT + 1)
            sem(f"{ln}_rstd", 1)
            sem(f"{ln}_norm", NT, 1 if ln == "fin" else 0)
        for name, per in [
            ("x_in", 16), ("x_res_in", 16), ("ctx_in", 32),
            ("h1", NF), ("h2", NF), ("h3", NF), ("psn_done", NF), ("inn_done", NF), ("xT_done", NF),
            ("q_hi_done", NF), ("k_hi_done", NF), ("q_lo_done", NF), ("k_lo_done", NF),
            ("q_hi_out", 16 * NF), ("q_lo_out", 16 * NF), ("k_hi_out", 16 * NF), ("k_lo_out", 16 * NF),
            ("q2_hi_out", 16 * NF), ("q2_lo_out", 16 * NF), ("k2_hi_out", 16), ("k2_lo_out", 16),
            ("q_stacked", 16 * 6), ("k_stacked", 16 * 6), ("q2_stacked", 16 * 6), ("k2_stacked", 16 * 12),
            ("v_done", 2), ("ctxT_done", 1), ("k2_hi_done", 1), ("k2_lo_done", 1), ("v2_done", 2),
            ("tokT_done", NF), ("tok_done", 1),
            ("max_done", len(MAX_UNITS)), ("nm_hi_done", 1), ("nm_lo_done", 1), ("nmT_done", 1),
            ("max_stacked", 64),
            ("exp_done", len(ST_UNITS)), ("pv_used", NG * NT),
            ("pv_out", NG), ("rsum_done", NG), ("att_done", NG), ("x1_done", 2),
            ("q2_hi_done", NF), ("q2_lo_done", NF),
            ("max2_done", NT), ("nm2_hi_done", 1), ("nm2_lo_done", 1), ("nmT2_done", 1), ("max2_stacked", 64),
            ("exp2_done", NP // 2), ("pv2_out", NG), ("rsum2_done", NG), ("att2_done", NG), ("x2_done", 2),
            ("x2b_done", 1), ("gelu_done", NFF), ("x3_done", NT),
            ("rmax_done", 1), ("rbias_done", 1), ("rexp_done", NT), ("rtotal_done", 1), ("rden_done", 1),
            ("routeT_done", 1), ("routed_done", NT), ("tr_done", NF), ("tu_done", NF), ("rp_done", NF),
            ("cand_done", NF), ("diff_done", NF), ("step_done", NF), ("new_done", NF), ("gained", 1),
            ("y_done", 1),
        ]:
            sem(name, per)
        sem("y_stored", 16)
        sem("y_left", 1, 1)

        BANK_OF = {
            "ln1T": [(("ln1T", f), ("h1", f + 1)) for f in range(NF)],
            "q": [(("q", f), ("q_lo_done", f + 1)) for f in range(NF)],
            "k": [(("k", f), ("k_lo_done", f + 1)) for f in range(NF)],
            "v": [(("v", i), ("v_done", i + 1)) for i in range(2)],
            "negm": [(("negmT", 0), ("nmT_done", 1))],
            "ctxT": [(("ctxT", 0), ("ctxT_done", 1))],
            "k2": [(("k2", 0), ("k2_lo_done", 1))],
            "v2": [(("v2", 0), ("v2_done", 2))],
            "tokT": [(("tokT", 0), ("tokT_done", NF))],
            "tok": [(("tok", 0), ("tok_done", 1))],
            "ln2T": [(("ln2T", f), ("h2", f + 1)) for f in range(NF)],
            "q2": [(("q2", f), ("q2_lo_done", f + 1)) for f in range(NF)],
            "negm2": [(("negm2T", 0), ("nmT2_done", 1))],
            "ln3T": [(("ln3T", f), ("h3", f + 1)) for f in range(NF)],
            "xT": [(("xT", f), ("xT_done", f + 1)) for f in range(NF)],
            "route": [(("route", 0), ("rexp_done", NT))],
            "psnT": [(("psnT", f), ("psn_done", f + 1)) for f in range(NF)],
            "routeT": [(("routeT", 0), ("routeT_done", 1))],
            "routed": [(("routed", i), ("routed_done", 2 * i + 2)) for i in range(2)],
            "innT": [(("innT", f), ("inn_done", f + 1)) for f in range(NF)],
            "new": [(("new", i), ("fin_norm", 2 * i + 2)) for i in range(2)],
        }
        for g in range(NG):
            BANK_OF["norm", g] = [(("sum", g), ("rsum_done", g + 1))]
            BANK_OF["pv2", g] = [(("pv2", g), ("pv2_out", g + 1))]
            BANK_OF["norm2", g] = [(("sum2", g), ("rsum2_done", g + 1))]
        for i in range(2):
            BANK_OF["proj", i] = [(("proj", i), ("x1_done", i + 1))]
            BANK_OF["proj2", i] = [(("proj2", i), ("x2_done", i + 1))]
            BANK_OF["r", i] = [(("r", i), ("tr_done", i + 1))]
            BANK_OF["u", i] = [(("u", i), ("tu_done", i + 1))]
            BANK_OF["n", i] = [(("n", i), ("cand_done", i + 1))]
        for f in range(NFF):
            BANK_OF["ff1", f] = [(("ff1", f), ("gelu_done", f + 1))]
        for t in range(NT):
            BANK_OF["ff2", t] = [(("ff2", t), ("x3_done", t + 1))]
        ACC_OF = {("pv", NT * g): [(("pv", g), ("pv_out", g + 1))] for g in range(NG)}
        WIDE_OF = {("max", u): [(("max", u), ("max_done", u + 1))] for u in range(len(MAX_UNITS))}
        WIDE_OF.update({("st", st): [(("st", u), ("exp_done", u + 1)) for u in (2 * st, 2 * st + 1)]
                        for st in range(NS)})
        WIDE_OF.update({("max2", t): [(("max2", t), ("max2_done", t + 1))] for t in range(NT)})
        WIDE_OF.update({("st2", u): [(("st2", u), ("exp2_done", u + 1))] for u in range(NP // 2)})
        BY_STEPS = {("pv", g): ("pv_used", NT * (g + 1)) for g in range(NG)}

        PLACE = {}
        LAST = {}
        FILLS = {}
        for ring, tiles, of in (("bank", bank, BANK_OF), ("acc", acc, ACC_OF), ("wide", wide, WIDE_OF)):
            for phase, steps in PHASES.items():
                k = 0
                for stage, name, i in steps:
                    for use, reader in of.get((name, i), of.get(name, []) if i == 0 else []):
                        before = LAST.get((phase, ring, k))
                        fills = FILLS.get((phase, ring, k), 0) + (use not in BY_STEPS)
                        PLACE[phase, use] = (ring, k, before, fills)
                        FILLS[phase, ring, k] = fills
                        LAST[phase, ring, k] = (stage, *reader)
                        k = (k + 1) % len(tiles)
            for k in range(len(tiles)):
                sem(f"{ring}_full{k}", FILLS["loop", ring, k])
        TILES = {"bank": bank, "acc": acc, "wide": wide}

        class Now:

            def __init__(self):
                self.phase, self.j = "first", 0

            def batch(self, stage):
                return {"first": (0, 0), "loop": (self.j, 1 if stage == "A" else 0), "last": (0, B - 1)}[self.phase]

        def free(pe, now, b, use):
            ring, k, before, _ = PLACE[now.phase, use]
            if before is not None:
                stage, name, c = before
                pe.wait_ge(S[name], n(name, now.batch(stage), c))
            elif now.phase != "first":
                j, ahead = (now.j, 1) if now.phase == "loop" else (0, B)
                for phase in ("first", "loop"):
                    if (phase, ring, k) in LAST:
                        stage, name, _ = LAST[phase, ring, k]
                        pe.wait_ge(S[name], n(name, (j, ahead if stage == "A" else ahead - 1), 0))
            return TILES[ring][k]

        def filled(now, use):
            ring, k, _, _ = PLACE[now.phase, use]
            return S[BY_STEPS[use][0]] if use in BY_STEPS else S[f"{ring}_full{k}"]

        def full(eng, now, use):
            ring, k, _, fills = PLACE[now.phase, use]
            if use in BY_STEPS:
                name, c = BY_STEPS[use]
                eng.wait_ge(S[name], n(name, now.batch("A"), c))
            else:
                ahead = FILLS.get(("first", ring, k), 0)
                if now.phase == "first":
                    eng.wait_ge(S[f"{ring}_full{k}"], fills)
                else:
                    j, off = (now.j, 0) if now.phase == "loop" else (0, B - 1)
                    eng.wait_ge(S[f"{ring}_full{k}"], n(f"{ring}_full{k}", (j, off), ahead + fills))
            return TILES[ring][k]

        def outs_batch(now, b, use):
            if use == "q2":
                return now.batch("A") if now.phase == "loop" else (0, B - 1)
            return b

        def run(eng, now, steps):
            for stage, name, i in PHASES["first"]:
                if name in steps:
                    steps[name](now.batch(stage), i)
            now.phase = "loop"
            with eng.Fori(0, B - 1) as j:
                now.j = j
                for stage, name, i in PHASES["loop"]:
                    if name in steps:
                        steps[name](now.batch(stage), i)
            now.phase, now.j = "last", 0
            for stage, name, i in PHASES["last"]:
                if name in steps:
                    steps[name](now.batch(stage), i)

        w_in = es.enter_context(nc.semaphore("w_in"))
        zeroed = es.enter_context(nc.semaphore("zeroed"))
        pads_in = es.enter_context(nc.semaphore("pads_in"))
        consts = es.enter_context(nc.semaphore("consts"))
        consts_dve = es.enter_context(nc.semaphore("consts_dve"))
        N_ZERO, N_CONST, N_CONST_DVE, N_PAD = 9, 6, 11, 16 * 2 * (HG + 1)
        N_LOAD = 16 * (len(COLS) + 1 + 4 + 7 + 2 * NC)

        block = es.enter_context(nc.Block())
        x_v = x.rearrange("b (t p) d -> b p t d", p=P)
        out_v = out.rearrange("b (t p) d -> b p t d", p=P)

        @block.sync
        def _(sp):
            loads = []

            def load(dst, src):
                loads.append(16)
                sp.dma_start(dst, src).then_inc(w_in, 16)

            with nc.allow_non_contiguous_dma(reason="vectors over features, once"):
                for i, v in enumerate(cols_dram):
                    load(cols[:, i, :], v.rearrange("(f p) -> p f", p=P))
                load(bff1[:, :], l0_bff1.rearrange("(f p) -> p f", p=P))
            for row, v in ((bff2_row, l0_bff2), (btok_row, l1_b_proj), (gout_row, l1_g_out),
                           (bout_row, l1_beta_out)):
                load(row[:, :], v.rearrange("(a n) -> a n", a=1).broadcast_to((P, D)))
            for dst, w in ((wqkv, l0_wqkv), (wq_ca, l0_wq_ca), (wff1, l0_wff1), (wff2, l0_wff2), (w_u, l1_w_u),
                           (w_r, l1_w_r), (w_n, l1_w_n)):
                load(dst[:, :, :], w.rearrange("(f p) n -> p f n", p=P))
            for c in range(NC):
                load(wkv_ca[0:CK[c], c, :], l0_wkv_ca[c * P:c * P + CK[c], :])
                load(wtok[0:CK[c], c, :], l1_w_proj[c * P:c * P + CK[c], :])
            assert sum(loads) == N_LOAD
            sp.wait_ge(zeroed, N_ZERO)
            for dst, w, bias in ((wproj_sa, l0_wproj_sa, l0_bproj_sa), (wproj_ca, l0_wproj_ca, l0_bproj_ca)):
                wv = w.rearrange("(g j d) n -> j d g n", j=HG, d=DH)
                for j in range(HG):
                    sp.dma_start(dst[j * QW:j * QW + DH, :, :], wv[j]).then_inc(pads_in, 16)
                sp.dma_start(dst[DH:DH + 1, 0, :], bias.rearrange("(a n) -> a n", a=1)).then_inc(pads_in, 16)

            now = Now()

            def load_a(b, _):
                if now.phase != "first":
                    sp.wait_ge(S["ln1_norm"], n("ln1_norm", b, 0))
                sp.dma_start(x_ln[:, :, :], x_v[b[0] + b[1]]).then_inc(S["x_in"], 16)

            def load_b(b, _):
                sp.dma_start(x_res[:, :, :], x_v[b[0] + b[1]]).then_inc(S["x_res_in"], 16)
                for half in range(2):
                    sp.dma_start(ctx_sb[half * C:half * C + C, :], ctx_768[b[0] + b[1]]).then_inc(S["ctx_in"], 16)

            def parts_out(b, name, dram):
                for f in range(NF):
                    for p, part in enumerate(("hi", "lo")):
                        src = (part_hi, part_lo)[p]
                        sp.wait_ge(S[f"{name}_{part}_done"], n(f"{name}_{part}_done", b, f + 1))
                        sp.dma_start(dram[p, f * P:f * P + P, :], src[:, f, :].bitcast(f32))\
                          .then_inc(S[f"{name}_{part}_out"], 16)

            def stack(b, name, dram, slots, dst, base_odd):
                for p, part in enumerate(("hi", "lo")):
                    out_sem = f"{name}_{part}_out"
                    sp.wait_ge(S[out_sem], n(out_sem, b, 16 * NF))
                    src = dram[p].rearrange("(m e d) t -> e d m t", e=2, d=DH)
                    for slot, of in enumerate(slots):
                        if of == p:
                            for e in range(2):
                                row = e * base_odd + slot * DH
                                sp.dma_start(dst[row:row + DH, :, :].bitcast(f32), src[e])\
                                  .then_inc(S[f"{name}_stacked"], 16)

            def stack_a(b, _):
                stack(b, "q", d_q, (0, 0, 1), q_st, P // 2)
                stack(b, "k", d_k, (0, 1, 0), k_st, P // 2)

            def k2_out(b, _):
                for p, part in enumerate(("hi", "lo")):
                    sp.wait_ge(S[f"k2_{part}_done"], n(f"k2_{part}_done", b, 1))
                    sp.dma_start(d_k2[p].rearrange("(f p) c -> p f c", p=P), (k2_hi, k2_lo)[p][:, :, :].bitcast(f32))\
                      .then_inc(S[f"k2_{part}_out"], 16)

            def stack_b(b, _):
                stack(b, "q2", d_q2, (0, 0, 1), q2_st, 3 * DH)
                for p, part in enumerate(("hi", "lo")):
                    out_sem = f"k2_{part}_out"
                    sp.wait_ge(S[out_sem], n(out_sem, b, 16))
                    src = d_k2[p].rearrange("(m e d) c -> e d m c", e=2, d=DH)
                    for slot, of in enumerate((0, 1, 0)):
                        if of == p:
                            for e in range(2):
                                row = e * 3 * DH + slot * DH
                                for half in range(2):
                                    sp.dma_start(k2_st[row:row + DH, 4 * half:4 * half + 4, e * C:e * C + C].bitcast(f32),
                                                 src[e][:, 4 * half:4 * half + 4, :]).then_inc(S["k2_stacked"], 16)

            def maxima(b, ready, done, dst, row_of):
                sp.wait_ge(S[ready], n(ready, b, 1))
                for part in range(4):
                    row = row_of(part)
                    sp.dma_start(dst[row:row + 1, :, :].bitcast(f32), nmT[part * NP:part * NP + NP, :].bitcast(f32))\
                      .then_inc(S[done], 16)

            run(sp, now, {
                "load_a": load_a, "load_b": load_b,
                "q": lambda b, _: parts_out(b, "q", d_q),
                "k": lambda b, _: parts_out(b, "k", d_k),
                "q2": lambda b, _: parts_out(b, "q2", d_q2),
                "stack": stack_a, "k2": k2_out, "stack2": stack_b,
                "negm": lambda b, _: maxima(b, "nmT_done", "max_stacked", q_st, lambda p: p // 2 * 64 + SA_K + p % 2),
                "negm2": lambda b, _: maxima(b, "nmT2_done", "max2_stacked", q2_st, lambda p: CA_K + p),
            })

        @block.gpsimd
        def _(pool):
            for tile in (wproj_sa, wproj_ca, v_sa):
                pool.memset(tile[:], 0.0).then_inc(zeroed, 1)
            for tile in (ident, ident_bf, sel, mask_bf, maskT_bf, v_ca):
                pool.memset(tile[:], 0.0).then_inc(zeroed, 1)
            pool.memset(neg_half[:, :], -0.5).then_inc(consts, 1)
            pool.wait_ge(zeroed, N_ZERO)
            pool.affine_select(out=ident[:, :], in_=ident[:, :], compare_op=ALU.not_equal, fill=1.0, base=0,
                               pattern=[[-1, P]], channel_multiplier=1).then_inc(consts, 1)
            pool.affine_select(out=ident_bf[:, :], in_=ident_bf[:, :], compare_op=ALU.not_equal, fill=1.0, base=0,
                               pattern=[[-1, P]], channel_multiplier=1).then_inc(consts, 1)
            sel_v = sel[:, :].rearrange("p (j c) -> p j c", j=HG)
            pool.affine_select(out=sel_v, in_=sel_v, compare_op=ALU.not_equal, fill=1.0, base=-DH,
                               pattern=[[-QW, HG], [0, QW]], channel_multiplier=1).then_inc(consts, 1)
            pool.affine_select(out=mask_bf[:, :], in_=mask_bf[:, :], compare_op=ALU.is_ge, fill=MASKED, base=0,
                               pattern=[[-1, P]], channel_multiplier=1).then_inc(consts, 1)
            pool.affine_select(out=maskT_bf[:, :], in_=maskT_bf[:, :], compare_op=ALU.is_ge, fill=MASKED, base=0,
                               pattern=[[1, P]], channel_multiplier=-1).then_inc(consts, 1)

            pool.wait_ge(consts, N_CONST)
            now = Now()

            def root(ln):
                def step(b, _):
                    pool.wait_ge(S[f"{ln}_var"], n(f"{ln}_var", b, NT + 1))
                    pool.tensor_tensor(rstd[:, :], ve[:, :], neg_half[:, :], ALU.pow).then_inc(S[f"{ln}_rstd"], 1)
                return step

            def hidden_bias(b, _):
                pool.wait_ge(S["ln3_norm"], n("ln3_norm", b, NT))
                for t in range(NT):
                    last = pool.tensor_tensor(xs[:, t, :], xs[:, t, :], bff2_row[:, :], ALU.add)
                last.then_inc(S["x2b_done"], 1)

            def finish(b, _):
                pool.wait_ge(S["fin_norm"], n("fin_norm", b, NT))
                for t in range(NT):
                    last = pool.tensor_tensor(xs[:, t, :], xs[:, t, :], gout_row[:, :], ALU.mult)
                last.then_inc(S["gained"], 1)
                pool.wait_ge(S["gained"], n("gained", b, 1))
                for t in range(NT):
                    last = pool.tensor_tensor(xs[:, t, :], xs[:, t, :], bout_row[:, :], ALU.add)
                last.then_inc(S["y_done"], 1)
                pool.wait_ge(S["y_done"], n("y_done", b, 1))
                pool.dma_start(out_v[b[0] + b[1]], xs[:, :, :]).then_inc(S["y_stored"], 16)
                pool.wait_ge(S["y_stored"], n("y_stored", b, 16))
                pool.tensor_tensor(mark[:, :], neg_half[:, 0:1], neg_half[:, 0:1], ALU.mult).then_inc(S["y_left"], 1)

            run(pool, now, {**{f"{ln}_stat": root(ln) for ln in ("ln1", "ln2", "ln3", "psn", "inn", "fin")},
                            "ln3_norm": hidden_bias, "fin_norm": finish})
            pool.wait_ge(S["y_stored"], n("y_stored", (0, B), 0))

        @block.scalar
        def _(act):
            act.wait_ge(w_in, N_LOAD)
            act.wait_ge(consts_dve, N_CONST_DVE)
            act.wait_ge(consts, N_CONST)
            now = Now()

            def turned(use, dst, done, gain, bias):
                def step(b, _):
                    for f in range(NF):
                        ps = full(act, now, (use, f))
                        act.activation(dst[:, f, :], ps[:, :], ACT.Identity, scale=col(gain, f), bias=col(bias, f))\
                           .then_inc(S[done], 1)
                return step

            def high(use, before):
                def step(b, _):
                    for f in range(NF):
                        ps = full(act, now, (use, f))
                        if before is not None and f == 0:
                            ob = outs_batch(now, b, use)
                            act.wait_ge(S[f"{before}_lo_done"], n(f"{before}_lo_done", ob, NF))
                            act.wait_ge(S[f"{before}_hi_out"], n(f"{before}_hi_out", ob, 16 * NF))
                        act.activation(part_hi[:, f, :], ps[:, :], ACT.Copy).then_inc(S[f"{use}_hi_done"], 1)
                return step

            def values(b, _):
                for i in range(2):
                    ps = full(act, now, ("v", i))
                    for t in range(2):
                        last = act.activation(v_sa[:, 2 * i + t, :, 0:DH],
                                              ps[:, t * D:t * D + D].rearrange("p (h d) -> p h d", h=H), ACT.Copy)
                    last.then_inc(S["v_done"], 1)

            def ctx_turned(b, _):
                ps = full(act, now, ("ctxT", 0))
                act.activation(ctxT[:, 0, :], ps[:, 0:P], ACT.Copy)
                act.activation(ctxT[0:CK[1], 1, :], ps[0:CK[1], P:2 * P], ACT.Copy).then_inc(S["ctxT_done"], 1)

            def keys2_high(b, _):
                ps = full(act, now, ("k2", 0))
                act.activation(k2_hi[:, :, :], ps[:, 0:NF * C].rearrange("p (f c) -> p f c", f=NF), ACT.Copy)\
                   .then_inc(S["k2_hi_done"], 1)

            def values2(b, _):
                ps = full(act, now, ("v2", 0))
                for e in range(2):
                    rows = slice(e * C, e * C + C)
                    act.activation(v_ca[rows, :, e * QW:e * QW + DH],
                                   ps[rows, 0:D].rearrange("p (t e d) -> p e t d", e=2, d=DH)[:, e], ACT.Copy)\
                       .then_inc(S["v2_done"], 1)

            def tokens_turned(b, _):
                ps = full(act, now, ("tokT", 0))
                for f in range(NF):
                    act.activation(tokT[:, f, :], ps[:, f * C:f * C + C], ACT.Identity, bias=col("btok", f))\
                       .then_inc(S["tokT_done"], 1)

            def out_of(use, done, att):
                def step(b, g):
                    ps = full(act, now, (use, g))
                    if g >= 2:
                        act.wait_ge(S[att], n(att, b, g - 1))
                    act.activation(pv_sb[:, g % 2, :], ps[:, :], ACT.Copy).then_inc(S[done], 1)
                return step

            def maxima(use, done):
                def step(b, _):
                    ps = full(act, now, (use, 0))
                    act.activation(nmT[:, :], ps[0:2 * H, :], ACT.Copy).then_inc(S[done], 1)
                return step

            def exps(b, st):
                kb = st % NT
                for pr in range(2):
                    ps = full(act, now, ("st", 2 * st + pr))
                    if st >= 2:
                        act.wait_ge(S["pv_used"], n("pv_used", b, st - 1))
                    act.activation(probs[:, st % 2, 2 * pr:2 * pr + 2, kb * P:T], ps[:, :, 0:T - kb * P], ACT.Exp,
                                   scale=ATT_SCALE).then_inc(S["exp_done"], 1)

            def exps2(b, u):
                ps = full(act, now, ("st2", u))
                act.activation(probs[:, u // 2, 2 * (u % 2):2 * (u % 2) + 2, :], ps[:, :, :], ACT.Exp,
                               scale=ATT_SCALE).then_inc(S["exp2_done"], 1)

            def gelu(b, f):
                ps = full(act, now, ("ff1", f))
                act.activation(gT[:, f, :], ps[:, :], ACT.Gelu, bias=bff1[:, f:f + 1]).then_inc(S["gelu_done"], 1)

            def state_turned(b, _):
                for f in range(NF):
                    ps = full(act, now, ("xT", f))
                    act.activation(xT[:, f, :], ps[:, :], ACT.Copy).then_inc(S["xT_done"], 1)

            def route_exps(b, _):
                ps = full(act, now, ("route", 0))
                act.wait_ge(S["rbias_done"], n("rbias_done", b, 1))
                for t in range(NT):
                    act.activation(route[:, t, :], ps[:, t * C:t * C + C], ACT.Exp, bias=rmax[:, NT + t:NT + t + 1],
                                   scale=ROUTE_SCALE).then_inc(S["rexp_done"], 1)

            def route_turned(b, _):
                ps = full(act, now, ("routeT", 0))
                act.activation(routeT[:, :, :], ps[:, 0:2 * P].rearrange("p (i c) -> p i c", i=2), ACT.Copy)\
                   .then_inc(S["routeT_done"], 1)

            def gate(i, use, dst, done):
                def step(b, f):
                    ps = full(act, now, (use, f))
                    act.activation(dst[:, f, :], ps[:, :], ACT.Tanh, scale=0.5, bias=half_bias[:, i, f:f + 1])\
                       .then_inc(S[done], 1)
                return step

            def candidate(b, f):
                ps = full(act, now, ("n", f))
                act.activation(cand[:, f, :], ps[:, :], ACT.Tanh, bias=col("b_n", f)).then_inc(S["cand_done"], 1)

            run(act, now, {
                "ln1T": turned("ln1T", hT_a, "h1", "g1", "b1"),
                "q": high("q", None), "k": high("k", "q"), "q2": high("q2", "k"),
                "v": values, "ctxT": ctx_turned, "k2": keys2_high, "v2": values2, "tokT": tokens_turned,
                "ln2T": turned("ln2T", hT, "h2", "g2", "b2"),
                "ln3T": turned("ln3T", hT, "h3", "g3", "b3"),
                "psnT": turned("psnT", psnT, "psn_done", "g_state", "beta_state"),
                "innT": turned("innT", hT, "inn_done", "g_input", "beta_input"),
                "negm": maxima("negmT", "nmT_done"), "negm2": maxima("negm2T", "nmT2_done"),
                "st": exps, "st2": exps2,
                "take": out_of("pv", "pv_out", "att_done"), "norm2": out_of("pv2", "pv2_out", "att2_done"),
                "ff1": gelu, "xT": state_turned, "route": route_exps, "routeT": route_turned,
                "r": gate(0, "r", t_r, "tr_done"), "u": gate(1, "u", t_u, "tu_done"), "n": candidate,
            })

        @block.vector
        def _(dve):
            dve.memset(k_st[:, :, :].bitcast(f32), 1.0).then_inc(consts_dve, 1)
            dve.memset(k2_st[:, :, :].bitcast(f32), 0.0).then_inc(consts_dve, 1)
            dve.wait_ge(consts_dve, 2)
            dve.memset(k2_st[CA_K:CA_K + 2, :, 0:C].bitcast(f32), 1.0).then_inc(consts_dve, 1)
            dve.memset(k2_st[CA_K:CA_KM, :, C:2 * C].bitcast(f32), 1.0).then_inc(consts_dve, 1)
            dve.wait_ge(consts_dve, 4)
            dve.memset(k2_st[CA_K:CA_K + 2, :, C:2 * C].bitcast(f32), 0.0).then_inc(consts_dve, 1)
            dve.wait_ge(zeroed, N_ZERO)
            dve.memset(v_sa[:, :, :, DH:DH + 1], 1.0).then_inc(consts_dve, 1)
            dve.memset(v_ca[0:C, :, DH:DH + 1], 1.0).then_inc(consts_dve, 1)
            dve.memset(v_ca[C:2 * C, :, QW + DH:QW + DH + 1], 1.0).then_inc(consts_dve, 1)
            dve.wait_ge(w_in, N_LOAD)
            dve.tensor_scalar(half_bias[:, 0, :], cols[:, COLS.index("b_r"), :], 0.5, None, ALU.mult)\
               .then_inc(consts_dve, 1)
            dve.tensor_scalar(half_bias[:, 1, :], cols[:, COLS.index("b_u"), :], 0.5, None, ALU.mult)\
               .then_inc(consts_dve, 1)
            dve.tensor_scalar(w_n[:, 0:NF, :], w_n[:, 0:NF, :], 0.5, None, ALU.mult).then_inc(consts_dve, 1)

            dve.memset(rmax[0:1, 0:1], 0.0).then_inc(S["fin_norm"], 1)
            dve.memset(rmax[0:1, 1:2], 0.0).then_inc(S["y_left"], 1)
            now = Now()

            def new_state(t):
                _, k, _, _ = PLACE[now.phase, ("new", t // 2)]
                return bank[k][:, (t % 2) * D:(t % 2) * D + D]

            def stat(ln, src, ready=None):
                def step(b, _):
                    if ready is not None:
                        dve.wait_ge(S[ready[0]], n(ready[0], b, ready[1]))
                    for t in range(NT):
                        if ln == "fin" and t % 2 == 0:
                            full(dve, now, ("new", t // 2))
                        dve.bn_stats(stats[:, t, :], src(t))
                    dve.drain()
                    for t in range(NT):
                        dve.bn_aggr(mv[:, t, :], stats[:, t, :]).then_inc(S[f"{ln}_var"], 1)
                    dve.wait_ge(S[f"{ln}_var"], n(f"{ln}_var", b, NT))
                    dve.tensor_scalar(ve[:, :], mv[:, :, 1], EPS, None, ALU.add).then_inc(S[f"{ln}_var"], 1)
                return step

            def norm(ln, src, dst):
                def step(b, _):
                    dve.wait_ge(S[f"{ln}_rstd"], n(f"{ln}_rstd", b, 1))
                    for t in range(NT):
                        dve.tensor_scalar(dst[:, t, :], src(t), mv[:, t, 0:1], rstd[:, t:t + 1], ALU.subtract, ALU.mult)\
                           .then_inc(S[f"{ln}_norm"], 1)
                return step

            def low(use, outs):
                def step(b, _):
                    for f in range(NF):
                        dve.wait_ge(S[f"{use}_hi_done"], n(f"{use}_hi_done", b, f + 1))
                        ps = full(dve, now, (use, f))
                        if outs is not None and f == 0:
                            dve.wait_ge(S[outs], n(outs, outs_batch(now, b, use), 16 * NF))
                        dve.tensor_tensor(part_lo[:, f, :], ps[:, :], part_hi[:, f, :].bitcast(f32), ALU.subtract)\
                           .then_inc(S[f"{use}_lo_done"], 1)
                return step

            def keys2_low(b, _):
                ps = full(dve, now, ("k2", 0))
                dve.wait_ge(S["k2_hi_done"], n("k2_hi_done", b, 1))
                dve.tensor_tensor(k2_lo[:, :, :], ps[:, 0:NF * C].rearrange("p (f c) -> p f c", f=NF),
                                  k2_hi[:, :, :].bitcast(f32), ALU.subtract).then_inc(S["k2_lo_done"], 1)

            def tokens(b, _):
                ps = full(dve, now, ("tok", 0))
                dve.tensor_tensor(tok[:, :], ps[:, 0:D], btok_row[:, :], ALU.add).then_inc(S["tok_done"], 1)

            def maximum(b, u):
                qb, h, per = MAX_UNITS[u]
                w = (qb + 1) * P
                ps = full(dve, now, ("max", u))
                dve.tensor_reduce(negm[:, qb, h:h + 2 * per].rearrange("p (m e) -> p e m", e=2),
                                  ps[:, :, 0:per * w].rearrange("p a (h w) -> p a h w", w=w), AX.X, ALU.max,
                                  negate=True).then_inc(S["max_done"], 1)

            def maximum2(b, t):
                ps = full(dve, now, ("max2", t))
                dve.tensor_reduce(negm2[:, t, :].rearrange("p (a h) -> p a h", a=2),
                                  ps[:, :, :].rearrange("p a (h c) -> p a h c", c=C), AX.X, ALU.max,
                                  negate=True).then_inc(S["max2_done"], 1)

            def split_max(src, ready, count, hi_done, lo_done):
                def step(b, _):
                    dve.wait_ge(S[ready], n(ready, b, count))
                    parts = nm2[:, :, :, :].rearrange("p t a (b m) -> p t a b m", b=2)
                    heads = src[:, :, :].rearrange("p t (m e) -> p t e m", e=2)
                    dve.tensor_copy(parts[:, :, :, 0, :], heads).then_inc(S[hi_done], 1)
                    dve.wait_ge(S[hi_done], n(hi_done, b, 1))
                    dve.tensor_tensor(parts[:, :, :, 1, :], heads, parts[:, :, :, 0, :].bitcast(f32), ALU.subtract)\
                       .then_inc(S[lo_done], 1)
                return step

            def normalise(use, rs_done, out_done, done):
                def step(b, g):
                    ps = full(dve, now, (use, g))
                    dve.reciprocal(attT[:, g, :], ps[:, :]).then_inc(S[rs_done], 1)
                    dve.wait_ge(S[rs_done], n(rs_done, b, g + 1))
                    dve.tensor_tensor(attT[:, g, :], pv_sb[:, g % 2, :], attT[:, g, :], ALU.mult)\
                       .then_inc(S[done], 1)
                return step

            def residual(use, src, done, first=None):
                def step(b, i):
                    if i == 0 and first is not None:
                        first(b)
                    ps = full(dve, now, (use, i))
                    dve.tensor_tensor(xs[:, 2 * i:2 * i + 2, :], ps[:, :].rearrange("p (t d) -> p t d", t=2),
                                      src[:, 2 * i:2 * i + 2, :], ALU.add).then_inc(S[done], 1)
                return step

            def first_residual(b):
                dve.wait_ge(S["x_res_in"], n("x_res_in", b, 16))
                dve.wait_ge(S["y_left"], n("y_left", b, 0))

            def hidden_residual(b, t):
                if t == 0:
                    dve.wait_ge(S["x2b_done"], n("x2b_done", b, 1))
                ps = full(dve, now, ("ff2", t))
                dve.tensor_tensor(xs[:, t, :], ps[:, 0:D], xs[:, t, :], ALU.add).then_inc(S["x3_done"], 1)

            def route_max(b, _):
                ps = full(dve, now, ("route", 0))
                dve.tensor_reduce(rmax[:, 0:NT], ps[:, 0:NT * C].rearrange("p (t c) -> p t c", t=NT), AX.X, ALU.max,
                                  negate=True).then_inc(S["rmax_done"], 1)
                dve.wait_ge(S["rmax_done"], n("rmax_done", b, 1))
                dve.tensor_scalar(rmax[:, NT:2 * NT], rmax[:, 0:NT], ROUTE_SCALE, None, ALU.mult)\
                   .then_inc(S["rbias_done"], 1)

            def route_sum(b, _):
                dve.wait_ge(S["rexp_done"], n("rexp_done", b, NT))
                dve.tensor_reduce(rden[:, 0:NT], route[:, :, :], AX.X, ALU.add).then_inc(S["rtotal_done"], 1)
                dve.wait_ge(S["rtotal_done"], n("rtotal_done", b, 1))
                dve.reciprocal(rden[:, NT:2 * NT], rden[:, 0:NT]).then_inc(S["rden_done"], 1)

            def routed_norm(b, _):
                dve.wait_ge(S["rden_done"], n("rden_done", b, 1))
                for i in range(2):
                    ps = full(dve, now, ("routed", i))
                    for t in (i, i + 2):
                        dve.tensor_scalar(routed[:, t, :], ps[:, (t // 2) * D:(t // 2) * D + D],
                                          rden[:, NT + t:NT + t + 1], None, ALU.mult).then_inc(S["routed_done"], 1)

            def reset(b, f):
                dve.wait_ge(S["tr_done"], n("tr_done", b, f + 1))
                dve.scalar_tensor_tensor(out=t_r[:, f, :], in0=t_r[:, f, :], scalar=1.0, in1=psnT[:, f, :],
                                         op0=ALU.add, op1=ALU.mult).then_inc(S["rp_done"], 1)

            def update(b, f):
                dve.wait_ge(S["cand_done"], n("cand_done", b, f + 1))
                dve.tensor_tensor(cand[:, f, :], cand[:, f, :], xT[:, f, :], ALU.subtract)\
                   .then_inc(S["diff_done"], 1)
                dve.wait_ge(S["diff_done"], n("diff_done", b, f + 1))
                dve.scalar_tensor_tensor(out=t_u[:, f, :], in0=t_u[:, f, :], scalar=1.0, in1=cand[:, f, :],
                                         op0=ALU.add, op1=ALU.mult).then_inc(S["step_done"], 1)
                dve.wait_ge(S["step_done"], n("step_done", b, f + 1))
                dve.scalar_tensor_tensor(out=cand[:, f, :], in0=t_u[:, f, :], scalar=0.5, in1=xT[:, f, :],
                                         op0=ALU.mult, op1=ALU.add).then_inc(S["new_done"], 1)

            def of(tile):
                return lambda t: tile[:, t, :]

            run(dve, now, {
                "ln1_stat": stat("ln1", of(x_ln), ("x_in", 16)), "ln1_norm": norm("ln1", of(x_ln), xh_a),
                "ln2_stat": stat("ln2", of(xs), ("x1_done", 2)), "ln2_norm": norm("ln2", of(xs), xh),
                "ln3_stat": stat("ln3", of(xs), ("x2_done", 2)), "ln3_norm": norm("ln3", of(xs), xh),
                "psn_stat": stat("psn", of(xs), ("x3_done", NT)), "psn_norm": norm("psn", of(xs), xh),
                "inn_stat": stat("inn", of(routed), ("routed_done", NT)), "inn_norm": norm("inn", of(routed), xh),
                "fin_stat": stat("fin", new_state), "fin_norm": norm("fin", new_state, xs),
                "q": low("q", None), "k": low("k", "q_lo_out"), "q2": low("q2", "k_lo_out"),
                "k2": keys2_low, "tok": tokens, "max": maximum, "max2": maximum2,
                "negm": split_max(negm, "max_done", len(MAX_UNITS), "nm_hi_done", "nm_lo_done"),
                "negm2": split_max(negm2, "max2_done", NT, "nm2_hi_done", "nm2_lo_done"),
                "norm": normalise("sum", "rsum_done", "pv_out", "att_done"),
                "norm2": normalise("sum2", "rsum2_done", "pv2_out", "att2_done"),
                "proj": residual("proj", x_res, "x1_done", first_residual),
                "proj2": residual("proj2", xs, "x2_done"), "ff2": hidden_residual,
                "route": route_max, "routeT": route_sum, "routed": routed_norm, "r": reset, "n": update,
            })

        @block.tensor
        def _(pe):
            pe.wait_ge(w_in, N_LOAD)
            pe.wait_ge(consts, N_CONST)
            pe.wait_ge(consts_dve, N_CONST_DVE)
            pe.wait_ge(pads_in, N_PAD)
            now = Now()

            def turn(use, src, ready):
                def step(b, _):
                    for f in range(NF):
                        ps = free(pe, now, b, (use, f))
                        for t in range(NT):
                            if f == 0:
                                pe.wait_ge(S[ready], n(ready, b, t + 1))
                            last = pe.transpose(ps[:, t * P:t * P + P], src[:, t, f * P:f * P + P], ident[:, :])
                        last.then_inc(filled(now, (use, f)), 1)
                return step

            def project_T(use, w, at, rhs, ready):
                def step(b, _):
                    for f in range(NF):
                        ps = free(pe, now, b, (use, f))
                        for kt in range(NF):
                            pe.wait_ge(S[ready], n(ready, b, kt + 1))
                            last = pe.matmul(ps[:, :], w[:, kt, at + f * P:at + f * P + P], rhs[:, kt, :],
                                             start=(kt == 0), stop=(kt == NF - 1))
                        last.then_inc(filled(now, (use, f)), 1)
                return step

            def values(b, _):
                for i in range(2):
                    ps = free(pe, now, b, ("v", i))
                    for t in (2 * i, 2 * i + 1):
                        for kt in range(NF):
                            last = pe.matmul(ps[:, (t % 2) * D:(t % 2) * D + D], hT_a[:, kt, t * P:t * P + P],
                                             wqkv[:, kt, 2 * D:3 * D], start=(kt == 0), stop=(kt == NF - 1))
                    last.then_inc(filled(now, ("v", i)), 1)

            def ctx_turn(b, _):
                ps = free(pe, now, b, ("ctxT", 0))
                pe.wait_ge(S["ctx_in"], n("ctx_in", b, 32))
                for c in range(NC):
                    last = pe.transpose(ps[0:CK[c], c * P:c * P + P], ctx_sb[:, c * P:c * P + CK[c]], ident[:, :])
                last.then_inc(filled(now, ("ctxT", 0)), 1)

            def ctx_features(use, w):
                def step(b, _):
                    ps = free(pe, now, b, (use, 0))
                    pe.wait_ge(S["ctxT_done"], n("ctxT_done", b, 1))
                    for f in range(NF):
                        for c in range(NC):
                            last = pe.matmul(ps[:, f * C:f * C + C], w[0:CK[c], c, f * P:f * P + P],
                                             ctxT[0:CK[c], c, 0:C], start=(c == 0), stop=(c == NC - 1))
                    last.then_inc(filled(now, (use, 0)), 1)
                return step

            def ctx_rows(use, w, at):
                def step(b, _):
                    ps = free(pe, now, b, (use, 0))
                    for c in range(NC):
                        last = pe.matmul(ps[:, 0:D], ctxT[0:CK[c], c, :], w[0:CK[c], c, at:at + D],
                                         start=(c == 0), stop=(c == NC - 1))
                    last.then_inc(filled(now, (use, 0)), 1)
                return step

            def scores(b, u):
                if u == 0:
                    pe.wait_ge(S["q_stacked"], n("q_stacked", b, PER["q_stacked"]))
                    pe.wait_ge(S["k_stacked"], n("k_stacked", b, PER["k_stacked"]))
                qb, h0, per = MAX_UNITS[u]
                w = (qb + 1) * P
                ps = free(pe, now, b, ("max", u))
                for i in range(2 * per):
                    e, m, at = i % 2, (h0 + i) // 2, (i // 2) * w
                    pe.matmul(ps[:, e, at:at + w], q_st[64 * e:64 * e + SA_K, m, qb * P:qb * P + P],
                              k_st[64 * e:64 * e + SA_K, m, 0:w], start=True, stop=False)
                    last = pe.matmul(ps[:, e, at + qb * P:at + w], ident_bf[:, :], mask_bf[:, :],
                                     start=False, stop=True)
                last.then_inc(filled(now, ("max", u)), 1)

            def scores2(b, t):
                if t == 0:
                    pe.wait_ge(S["q2_stacked"], n("q2_stacked", b, PER["q2_stacked"]))
                    pe.wait_ge(S["k2_stacked"], n("k2_stacked", b, PER["k2_stacked"]))
                ps = free(pe, now, b, ("max2", t))
                for m in range(NP):
                    at = (m % 4) * 2 * C
                    last = pe.matmul(ps[:, m // 4, at:at + 2 * C], q2_st[0:CA_K, m, t * P:t * P + P],
                                     k2_st[0:CA_K, m, :], start=True, stop=True)
                last.then_inc(filled(now, ("max2", t)), 1)

            def turn_max(use, ready):
                def step(b, _):
                    ps = free(pe, now, b, (use, 0))
                    pe.wait_ge(S[ready], n(ready, b, 1))
                    for t in range(NT):
                        last = pe.transpose(ps[0:2 * H, t * P:t * P + P],
                                            nm2[:, t, :, :].bitcast(f32).rearrange("p a h -> p (a h)"), ident[:, :])
                    last.then_inc(filled(now, (use, 0)), 1)
                return step

            def scores_T(b, st):
                g, kb = st // NT, st % NT
                if st == 0:
                    pe.wait_ge(S["max_stacked"], n("max_stacked", b, 64))
                for pr in range(2):
                    u = 2 * st + pr
                    ps = free(pe, now, b, ("st", u))
                    m = (HG * g + 2 * pr) // 2
                    for i in range(2):
                        pe.matmul(ps[:, i, 0:T - kb * P], k_st[64 * i:64 * i + SA_KM, m, kb * P:kb * P + P],
                                  q_st[64 * i:64 * i + SA_KM, m, kb * P:T], start=True, stop=False)
                    for i in range(2):
                        last = pe.matmul(ps[:, i, 0:P], ident_bf[:, :], maskT_bf[:, :], start=False, stop=True)
                    last.then_inc(filled(now, ("st", u)), 1)

            def weigh(b, st):
                g, kb = st // NT, st % NT
                if st == 0:
                    pe.wait_ge(S["v_done"], n("v_done", b, 2))
                ps = free(pe, now, b, ("pv", g)) if kb == 0 else acc[0]
                pe.wait_ge(S["exp_done"], n("exp_done", b, 2 * st + 2))
                for j in range(HG):
                    last = pe.matmul(ps[j * QW:j * QW + QW, kb * P:T], v_sa[:, kb, HG * g + j, :],
                                     probs[:, st % 2, j, kb * P:T], start=(kb == 0), stop=(kb == NT - 1))
                last.then_inc(S["pv_used"], 1)

            def scores2_T(b, u):
                if u == 0:
                    pe.wait_ge(S["max2_stacked"], n("max2_stacked", b, 64))
                ps = free(pe, now, b, ("st2", u))
                for i in range(2):
                    last = pe.matmul(ps[:, i, :], k2_st[0:CA_KM, 2 * u + i, :], q2_st[0:CA_KM, 2 * u + i, :],
                                     start=True, stop=True)
                last.then_inc(filled(now, ("st2", u)), 1)

            def weigh2(b, g):
                if g == 0:
                    pe.wait_ge(S["v2_done"], n("v2_done", b, 2))
                ps = free(pe, now, b, ("pv2", g))
                pe.wait_ge(S["exp2_done"], n("exp2_done", b, g + 1))
                for i in range(2):
                    last = pe.matmul(ps[i * 2 * QW:i * 2 * QW + 2 * QW, :], v_ca[:, 2 * g + i, :],
                                     probs[:, g // 2, 2 * (g % 2) + i, :], start=True, stop=True)
                last.then_inc(filled(now, ("pv2", g)), 1)

            def spread(use, out_done):
                def step(b, g):
                    ps = free(pe, now, b, (use, g))
                    pe.wait_ge(S[out_done], n(out_done, b, g + 1))
                    pe.matmul(ps[:, :], sel[:, :], pv_sb[:, g % 2, :], start=True, stop=True)\
                      .then_inc(filled(now, (use, g)), 1)
                return step

            def project_out(use, w, done):
                def step(b, i):
                    ps = free(pe, now, b, (use, i))
                    for t in (2 * i, 2 * i + 1):
                        for g in range(NG):
                            if t == 0:
                                pe.wait_ge(S[done], n(done, b, g + 1))
                            last = pe.matmul(ps[:, (t % 2) * D:(t % 2) * D + D], attT[:, g, t * P:t * P + P],
                                             w[:, g, :], start=(g == 0), stop=(g == NG - 1))
                    last.then_inc(filled(now, (use, i)), 1)
                return step

            def hidden(b, f):
                ps = free(pe, now, b, ("ff1", f))
                for kt in range(NF):
                    if f == 0:
                        pe.wait_ge(S["h3"], n("h3", b, kt + 1))
                    last = pe.matmul(ps[:, :], wff1[:, kt, f * P:f * P + P], hT[:, kt, :],
                                     start=(kt == 0), stop=(kt == NF - 1))
                last.then_inc(filled(now, ("ff1", f)), 1)

            def hidden_out(b, t):
                ps = free(pe, now, b, ("ff2", t))
                for f in range(NFF):
                    if t == 0:
                        pe.wait_ge(S["gelu_done"], n("gelu_done", b, f + 1))
                    last = pe.matmul(ps[:, 0:D], gT[:, f, t * P:t * P + P], wff2[:, f, :],
                                     start=(f == 0), stop=(f == NFF - 1))
                last.then_inc(filled(now, ("ff2", t)), 1)

            def route_scores(b, _):
                ps = free(pe, now, b, ("route", 0))
                pe.wait_ge(S["xT_done"], n("xT_done", b, NF))
                pe.wait_ge(S["tokT_done"], n("tokT_done", b, NF))
                for t in range(NT):
                    for kt in range(NF):
                        last = pe.matmul(ps[:, t * C:t * C + C], xT[:, kt, t * P:t * P + P], tokT[:, kt, :],
                                         start=(kt == 0), stop=(kt == NF - 1))
                last.then_inc(filled(now, ("route", 0)), 1)

            def route_turn(b, _):
                ps = free(pe, now, b, ("routeT", 0))
                pe.wait_ge(S["rexp_done"], n("rexp_done", b, NT))
                for i in range(2):
                    last = pe.transpose(ps[:, i * P:i * P + P],
                                        route[:, 2 * i:2 * i + 2, :].rearrange("p t c -> p (t c)"), ident[:, :])
                last.then_inc(filled(now, ("routeT", 0)), 1)

            def route_tokens(b, _):
                pe.wait_ge(S["routeT_done"], n("routeT_done", b, 1))
                pe.wait_ge(S["tok_done"], n("tok_done", b, 1))
                for i in range(2):
                    ps = free(pe, now, b, ("routed", i))
                    rows = slice(i * C, i * C + C)
                    for t in (i, i + 2):
                        last = pe.matmul(ps[:, (t // 2) * D:(t // 2) * D + D], routeT[rows, t // 2, :], tok[rows, :],
                                         start=True, stop=True)
                    last.then_inc(filled(now, ("routed", i)), 1)

            def gate(use, w, first, first_ready):
                def step(b, f):
                    ps = free(pe, now, b, (use, f))
                    for kt in (2, 3, 0, 1):
                        rhs, ready, c = ((first, first_ready, kt + 1) if kt < NF else (hT, "inn_done", kt - NF + 1))
                        if f == 0:
                            pe.wait_ge(S[ready], n(ready, b, c))
                        last = pe.matmul(ps[:, :], w[:, kt, f * P:f * P + P], rhs[:, kt % NF, :],
                                         start=(kt == 2), stop=(kt == 1))
                    last.then_inc(filled(now, (use, f)), 1)
                return step

            def new_turn(b, _):
                for i in range(2):
                    ps = free(pe, now, b, ("new", i))
                    if i == 0:
                        pe.wait_ge(S["new_done"], n("new_done", b, NF))
                    for t in (2 * i, 2 * i + 1):
                        for f in range(NF):
                            at = (t % 2) * D + f * P
                            last = pe.transpose(ps[:, at:at + P], cand[:, f, t * P:t * P + P], ident[:, :])
                    last.then_inc(filled(now, ("new", i)), 1)

            run(pe, now, {
                "ln1T": turn("ln1T", xh_a, "ln1_norm"), "ln2T": turn("ln2T", xh, "ln2_norm"),
                "ln3T": turn("ln3T", xh, "ln3_norm"), "psnT": turn("psnT", xh, "psn_norm"),
                "innT": turn("innT", xh, "inn_norm"), "xT": turn("xT", xs, "x3_done"),
                "q": project_T("q", wqkv, 0, hT_a, "h1"), "k": project_T("k", wqkv, D, hT_a, "h1"),
                "q2": project_T("q2", wq_ca, 0, hT, "h2"), "v": values, "ctxT": ctx_turn,
                "k2": ctx_features("k2", wkv_ca), "tokT": ctx_features("tokT", wtok),
                "v2": ctx_rows("v2", wkv_ca, D), "tok": ctx_rows("tok", wtok, 0),
                "max": scores, "max2": scores2, "negm": turn_max("negmT", "nm_lo_done"),
                "negm2": turn_max("negm2T", "nm2_lo_done"), "st": scores_T, "pv": weigh, "st2": scores2_T,
                "pv2": weigh2, "norm": spread("sum", "pv_out"), "norm2": spread("sum2", "pv2_out"),
                "proj": project_out("proj", wproj_sa, "att_done"),
                "proj2": project_out("proj2", wproj_ca, "att2_done"),
                "ff1": hidden, "ff2": hidden_out, "route": route_scores, "routeT": route_turn,
                "routed": route_tokens, "r": gate("r", w_r, psnT, "psn_done"), "u": gate("u", w_u, psnT, "psn_done"),
                "n": gate("n", w_n, t_r, "rp_done"), "new": new_turn,
            })


_OUTS = [((16, 512, 256), 'float32')]


def kernel(**inputs):
    import numpy as _np
    import concourse.bacc as _bacc
    from concourse import mybir as _mybir
    from concourse.bass_utils import run_bass_kernel_spmd as _run

    names = ["x", "ctx_768"] + [f"L0_xattn_{w}" for w in (
        "Wqkv", "Wproj_sa", "bproj_sa", "g1", "b1", "Wq_ca", "Wkv_ca", "Wproj_ca", "bproj_ca", "g2", "b2", "Wff1",
        "bff1", "Wff2", "bff2", "g3", "b3")] + [f"L1_xattn_{w}" for w in (
            "W_proj", "b_proj", "g_state", "beta_state", "g_input", "beta_input", "g_out", "beta_out", "W_u", "b_u",
            "W_r", "b_r", "W_n", "b_n")]
    nc = _bacc.Bacc("TRN2", target_bir_lowering=False, num_devices=1)
    arrays, args = {}, []
    for name in names:
        a = _np.ascontiguousarray(inputs[name])
        arrays[f"in_{name}_dram"] = a
        args.append(nc.dram_tensor(f"in_{name}_dram", a.shape, _mybir.dt.from_np(a.dtype), kind="ExternalInput").ap())
    for i, (shape, dtype) in enumerate(_OUTS):
        dt = _mybir.dt.from_np(_np.dtype(dtype))
        args.append(nc.dram_tensor(f"out_{i}_dram", shape, dt, kind="ExternalOutput").ap())
    build(nc, *args)
    r = _run(nc, [arrays], core_ids=[0])
    return r.results[0]["out_0_dram"]
```

```python
import concourse.bass as bass
from concourse import mybir
from contextlib import ExitStack


def build(nc, x, ctx_768, l0_wqkv, l0_wproj_sa, l0_bproj_sa, l0_g1, l0_b1, l0_wq_ca, l0_wkv_ca, l0_wproj_ca,
          l0_bproj_ca, l0_g2, l0_b2, l0_wff1, l0_bff1, l0_wff2, l0_bff2, l0_g3, l0_b3, l1_w_proj, l1_b_proj,
          l1_g_state, l1_beta_state, l1_g_input, l1_beta_input, l1_g_out, l1_beta_out, l1_w_u, l1_b_u, l1_w_r,
          l1_b_r, l1_w_n, l1_b_n, out):
    f32 = mybir.dt.float32
    f32r = mybir.dt.float32r
    bf16 = mybir.dt.bfloat16
    ALU = mybir.AluOpType
    ACT = mybir.ActivationFunctionType
    AX = mybir.AxisListType

    B, T, D = x.shape
    C, DC = ctx_768.shape[1:]
    DFF = l0_wff1.shape[1]
    P = 128
    H = 16
    DH = D // H
    NT = T // P
    NF = D // P
    NFF = DFF // P
    NC = 2
    CK = [P, DC - P]
    HG = 4
    NG = H // HG
    NP = H // 2
    QW = 32
    EPS = 1e-5
    ATT_SCALE = float(DH) ** -0.5
    ROUTE_SCALE = float(D) ** -0.5
    MASKED = -1e30
    SA_K = 3 * DH
    SA_KM = SA_K + 2
    CA_K = 6 * DH
    CA_KM = CA_K + 4

    es = ExitStack()
    with es:
        def sb(name, shape, dt=f32):
            return es.enter_context(nc.sbuf_tensor(name, shape, dt))

        def sb_over(name, shape, dt, name2, shape2, dt2):
            with nc.sbuf_tensor(name, shape, dt) as first:
                pass
            return first, sb(name2, shape2, dt2)

        wqkv = sb("wqkv", [P, NF, 3 * D])
        wproj_sa = sb("wproj_sa", [P, NG // 2, D])
        wproj_ca = sb("wproj_ca", [P, NG // 2, D])
        wq_ca = sb("wq_ca", [P, NF, D])
        wkv_ca = sb("wkv_ca", [P, NC, 2 * D])
        wff1_hi = sb("wff1_hi", [P, NF, DFF], f32r)
        wff1_lo = sb("wff1_lo", [P, NF, DFF], f32r)
        wff2_hi = sb("wff2_hi", [P, NFF, D], f32r)
        wff2_lo = sb("wff2_lo", [P, NFF, D], f32r)
        wtok = sb("wtok", [P, NC, D])
        w_u = sb("w_u", [P, 2 * NF, D])
        w_r = sb("w_r", [P, 2 * NF, D])
        w_n = sb("w_n", [P, 2 * NF, D])
        COLS = ["g1", "b1", "g2", "b2", "g3", "b3", "g_state", "beta_state", "g_input", "beta_input",
                "btok", "b_u", "b_r", "b_n"]
        cols_dram = [l0_g1, l0_b1, l0_g2, l0_b2, l0_g3, l0_b3, l1_g_state, l1_beta_state, l1_g_input,
                     l1_beta_input, l1_b_proj, l1_b_u, l1_b_r, l1_b_n]
        cols = sb("cols", [P, len(COLS), NF])
        bff1 = sb("bff1", [P, NFF])
        half_bias = sb("half_bias", [P, 2, NF])
        bproj_sa_row = sb("bproj_sa_row", [P, D])
        bproj_ca_row = sb("bproj_ca_row", [P, D])
        bff2_row = sb("bff2_row", [P, D])
        btok_row = sb("btok_row", [P, D])
        gout_row = sb("gout_row", [P, D])
        bout_row = sb("bout_row", [P, D])

        def col(name, f):
            return cols[:, COLS.index(name), f:f + 1]

        ident = sb("ident", [P, P])
        ident_bf = sb("ident_bf", [P, P], bf16)
        mask_bf = sb("mask_bf", [P, P], bf16)
        maskT_bf = sb("maskT_bf", [P, P], bf16)
        neg_half = sb("neg_half", [P, NT])
        mark = sb("mark", [P, 1])

        xs = sb("xs", [P, NT, D])
        NORMS = ("ln1", "ln2", "ln3", "psn", "inn", "fin")
        stats_of = sb("stats", [P, len(NORMS), NT, 6])
        mv_of = sb("mv", [P, len(NORMS), NT, 2])
        ve_of = sb("ve", [P, len(NORMS), NT])
        rstd_of = sb("rstd", [P, len(NORMS), NT])
        xh = sb("xh", [P, NT, D])
        x_ln = xh
        hT_a = sb("hT_a", [P, NF, T])
        hidden_sb = hT_a
        psnT = hT_a
        hT = sb("hT", [P, NF, T])
        h3_parts, weighed_sb = sb_over("h3_parts", [P, 2, NF, T], f32r, "weighed_sb", [P, 2, 2, T], f32)
        h3_hi, h3_lo = h3_parts[:, 0], h3_parts[:, 1]
        parts = sb("parts", [P, 2, NF, T], f32r)
        part_hi, part_lo = parts[:, 0, :, :], parts[:, 1, :, :]
        att2T = part_hi.bitcast(f32)
        q_st = sb("q_st", [P, NP, T], f32r)
        k_st = sb("k_st", [P, NP, T], f32r)
        q2_st = sb("q2_st", [P, NP, T], f32r)
        gT_lo = q2_st
        v_sa = sb("v_sa", [P, NT, H, QW])
        negm = sb("negm", [P, NT, H])
        negm2 = sb("negm2", [P, NT, H])
        nm2 = sb("nm2", [P, NT, 2, H], f32r)
        nmT = sb("nmT", [2 * H, T], f32r)
        gT_hi, probs = sb_over("gT_hi", [P, NFF, T], f32r, "probs", [P, 2, HG, T], f32)
        ff_f32 = probs[:, :, :, :].rearrange("p w f t -> p w (f t)")
        turned, packed = weighed_sb[:, 0], weighed_sb[:, 1]
        inv = sb("inv", [P, T // QW])
        attT = sb("attT", [P, NG // 2, T])
        ctx_sb = sb("ctx_sb", [P, DC])
        ctxT = sb("ctxT", [P, NC, P])
        k2_hi = sb("k2_hi", [P, NF, C], f32r)
        k2_lo = sb("k2_lo", [P, NF, C], f32r)
        k2_st = sb("k2_st", [P, NP, 2 * C], f32r)
        v_ca = sb("v_ca", [P, NP, 2 * QW])
        tokT = sb("tokT", [P, NF, C])
        tok = sb("tok", [P, D])
        rmax = sb("rmax", [P, 2 * NT])
        rden = sb("rden", [P, 2 * NT])
        route = turned[:, 0, 0:NT * C].rearrange("p (t c) -> p t c", c=C)
        routeT = turned[:, 0, NT * C:NT * C + 2 * P].rearrange("p (i c) -> p i c", c=P)
        gates = sb("gates", [P, 4, NF, T])
        xT, t_r, t_u, cand = (gates[:, k, :, :] for k in range(4))
        probs2 = gates[:, :, :, :].rearrange("p k f t -> p (k f) t")
        routed = cand.rearrange("p a (b d) -> p (a b) d", d=D)
        y_sb = t_r.rearrange("p a (b d) -> p (a b) d", d=D)
        d_q = nc.dram_tensor("d_q", [2, 2 * DH, NP, T], f32, kind="Internal").ap()
        d_k = nc.dram_tensor("d_k", [2, 2 * DH, NP, T], f32, kind="Internal").ap()
        d_q2 = nc.dram_tensor("d_q2", [2, 2 * DH, NP, T], f32, kind="Internal").ap()
        d_k2 = nc.dram_tensor("d_k2", [2, D, C], f32, kind="Internal").ap()

        bank = [es.enter_context(nc.psum_tensor(f"bank{k}", [P, 512], f32)) for k in range(3)]
        acc = [es.enter_context(nc.psum_tensor("acc0", [P, 512], f32))]
        wide = [es.enter_context(nc.psum_tensor(f"wide{k}", [P, 2, 512], f32)) for k in range(2)]

        MAX_UNITS = []
        for qb in range(NT):
            per = T // ((qb + 1) * P)
            MAX_UNITS += [(qb, h, per) for h in range(0, H, 2 * per)]
        ST_UNITS = [(g, kb, pr) for g in range(NG) for kb in range(NT) for pr in range(2)]

        def steps_of(text):
            words = [w.split(".") for w in text.split()]
            return [(w[0][0], w[0][1:], int(w[1]) if len(w) > 1 else 0) for w in words]

        NS = NG * NT
        NMAX = len(MAX_UNITS)

        def attend(lo, hi):
            steps = []
            for st in range(lo, hi):
                steps += [("A", "st", st)] if st < NS else []
                steps += [("A", "pv", st - 1)] if st else []
                if st and st % NT == 0:
                    steps += [("A", "norm", st // NT - 1)]
            return steps

        def maxes(lo, hi):
            return [("P", "max", u) for u in range(lo, hi)]

        ORDER = (
            steps_of("Bproj.0 Bproj.1 Bln2_stat") + attend(0, 1) + steps_of("Fnew Ffin_stat") + attend(1, 2)
            + steps_of("Bln2_norm Ffin_norm") + attend(2, 3) + steps_of("BctxT") + attend(3, 4)
            + steps_of("Bln2T Pload_p Bk2 Bk2_stack Bq2 Bstack2 Bv2 Aload_ctx") + attend(4, 6)
            + steps_of("Pln1_stat") + attend(6, 7) + steps_of("Pln1_norm") + attend(7, 9) + steps_of("Pln1T")
            + attend(9, 10) + steps_of("Pq Pk") + attend(10, 11)
            + steps_of("Bmax2.0 Bmax2.1 Bmax2.2 Bmax2.3") + attend(11, 12) + steps_of("Bnegm2") + attend(12, 14)
            + steps_of("Bst2.0 Bst2.1 Bpv2.0 Bst2.2 Bpv2.1 Bnorm2.0") + attend(14, 15)
            + steps_of("Bst2.3 Bpv2.2 Bnorm2.1 Bpv2.3 Bnorm2.2") + attend(15, 16)
            + steps_of("Bnorm2.3") + attend(16, 17) + steps_of("Pstack Pload_rest BtokT Bproj2.0 Bproj2.1 Bln3_stat "
                       "Bln3_norm Pv.0 Btok Bln3T Pv.1 Bff1.0"))
        at = 0
        for f in range(1, NFF):
            hi = at + (f >= 5)
            ORDER += steps_of(f"Bff1.{f}") + maxes(at, hi)
            at = hi
        for t in range(NT):
            ORDER += steps_of(f"Bff2.{t}") + maxes(at, at + 1)
            at += 1
        for text, more in (("Bpsn_stat BxT", 2), ("Broute", 2), ("Bpsn_norm", 1), ("BpsnT", 1), ("BrouteT", 1),
                           ("Brouted Bra.0 Binn_stat", 1), ("Bra.1 Binn_norm", 1), ("BinnT Aload_x", 1), ("Brb.0", 1),
                           ("Brb.1", 1), ("Bu.0", 1), ("Bu.1", 1)):
            hi = min(at + more, NMAX)
            ORDER += steps_of(text) + maxes(at, hi)
            at = hi
        ORDER += maxes(at, NMAX) + steps_of("Psplit_max Bn.0 Pnegm Bn.1 Abias_a Pprepare")

        AHEAD = {"P": 3, "A": 2, "B": 1, "F": 0}
        PHASES = {"fill0": (-3, "P"), "fill1": (-2, "AP"), "fill2": (-1, "BAP"), "loop": (0, "FBAP"),
                  "drain0": (B - 3, "FBA"), "drain1": (B - 2, "FB"), "drain2": (B - 1, "F")}
        PHASES = {name: (j, [x for x in ORDER if x[0] in stages]) for name, (j, stages) in PHASES.items()}
        BEFORE = {"fill0": [], "fill1": ["fill0"], "fill2": ["fill1"], "loop": ["fill2", "loop"],
                  "drain0": ["loop"], "drain1": ["drain0"], "drain2": ["drain1"]}

        PER, S = {}, {}

        def sem(name, per):
            PER[name] = per
            S[name] = es.enter_context(nc.semaphore(name))

        def n(name, b, c):
            j, off = b
            assert off * PER[name] + c > 0, "a wait for nothing"
            return j * PER[name] + (off * PER[name] + c)

        for ln in NORMS:
            sem(f"{ln}_var", NT + 1)
            sem(f"{ln}_rstd", 1)
            sem(f"{ln}_norm", NT)
        for name, per in [
            ("x_in", 16), ("x_res_in", 16), ("ctx_in", 32),
            ("h1", NF), ("h2", NF), ("h3", NF), ("psn_done", NF), ("inn_done", NF), ("xT_done", NF),
            ("q_hi_done", NF), ("k_hi_done", NF), ("q_lo_done", NF), ("k_lo_done", NF),
            ("q_hi_out", 16 * NF), ("q_lo_out", 16 * NF), ("k_hi_out", 16 * NF), ("k_lo_out", 16 * NF),
            ("q2_hi_out", 16 * NF), ("q2_lo_out", 16 * NF), ("k2_hi_out", 16), ("k2_lo_out", 16),
            ("q_stacked", 16 * 4), ("k_stacked", 16 * 4), ("q2_stacked", 16 * 4), ("k2_stacked", 16 * 12),
            ("v_done", 2), ("ctxT_done", 1), ("k2_hi_done", 1), ("k2_lo_done", 1), ("v2_done", 2),
            ("tokT_done", NF), ("tok_done", 1),
            ("max_done", len(MAX_UNITS)), ("nm_hi_done", 1), ("nm_lo_done", 1), ("nmT_done", 1),
            ("max_stacked", 64),
            ("exp_done", len(ST_UNITS)), ("pv_used", NG * NT),
            ("pv_turned", NG), ("sum_inv", NG), ("pv_divided", NG), ("att_done", NG // 2), ("x1_done", 2),
            ("q2_hi_done", NF), ("q2_lo_done", NF),
            ("max2_done", NT), ("nm2_hi_done", 1), ("nm2_lo_done", 1), ("nmT2_done", 1), ("max2_stacked", 64),
            ("exp2_done", NP // 2), ("pv2_turned", NG), ("sum2_inv", NG), ("pv2_divided", NG), 
            ("att2_done", NG // 2), ("x2_done", 2),
            ("x_biased", 1), ("x1b_done", 1), ("x2b_done", 1), ("h3_hi_done", NF), ("h3_lo_done", NF),
            ("gelu_done", NFF), ("gelu_hi", NFF), ("gelu_lo", NFF), ("x3_done", NT),
            ("rmax_done", 1), ("rbias_done", 1), ("rexp_done", NT), ("rtotal_done", 1), ("rden_done", 1),
            ("routeT_done", 1), ("routed_done", NT), ("tr_done", NF), ("tu_done", NF), ("rp_done", NF),
            ("cand_done", NF), ("diff_done", NF), ("step_done", NF), ("new_done", NF), ("gained", 1),
            ("y_done", 1),
        ]:
            sem(name, per)
        sem("y_stored", 16)
        sem("y_left", 1)

        BANK_OF = {
            "ln1T": [(("ln1T", f), ("h1", f + 1)) for f in range(NF)],
            "q": [(("q", f), ("q_lo_done", f + 1)) for f in range(NF)],
            "k": [(("k", f), ("k_lo_done", f + 1)) for f in range(NF)],
            "negm": [(("negmT", 0), ("nmT_done", 1))],
            "ctxT": [(("ctxT", 0), ("ctxT_done", 1))],
            "k2": [(("k2", 0), ("k2_lo_done", 1))],
            "v2": [(("v2", 0), ("v2_done", 2))],
            "tokT": [(("tokT", 0), ("tokT_done", NF))],
            "tok": [(("tok", 0), ("tok_done", 1))],
            "ln2T": [(("ln2T", f), ("h2", f + 1)) for f in range(NF)],
            "q2": [(("q2", f), ("q2_lo_done", f + 1)) for f in range(NF)],
            "negm2": [(("negm2T", 0), ("nmT2_done", 1))],
            "ln3T": [(("ln3T", f), ("h3_hi_done", f + 1)) for f in range(NF)],
            "xT": [(("xT", f), ("xT_done", f + 1)) for f in range(NF)],
            "route": [(("route", 0), ("rexp_done", NT))],
            "psnT": [(("psnT", f), ("psn_done", f + 1)) for f in range(NF)],
            "routeT": [(("routeT", 0), ("routeT_done", 1))],
            "routed": [(("routed", i), ("routed_done", 2 * i + 2)) for i in range(2)],
            "innT": [(("innT", f), ("inn_done", f + 1)) for f in range(NF)],
            "new": [(("new", i), ("fin_norm", 2 * i + 2)) for i in range(2)],
        }
        for g in range(NG):
            BANK_OF["pv2", g] = [(("pv2", g), ("pv2_turned", g + 1))]
        for i in range(2):
            BANK_OF["proj", i] = [(("proj", i), ("x1_done", i + 1))]
            BANK_OF["proj2", i] = [(("proj2", i), ("x2_done", i + 1))]
            BANK_OF["u", i] = [(("u", i), ("tu_done", i + 1))]
            BANK_OF["n", i] = [(("n", i), ("cand_done", i + 1))]
            BANK_OF["v", i] = [(("v", i), ("v_done", i + 1))]
        for f in range(NFF):
            BANK_OF["ff1", f] = [(("ff1", f), ("gelu_hi", f + 1))]
        for t in range(NT):
            BANK_OF["ff2", t] = [(("ff2", t), ("x3_done", t + 1))]
        BANK_OF["ra", 1] = [(("r", 1), ("tr_done", 2))]
        ACC_OF = {("pv", NT * g): [(("pv", g), ("pv_turned", g + 1))] for g in range(NG)}
        ACC_OF["ra", 0] = [(("r", 0), ("tr_done", 1))]
        WIDE_OF = {("max", u): [(("max", u), ("max_done", u + 1))] for u in range(len(MAX_UNITS))}
        WIDE_OF.update({("st", st): [(("st", u), ("exp_done", u + 1)) for u in (2 * st, 2 * st + 1)]
                        for st in range(NS)})
        WIDE_OF.update({("max2", t): [(("max2", t), ("max2_done", t + 1))] for t in range(NT)})
        WIDE_OF.update({("st2", u): [(("st2", u), ("exp2_done", u + 1))] for u in range(NP // 2)})
        BY_STEPS = {("pv", g): ("pv_used", NT * (g + 1)) for g in range(NG)}

        PLACE = {}
        LAST = {}
        FILLS = {}
        for ring, tiles, of in (("bank", bank, BANK_OF), ("acc", acc, ACC_OF), ("wide", wide, WIDE_OF)):
            for phase, (_, steps) in PHASES.items():
                k = 0
                for stage, name, i in steps:
                    for use, reader in of.get((name, i), of.get(name, []) if i == 0 else []):
                        before = LAST.get((phase, ring, k))
                        fills = FILLS.get((phase, ring, k), 0) + (use not in BY_STEPS)
                        PLACE[phase, use] = (ring, k, before, fills)
                        FILLS[phase, ring, k] = fills
                        LAST[phase, ring, k] = (stage, *reader)
                        k = (k + 1) % len(tiles)
            for k in range(len(tiles)):
                sem(f"{ring}_full{k}", FILLS["loop", ring, k])
        TILES = {"bank": bank, "acc": acc, "wide": wide}

        class Now:

            def __init__(self):
                self.phase, self.j = "fill0", 0

            def batch(self, stage):
                return self.j, min(PHASES[self.phase][0] + AHEAD[stage], B)

        def free(pe, now, b, use):
            ring, k, before, _ = PLACE[now.phase, use]
            if before is not None:
                stage, name, c = before
                pe.wait_ge(S[name], n(name, now.batch(stage), c))
            else:
                names = []
                for phase in BEFORE[now.phase]:
                    while (phase, ring, k) not in LAST and BEFORE[phase]:
                        phase = BEFORE[phase][0]
                    stage, name, _ = LAST.get((phase, ring, k), (None, None, 0))
                    if name is not None and name not in names:
                        names.append(name)
                        if now.phase != "loop" and now.batch(stage)[1] <= 0:
                            continue
                        pe.wait_ge(S[name], n(name, now.batch(stage), 0))
            return TILES[ring][k]

        def filled(now, use):
            ring, k, _, _ = PLACE[now.phase, use]
            return S[BY_STEPS[use][0]] if use in BY_STEPS else S[f"{ring}_full{k}"]

        def full(eng, now, use):
            ring, k, _, fills = PLACE[now.phase, use]
            if use in BY_STEPS:
                name, c = BY_STEPS[use]
                eng.wait_ge(S[name], n(name, now.batch("A"), c))
            else:
                j = PHASES[now.phase][0]
                ahead = sum(FILLS.get((phase, ring, k), 0) for phase, (at, _) in PHASES.items()
                            if at < j and phase != "loop")
                name = f"{ring}_full{k}"
                eng.wait_ge(S[name], n(name, (now.j, max(0, min(j, B - 3))), ahead + fills))
            return TILES[ring][k]

        def outs_batch(now, b, use):
            if use == "q2":
                return now.batch("P"), 0
            if use == "q":
                return (now.batch("B"), 1) if now.phase not in ("fill0", "fill1") else (None, 0)
            return b, 1

        def run(eng, now, steps):
            for phase, (_, order) in PHASES.items():
                now.phase = phase
                if phase == "loop":
                    with eng.Fori(0, B - 3) as j:
                        now.j = j
                        for stage, name, i in order:
                            if name in steps:
                                steps[name](now.batch(stage), i)
                    now.j = 0
                else:
                    for stage, name, i in order:
                        if name in steps:
                            steps[name](now.batch(stage), i)

        first_in = es.enter_context(nc.semaphore("first_in"))
        w_in = es.enter_context(nc.semaphore("w_in"))
        prepared = es.enter_context(nc.semaphore("prepared"))
        zeroed = es.enter_context(nc.semaphore("zeroed"))
        consts = es.enter_context(nc.semaphore("consts"))
        consts_dve = es.enter_context(nc.semaphore("consts_dve"))
        N_ZERO, N_CONST, N_CONST_DVE, N_PREPARED = 6, 5, 10, 5
        N_FIRST = 16 * (len(COLS) + 2)
        N_LOAD = 16 * (6 + 6 + 2 * NC + 2 * 2 * HG)

        block = es.enter_context(nc.Block())
        x_v = x.rearrange("b (t p) d -> b p t d", p=P)
        out_v = out.rearrange("b (t p) d -> b p t d", p=P)

        @block.sync
        def _(sp):
            loads = {first_in: 0, w_in: 0}

            def load(dst, src, arrived=w_in):
                loads[arrived] += 16
                sp.dma_start(dst, src).then_inc(arrived, 16)

            load(wqkv[:, :, :], l0_wqkv.rearrange("(f p) n -> p f n", p=P), first_in)
            sp.dma_start(x_ln[:, :, :], x_v[0]).then_inc(S["x_in"], 16)
            with nc.allow_non_contiguous_dma(reason="vectors over features, once"):
                for i, v in enumerate(cols_dram):
                    load(cols[:, i, :], v.rearrange("(f p) -> p f", p=P), first_in)
                load(bff1[:, :], l0_bff1.rearrange("(f p) -> p f", p=P), first_in)
            assert loads[first_in] == N_FIRST

            def load_rest(b, _):
                if now.phase != "fill0":
                    return
                for row, v in ((bproj_sa_row, l0_bproj_sa), (bproj_ca_row, l0_bproj_ca), (bff2_row, l0_bff2),
                               (btok_row, l1_b_proj), (gout_row, l1_g_out), (bout_row, l1_beta_out)):
                    load(row[:, :], v.rearrange("(a n) -> a n", a=1).broadcast_to((P, D)))
                for k, w in enumerate((l0_wff1, l0_wff2)):
                    load(ff_f32[:, k].rearrange("p (f n) -> p f n", n=w.shape[1]),
                         w.rearrange("(f p) n -> p f n", p=P))
                for dst, w in ((wq_ca, l0_wq_ca), (w_u, l1_w_u), (w_r, l1_w_r), (w_n, l1_w_n)):
                    load(dst[:, :, :], w.rearrange("(f p) n -> p f n", p=P))
                for c in range(NC):
                    load(wkv_ca[0:CK[c], c, :], l0_wkv_ca[c * P:c * P + CK[c], :])
                    load(wtok[0:CK[c], c, :], l1_w_proj[c * P:c * P + CK[c], :])
                for dst, w in ((wproj_sa, l0_wproj_sa), (wproj_ca, l0_wproj_ca)):
                    wv = w.rearrange("(q e j d) n -> e j d q n", e=2, j=HG, d=DH)
                    for j in range(HG):
                        for e in range(2):
                            row = j * QW + e * DH
                            load(dst[row:row + DH, :, :], wv[e, j])
                assert loads[w_in] == N_LOAD

            now = Now()

            def load_p(b, _):
                if now.phase == "fill0":
                    return
                if now.phase == "fill1":
                    sp.wait_ge(S["h1"], n("h1", b, 0))
                else:
                    sp.wait_ge(S["h2"], n("h2", now.batch("B"), NF))
                sp.dma_start(x_ln[:, :, :], x_v[b[0] + b[1]]).then_inc(S["x_in"], 16)

            def load_ctx(b, _):
                if now.phase != "fill1":
                    sp.wait_ge(S["ctxT_done"], n("ctxT_done", b, 0))
                for half in range(2):
                    sp.dma_start(ctx_sb[half * C:half * C + C, :], ctx_768[b[0] + b[1]]).then_inc(S["ctx_in"], 16)

            def load_x(b, _):
                if now.phase != "fill1":
                    sp.wait_ge(S["psn_norm"], n("psn_norm", b, 0))
                    sp.wait_ge(S["xT_done"], n("xT_done", b, 0))
                sp.dma_start(xs[:, :, :], x_v[b[0] + b[1]]).then_inc(S["x_res_in"], 16)

            def parts_out(b, name, dram):
                for f in range(NF):
                    for p, part in enumerate(("hi", "lo")):
                        src = (part_hi, part_lo)[p]
                        sp.wait_ge(S[f"{name}_{part}_done"], n(f"{name}_{part}_done", b, f + 1))
                        heads = slice(f * NP // NF, (f + 1) * NP // NF)
                        sp.dma_start(dram[p, :, heads, :].rearrange("r m t -> m r t"), src[:, f, :].bitcast(f32))\
                          .then_inc(S[f"{name}_{part}_out"], 16)

            def stack(b, name, dram, slots, dst, base_odd):
                for p, slot, k in slots:
                    out_sem = f"{name}_{('hi', 'lo')[p]}_out"
                    if name != "q":
                        sp.wait_ge(S[out_sem], n(out_sem, b, 16 * NF))
                    for e in range(2):
                        row = e * base_odd + slot * DH
                        src = dram[p, e * DH:e * DH + DH].rearrange("d m t -> d (m t)").unsqueeze(0)
                        sp.dma_start(dst[row:row + k * DH, :, :].bitcast(f32), src.to_broadcast([k, DH, NP * T]))\
                          .then_inc(S[f"{name}_stacked"], 16)

            Q_SLOTS = ((0, 0, 2), (1, 2, 1))
            K_SLOTS = ((0, 1, 2), (1, 0, 1))

            def stack_a(b, _):
                if now.phase != "fill0":
                    sp.wait_ge(S["exp_done"], n("exp_done", b, 0))
                stack(b, "q", d_q, Q_SLOTS, q_st, P // 2)
                stack(b, "k", d_k, K_SLOTS, k_st, P // 2)

            def k2_out(b, _):
                for p, part in enumerate(("hi", "lo")):
                    sp.wait_ge(S[f"k2_{part}_done"], n(f"k2_{part}_done", b, 1))
                    sp.dma_start(d_k2[p].rearrange("(f p) c -> p f c", p=P), (k2_hi, k2_lo)[p][:, :, :].bitcast(f32))\
                      .then_inc(S[f"k2_{part}_out"], 16)

            def stack_k2(b, _):
                for p, part in enumerate(("hi", "lo")):
                    out_sem = f"k2_{part}_out"
                    sp.wait_ge(S[out_sem], n(out_sem, b, 16))
                    src = d_k2[p].rearrange("(m e d) c -> e d m c", e=2, d=DH)
                    for slot, of in enumerate((1, 0, 0)):
                        if of == p:
                            for e in range(2):
                                row = e * 3 * DH + slot * DH
                                for half in range(2):
                                    heads = slice(4 * half, 4 * half + 4)
                                    sp.dma_start(k2_st[row:row + DH, heads, e * C:e * C + C].bitcast(f32),
                                                 src[e][:, heads, :]).then_inc(S["k2_stacked"], 16)

            def maxima(b, ready, done, dst, row_of):
                sp.wait_ge(S[ready], n(ready, b, 1))
                for part in range(4):
                    row = row_of(part)
                    sp.dma_start(dst[row:row + 1, :, :].bitcast(f32), nmT[part * NP:part * NP + NP, :].bitcast(f32))\
                      .then_inc(S[done], 16)

            run(sp, now, {
                "load_p": load_p, "load_ctx": load_ctx, "load_x": load_x, "load_rest": load_rest,
                "q": lambda b, _: parts_out(b, "q", d_q),
                "k": lambda b, _: parts_out(b, "k", d_k),
                "q2": lambda b, _: parts_out(b, "q2", d_q2),
                "stack": stack_a, "k2": k2_out, "k2_stack": stack_k2,
                "stack2": lambda b, _: stack(b, "q2", d_q2, Q_SLOTS, q2_st, 3 * DH),
                "negm": lambda b, _: maxima(b, "nmT_done", "max_stacked", q_st, lambda p: p // 2 * 64 + SA_K + p % 2),
                "negm2": lambda b, _: maxima(b, "nmT2_done", "max2_stacked", q2_st, lambda p: CA_K + p),
            })

        @block.gpsimd
        def _(pool):
            for tile in (v_sa, ident, ident_bf, mask_bf, maskT_bf, v_ca):
                pool.memset(tile[:], 0.0).then_inc(zeroed, 1)
            pool.memset(neg_half[:, :], -0.5).then_inc(consts, 1)
            pool.wait_ge(zeroed, N_ZERO)
            pool.affine_select(out=ident[:, :], in_=ident[:, :], compare_op=ALU.not_equal, fill=1.0, base=0,
                               pattern=[[-1, P]], channel_multiplier=1).then_inc(consts, 1)
            pool.affine_select(out=ident_bf[:, :], in_=ident_bf[:, :], compare_op=ALU.not_equal, fill=1.0, base=0,
                               pattern=[[-1, P]], channel_multiplier=1).then_inc(consts, 1)
            pool.affine_select(out=mask_bf[:, :], in_=mask_bf[:, :], compare_op=ALU.is_ge, fill=MASKED, base=0,
                               pattern=[[-1, P]], channel_multiplier=1).then_inc(consts, 1)
            pool.affine_select(out=maskT_bf[:, :], in_=maskT_bf[:, :], compare_op=ALU.is_ge, fill=MASKED, base=0,
                               pattern=[[1, P]], channel_multiplier=-1).then_inc(consts, 1)

            pool.wait_ge(consts, N_CONST)
            now = Now()

            def root(ln):
                k = NORMS.index(ln)

                def step(b, _):
                    pool.wait_ge(S[f"{ln}_var"], n(f"{ln}_var", b, NT + 1))
                    pool.tensor_tensor(rstd_of[:, k, :], ve_of[:, k, :], neg_half[:, :], ALU.pow)\
                        .then_inc(S[f"{ln}_rstd"], 1)
                return step

            def bias(tile, row, ready, count, done):
                def step(b, _):
                    pool.wait_ge(S[ready], n(ready, b, count))
                    for t in range(NT):
                        last = pool.tensor_tensor(tile[:, t, :], tile[:, t, :], row[:, :], ALU.add)
                    last.then_inc(S[done], 1)
                return step

            def finish(b, _):
                pool.wait_ge(S["fin_norm"], n("fin_norm", b, NT))
                for t in range(NT):
                    last = pool.tensor_tensor(y_sb[:, t, :], y_sb[:, t, :], gout_row[:, :], ALU.mult)
                last.then_inc(S["gained"], 1)
                pool.wait_ge(S["gained"], n("gained", b, 1))
                for t in range(NT):
                    last = pool.tensor_tensor(y_sb[:, t, :], y_sb[:, t, :], bout_row[:, :], ALU.add)
                last.then_inc(S["y_done"], 1)
                pool.wait_ge(S["y_done"], n("y_done", b, 1))
                pool.dma_start(out_v[b[0] + b[1]], y_sb[:, :, :]).then_inc(S["y_stored"], 16)
                pool.wait_ge(S["y_stored"], n("y_stored", b, 16))
                pool.tensor_tensor(mark[:, :], neg_half[:, 0:1], neg_half[:, 0:1], ALU.mult).then_inc(S["y_left"], 1)

            run(pool, now, {**{f"{ln}_stat": root(ln) for ln in NORMS},
                            "bias_a": bias(xs, bproj_sa_row, "x_res_in", 16, "x_biased"),
                            "ln2_norm": bias(xs, bproj_ca_row, "ln2_norm", NT, "x1b_done"),
                            "ln3_norm": bias(xs, bff2_row, "ln3_norm", NT, "x2b_done"), "fin_norm": finish})
            pool.wait_ge(S["y_stored"], n("y_stored", (0, B), 0))

        @block.scalar
        def _(act):
            act.wait_ge(first_in, N_FIRST)
            act.wait_ge(consts_dve, N_CONST_DVE)
            act.wait_ge(consts, N_CONST)
            now = Now()

            def turned(use, dst, done, gain, bias):
                def step(b, _):
                    for f in range(NF):
                        ps = full(act, now, (use, f))
                        act.activation(dst[:, f, :], ps[:, :], ACT.Identity, scale=col(gain, f), bias=col(bias, f))\
                           .then_inc(S[done], 1)
                return step

            def turned_high(b, _):
                for f in range(NF):
                    ps = full(act, now, ("ln3T", f))
                    for dst, done in ((hT, "h3"), (h3_hi, "h3_hi_done")):
                        act.activation(dst[:, f, :], ps[:, :], ACT.Identity, scale=col("g3", f), bias=col("b3", f))\
                           .then_inc(S[done], 1)

            def high(use, before):
                def step(b, _):
                    for f in range(NF):
                        ps = full(act, now, (use, f))
                        ob, own = outs_batch(now, b, use)
                        if ob is not None and f == 0:
                            act.wait_ge(S[f"{before}_lo_done"], n(f"{before}_lo_done", ob, own * NF))
                            act.wait_ge(S[f"{before}_hi_out"], n(f"{before}_hi_out", ob, own * 16 * NF))
                        act.activation(part_hi[:, f, :], ps[:, :], ACT.Copy).then_inc(S[f"{use}_hi_done"], 1)
                return step

            def values(b, i):
                ps = full(act, now, ("v", i))
                for t in range(2):
                    last = act.activation(v_sa[:, 2 * i + t, :, 0:DH],
                                          ps[:, t * D:t * D + D].rearrange("p (h d) -> p h d", h=H), ACT.Copy)
                last.then_inc(S["v_done"], 1)

            def ctx_turned(b, _):
                ps = full(act, now, ("ctxT", 0))
                act.activation(ctxT[:, 0, :], ps[:, 0:P], ACT.Copy)
                act.activation(ctxT[0:CK[1], 1, :], ps[0:CK[1], P:2 * P], ACT.Copy).then_inc(S["ctxT_done"], 1)

            def keys2_high(b, _):
                ps = full(act, now, ("k2", 0))
                act.activation(k2_hi[:, :, :], ps[:, 0:NF * C].rearrange("p (f c) -> p f c", f=NF), ACT.Copy)\
                   .then_inc(S["k2_hi_done"], 1)

            def values2(b, _):
                ps = full(act, now, ("v2", 0))
                for e in range(2):
                    rows = slice(e * C, e * C + C)
                    act.activation(v_ca[rows, :, e * QW:e * QW + DH],
                                   ps[rows, 0:D].rearrange("p (t e d) -> p e t d", e=2, d=DH)[:, e], ACT.Copy)\
                       .then_inc(S["v2_done"], 1)

            def tokens_turned(b, _):
                ps = full(act, now, ("tokT", 0))
                for f in range(NF):
                    act.activation(tokT[:, f, :], ps[:, f * C:f * C + C], ACT.Identity, bias=col("btok", f))\
                       .then_inc(S["tokT_done"], 1)

            def maxima(use, done):
                def step(b, _):
                    ps = full(act, now, (use, 0))
                    act.activation(nmT[:, :], ps[0:2 * H, :], ACT.Copy).then_inc(S[done], 1)
                return step

            def exps(b, st):
                kb = st % NT
                if st == 0 and now.phase == "fill1":
                    act.wait_ge(prepared, N_PREPARED)
                for pr in range(2):
                    ps = full(act, now, ("st", 2 * st + pr))
                    if st >= 2:
                        act.wait_ge(S["pv_used"], n("pv_used", b, st - 1))
                    act.activation(probs[:, st % 2, 2 * pr:2 * pr + 2, kb * P:T], ps[:, :, 0:T - kb * P], ACT.Exp,
                                   scale=ATT_SCALE).then_inc(S["exp_done"], 1)

            def exps2(b, u):
                ps = full(act, now, ("st2", u))
                if u == 0 and now.phase != "fill2":
                    act.wait_ge(S["y_left"], n("y_left", b, 0))
                act.activation(probs2[:, 2 * u:2 * u + 2, :], ps[:, :, :], ACT.Exp,
                               scale=ATT_SCALE).then_inc(S["exp2_done"], 1)

            def gelu(b, f):
                ps = full(act, now, ("ff1", f))
                if f >= 2:
                    act.wait_ge(S["gelu_lo"], n("gelu_lo", b, f - 1))
                act.activation(hidden_sb[:, f % 2, :], ps[:, :], ACT.Gelu, bias=bff1[:, f:f + 1])\
                   .then_inc(S["gelu_done"], 1)
                act.activation(gT_hi[:, f, :], ps[:, :], ACT.Gelu, bias=bff1[:, f:f + 1]).then_inc(S["gelu_hi"], 1)

            def state_turned(b, _):
                for f in range(NF):
                    ps = full(act, now, ("xT", f))
                    act.activation(xT[:, f, :], ps[:, :], ACT.Copy).then_inc(S["xT_done"], 1)

            def route_exps(b, _):
                ps = full(act, now, ("route", 0))
                act.wait_ge(S["rbias_done"], n("rbias_done", b, 1))
                for t in range(NT):
                    act.activation(route[:, t, :], ps[:, t * C:t * C + C], ACT.Exp, bias=rmax[:, NT + t:NT + t + 1],
                                   scale=ROUTE_SCALE).then_inc(S["rexp_done"], 1)

            def route_turned(b, _):
                ps = full(act, now, ("routeT", 0))
                act.activation(routeT, ps[:, 0:2 * P].rearrange("p (i c) -> p i c", i=2), ACT.Copy)\
                   .then_inc(S["routeT_done"], 1)

            def gate(i, use, dst, done):
                def step(b, f):
                    ps = full(act, now, (use, f))
                    act.activation(dst[:, f, :], ps[:, :], ACT.Tanh, scale=0.5, bias=half_bias[:, i, f:f + 1])\
                       .then_inc(S[done], 1)
                return step

            def candidate(b, f):
                ps = full(act, now, ("n", f))
                act.activation(cand[:, f, :], ps[:, :], ACT.Tanh, bias=col("b_n", f)).then_inc(S["cand_done"], 1)

            run(act, now, {
                "ln1T": turned("ln1T", hT_a, "h1", "g1", "b1"),
                "q": high("q", "q2"), "k": high("k", "q"), "q2": high("q2", "k"),
                "v": values, "ctxT": ctx_turned, "k2": keys2_high, "v2": values2, "tokT": tokens_turned,
                "ln2T": turned("ln2T", hT, "h2", "g2", "b2"),
                "ln3T": turned_high,
                "psnT": turned("psnT", psnT, "psn_done", "g_state", "beta_state"),
                "innT": turned("innT", hT, "inn_done", "g_input", "beta_input"),
                "negm": maxima("negmT", "nmT_done"), "negm2": maxima("negm2T", "nmT2_done"),
                "st": exps, "st2": exps2,
                "ff1": gelu, "xT": state_turned, "route": route_exps, "routeT": route_turned,
                "rb": gate(0, "r", t_r, "tr_done"), "u": gate(1, "u", t_u, "tu_done"), "n": candidate,
            })

        @block.vector
        def _(dve):
            dve.memset(k_st[:, :, :].bitcast(f32), 1.0).then_inc(consts_dve, 1)
            dve.memset(k2_st[:, :, :].bitcast(f32), 0.0).then_inc(consts_dve, 1)
            dve.wait_ge(consts_dve, 2)
            dve.memset(k2_st[CA_K:CA_K + 2, :, 0:C].bitcast(f32), 1.0).then_inc(consts_dve, 1)
            dve.memset(k2_st[CA_K:CA_KM, :, C:2 * C].bitcast(f32), 1.0).then_inc(consts_dve, 1)
            dve.wait_ge(consts_dve, 4)
            dve.memset(k2_st[CA_K:CA_K + 2, :, C:2 * C].bitcast(f32), 0.0).then_inc(consts_dve, 1)
            dve.wait_ge(zeroed, N_ZERO)
            dve.memset(v_sa[:, :, :, DH:DH + 1], 1.0).then_inc(consts_dve, 1)
            dve.memset(v_ca[0:C, :, DH:DH + 1], 1.0).then_inc(consts_dve, 1)
            dve.memset(v_ca[C:2 * C, :, QW + DH:QW + DH + 1], 1.0).then_inc(consts_dve, 1)
            dve.wait_ge(first_in, N_FIRST)
            dve.tensor_scalar(half_bias[:, 0, :], cols[:, COLS.index("b_r"), :], 0.5, None, ALU.mult)\
               .then_inc(consts_dve, 1)
            dve.tensor_scalar(half_bias[:, 1, :], cols[:, COLS.index("b_u"), :], 0.5, None, ALU.mult)\
               .then_inc(consts_dve, 1)
            now = Now()

            def new_state(t):
                _, k, _, _ = PLACE[now.phase, ("new", t // 2)]
                return bank[k][:, (t % 2) * D:(t % 2) * D + D]

            def stat(ln, src, ready=None):
                k = NORMS.index(ln)
                stats, mv, ve = stats_of[:, k], mv_of[:, k], ve_of[:, k]

                def step(b, _):
                    if ready is not None:
                        dve.wait_ge(S[ready[0]], n(ready[0], b, ready[1]))
                    for t in range(NT):
                        if ln == "fin" and t % 2 == 0:
                            full(dve, now, ("new", t // 2))
                        dve.bn_stats(stats[:, t, :], src(t))
                    dve.drain()
                    for t in range(NT):
                        dve.bn_aggr(mv[:, t, :], stats[:, t, :]).then_inc(S[f"{ln}_var"], 1)
                    dve.wait_ge(S[f"{ln}_var"], n(f"{ln}_var", b, NT))
                    dve.tensor_scalar(ve[:, :], mv[:, :, 1], EPS, None, ALU.add).then_inc(S[f"{ln}_var"], 1)
                return step

            def norm(ln, src, dst):
                k = NORMS.index(ln)
                mv, rstd = mv_of[:, k], rstd_of[:, k]

                def step(b, _):
                    dve.wait_ge(S[f"{ln}_rstd"], n(f"{ln}_rstd", b, 1))
                    for t in range(NT):
                        dve.tensor_scalar(dst[:, t, :], src(t), mv[:, t, 0:1], rstd[:, t:t + 1], ALU.subtract,
                                          ALU.mult)\
                           .then_inc(S[f"{ln}_norm"], 1)
                return step

            def low(use, outs):
                def step(b, _):
                    for f in range(NF):
                        dve.wait_ge(S[f"{use}_hi_done"], n(f"{use}_hi_done", b, f + 1))
                        ps = full(dve, now, (use, f))
                        ob, own = outs_batch(now, b, use)
                        if ob is not None and f == 0:
                            dve.wait_ge(S[outs], n(outs, ob, own * 16 * NF))
                        dve.tensor_tensor(part_lo[:, f, :], ps[:, :], part_hi[:, f, :].bitcast(f32), ALU.subtract)\
                           .then_inc(S[f"{use}_lo_done"], 1)
                return step

            def keys2_low(b, _):
                ps = full(dve, now, ("k2", 0))
                dve.wait_ge(S["k2_hi_done"], n("k2_hi_done", b, 1))
                dve.tensor_tensor(k2_lo[:, :, :], ps[:, 0:NF * C].rearrange("p (f c) -> p f c", f=NF),
                                  k2_hi[:, :, :].bitcast(f32), ALU.subtract).then_inc(S["k2_lo_done"], 1)

            def tokens(b, _):
                ps = full(dve, now, ("tok", 0))
                dve.tensor_tensor(tok[:, :], ps[:, 0:D], btok_row[:, :], ALU.add).then_inc(S["tok_done"], 1)

            def maximum(b, u):
                qb, h, per = MAX_UNITS[u]
                w = (qb + 1) * P
                ps = full(dve, now, ("max", u))
                dve.tensor_reduce(negm[:, qb, h:h + 2 * per].rearrange("p (m e) -> p e m", e=2),
                                  ps[:, :, 0:per * w].rearrange("p a (h w) -> p a h w", w=w), AX.X, ALU.max,
                                  negate=True).then_inc(S["max_done"], 1)

            def maximum2(b, t):
                ps = full(dve, now, ("max2", t))
                dve.tensor_reduce(negm2[:, t, :].rearrange("p (a h) -> p a h", a=2),
                                  ps[:, :, :].rearrange("p a (h c) -> p a h c", c=C), AX.X, ALU.max,
                                  negate=True).then_inc(S["max2_done"], 1)

            def split_max(src, ready, count, hi_done, lo_done):
                def step(b, _):
                    dve.wait_ge(S[ready], n(ready, b, count))
                    parts = nm2[:, :, :, :].rearrange("p t a (b m) -> p t a b m", b=2)
                    heads = src[:, :, :].rearrange("p t (m e) -> p t e m", e=2)
                    dve.tensor_copy(parts[:, :, :, 0, :], heads).then_inc(S[hi_done], 1)
                    dve.wait_ge(S[hi_done], n(hi_done, b, 1))
                    dve.tensor_tensor(parts[:, :, :, 1, :], heads, parts[:, :, :, 0, :].bitcast(f32), ALU.subtract)\
                       .then_inc(S[lo_done], 1)
                return step

            def normalise(use, turned, packed, att, names):
                blocked, inverted, divided, done = names
                blocks = turned.rearrange("p (t r) -> p t r", r=QW)
                pairs = packed.rearrange("p (t e r) -> p e t r", e=2, r=DH)

                def step(b, g):
                    if g:
                        dve.wait_ge(S[divided], n(divided, b, g))
                    ps = full(dve, now, (use, g))
                    dve.transpose(turned, ps[:, :]).then_inc(S[blocked], 1)
                    dve.wait_ge(S[blocked], n(blocked, b, g + 1))
                    dve.reciprocal(inv[:, :], blocks[:, :, DH]).then_inc(S[inverted], 1)
                    if g == 2:
                        dve.wait_ge(S[done], n(done, b, 1))
                    dve.wait_ge(S[inverted], n(inverted, b, g + 1))
                    dve.tensor_tensor(pairs[:, g % 2], blocks[:, :, 0:DH],
                                      inv[:, :].unsqueeze(2).to_broadcast([P, T // QW, DH]), ALU.mult)\
                       .then_inc(S[divided], 1)
                    if use == "pv2" and g == 1 and now.phase in ("fill2", "loop"):
                        dve.wait_ge(S["k_hi_out"], n("k_hi_out", now.batch("P"), 16 * NF))
                    if g % 2:
                        dve.wait_ge(S[divided], n(divided, b, g + 1))
                        dve.transpose(att[:, g // 2, :], packed).then_inc(S[done], 1)
                return step

            def residual(use, src, biased, done):
                def step(b, i):
                    if i == 0:
                        dve.wait_ge(S[biased], n(biased, b, 1))
                    ps = full(dve, now, (use, i))
                    dve.tensor_tensor(xs[:, 2 * i:2 * i + 2, :], ps[:, :].rearrange("p (t d) -> p t d", t=2),
                                      src[:, 2 * i:2 * i + 2, :], ALU.add).then_inc(S[done], 1)
                return step


            def hidden_residual(b, t):
                if t == 0:
                    dve.wait_ge(S["x2b_done"], n("x2b_done", b, 1))
                ps = full(dve, now, ("ff2", t))
                dve.tensor_tensor(xs[:, t, :], ps[:, 0:D], xs[:, t, :], ALU.add).then_inc(S["x3_done"], 1)

            def route_max(b, _):
                ps = full(dve, now, ("route", 0))
                dve.tensor_reduce(rmax[:, 0:NT], ps[:, 0:NT * C].rearrange("p (t c) -> p t c", t=NT), AX.X, ALU.max,
                                  negate=True).then_inc(S["rmax_done"], 1)
                dve.wait_ge(S["rmax_done"], n("rmax_done", b, 1))
                dve.tensor_scalar(rmax[:, NT:2 * NT], rmax[:, 0:NT], ROUTE_SCALE, None, ALU.mult)\
                   .then_inc(S["rbias_done"], 1)

            def route_sum(b, _):
                dve.wait_ge(S["rexp_done"], n("rexp_done", b, NT))
                dve.tensor_reduce(rden[:, 0:NT], route, AX.X, ALU.add).then_inc(S["rtotal_done"], 1)
                dve.wait_ge(S["rtotal_done"], n("rtotal_done", b, 1))
                dve.reciprocal(rden[:, NT:2 * NT], rden[:, 0:NT]).then_inc(S["rden_done"], 1)

            def routed_norm(b, _):
                dve.wait_ge(S["rden_done"], n("rden_done", b, 1))
                for i in range(2):
                    ps = full(dve, now, ("routed", i))
                    for t in (i, i + 2):
                        dve.tensor_scalar(routed[:, t, :], ps[:, (t // 2) * D:(t // 2) * D + D],
                                          rden[:, NT + t:NT + t + 1], None, ALU.mult).then_inc(S["routed_done"], 1)

            def reset(b, f):
                dve.wait_ge(S["tr_done"], n("tr_done", b, f + 1))
                dve.scalar_tensor_tensor(out=t_r[:, f, :], in0=t_r[:, f, :], scalar=1.0, in1=psnT[:, f, :],
                                         op0=ALU.add, op1=ALU.mult).then_inc(S["rp_done"], 1)

            def update(b, f):
                dve.wait_ge(S["cand_done"], n("cand_done", b, f + 1))
                dve.tensor_tensor(cand[:, f, :], cand[:, f, :], xT[:, f, :], ALU.subtract)\
                   .then_inc(S["diff_done"], 1)
                dve.wait_ge(S["diff_done"], n("diff_done", b, f + 1))
                dve.scalar_tensor_tensor(out=t_u[:, f, :], in0=t_u[:, f, :], scalar=1.0, in1=cand[:, f, :],
                                         op0=ALU.add, op1=ALU.mult).then_inc(S["step_done"], 1)
                dve.wait_ge(S["step_done"], n("step_done", b, f + 1))
                dve.scalar_tensor_tensor(out=cand[:, f, :], in0=t_u[:, f, :], scalar=0.5, in1=xT[:, f, :],
                                         op0=ALU.mult, op1=ALU.add).then_inc(S["new_done"], 1)

            def prepare(b, _):
                if now.phase != "fill0":
                    return
                dve.wait_ge(w_in, N_LOAD)
                dve.tensor_scalar(w_n[:, 0:NF, :], w_n[:, 0:NF, :], 0.5, None, ALU.mult).then_inc(prepared, 1)
                for w, (hi, lo) in enumerate(((wff1_hi, wff1_lo), (wff2_hi, wff2_lo))):
                    hi, lo = (part[:, :, :].rearrange("p f n -> p (f n)") for part in (hi, lo))
                    dve.tensor_copy(hi, ff_f32[:, w]).then_inc(prepared, 1)
                    dve.wait_ge(prepared, 2 * w + 2)
                    dve.tensor_tensor(lo, ff_f32[:, w], hi.bitcast(f32), ALU.subtract).then_inc(prepared, 1)

            def h3_low(b, _):
                for f in range(NF):
                    dve.wait_ge(S["h3_hi_done"], n("h3_hi_done", b, f + 1))
                    dve.tensor_tensor(h3_lo[:, f, :], hT[:, f, :], h3_hi[:, f, :].bitcast(f32), ALU.subtract)\
                       .then_inc(S["h3_lo_done"], 1)

            def hidden_low(b, f):
                dve.wait_ge(S["gelu_hi"], n("gelu_hi", b, f + 1))
                dve.tensor_tensor(gT_lo[:, f, :], hidden_sb[:, f % 2, :], gT_hi[:, f, :].bitcast(f32), ALU.subtract)\
                   .then_inc(S["gelu_lo"], 1)

            def of(tile):
                return lambda t: tile[:, t, :]

            run(dve, now, {
                "ln1_stat": stat("ln1", of(x_ln), ("x_in", 16)), "ln1_norm": norm("ln1", of(x_ln), x_ln),
                "ln2_stat": stat("ln2", of(xs), ("x1_done", 2)), "ln2_norm": norm("ln2", of(xs), xh),
                "ln3_stat": stat("ln3", of(xs), ("x2_done", 2)), "ln3_norm": norm("ln3", of(xs), xh),
                "psn_stat": stat("psn", of(xs), ("x3_done", NT)), "psn_norm": norm("psn", of(xs), xh),
                "inn_stat": stat("inn", of(routed), ("routed_done", NT)), "inn_norm": norm("inn", of(routed), xh),
                "fin_stat": stat("fin", new_state), "fin_norm": norm("fin", new_state, y_sb),
                "q": low("q", "q2_lo_out"), "k": low("k", "q_lo_out"), "q2": low("q2", "k_lo_out"),
                "k2": keys2_low, "tok": tokens, "max": maximum, "max2": maximum2,
                "split_max": split_max(negm, "max_done", len(MAX_UNITS), "nm_hi_done", "nm_lo_done"),
                "negm2": split_max(negm2, "max2_done", NT, "nm2_hi_done", "nm2_lo_done"),
                "norm": normalise("pv", turned[:, 0, :], packed[:, 0, :], attT,
                                  ("pv_turned", "sum_inv", "pv_divided", "att_done")),
                "norm2": normalise("pv2", turned[:, 1, :], packed[:, 1, :], att2T,
                                   ("pv2_turned", "sum2_inv", "pv2_divided", "att2_done")),
                "proj": residual("proj", xs, "x_biased", "x1_done"),
                "prepare": prepare, "ln3T": h3_low, "ff1": hidden_low,
                "proj2": residual("proj2", xs, "x1b_done", "x2_done"), "ff2": hidden_residual,
                "route": route_max, "routeT": route_sum, "routed": routed_norm, "rb": reset, "n": update,
            })

        @block.tensor
        def _(pe):
            pe.wait_ge(first_in, N_FIRST)
            pe.wait_ge(consts, N_CONST)
            pe.wait_ge(consts_dve, N_CONST_DVE)
            now = Now()

            def turn(use, src, ready):
                def step(b, _):
                    for f in range(NF):
                        ps = free(pe, now, b, (use, f))
                        for t in range(NT):
                            if f == 0:
                                pe.wait_ge(S[ready], n(ready, b, t + 1))
                            last = pe.transpose(ps[:, t * P:t * P + P], src[:, t, f * P:f * P + P], ident[:, :])
                        last.then_inc(filled(now, (use, f)), 1)
                return step

            def project_T(use, w, at, rhs, ready):
                def step(b, _):
                    for f in range(NF):
                        ps = free(pe, now, b, (use, f))
                        for kt in range(NF):
                            pe.wait_ge(S[ready], n(ready, b, kt + 1))
                            last = pe.matmul(ps[:, :], w[:, kt, at + f * P:at + f * P + P], rhs[:, kt, :],
                                             start=(kt == 0), stop=(kt == NF - 1))
                        last.then_inc(filled(now, (use, f)), 1)
                return step

            def values(b, i):
                ps = free(pe, now, b, ("v", i))
                for t in (2 * i, 2 * i + 1):
                    for kt in range(NF):
                        last = pe.matmul(ps[:, (t % 2) * D:(t % 2) * D + D], hT_a[:, kt, t * P:t * P + P],
                                         wqkv[:, kt, 2 * D:3 * D], start=(kt == 0), stop=(kt == NF - 1))
                last.then_inc(filled(now, ("v", i)), 1)

            def ctx_turn(b, _):
                ps = free(pe, now, b, ("ctxT", 0))
                pe.wait_ge(S["ctx_in"], n("ctx_in", b, 32))
                for c in range(NC):
                    last = pe.transpose(ps[0:CK[c], c * P:c * P + P], ctx_sb[:, c * P:c * P + CK[c]], ident[:, :])
                last.then_inc(filled(now, ("ctxT", 0)), 1)

            def ctx_features(use, w):
                def step(b, _):
                    ps = free(pe, now, b, (use, 0))
                    pe.wait_ge(S["ctxT_done"], n("ctxT_done", b, 1))
                    for f in range(NF):
                        for c in range(NC):
                            last = pe.matmul(ps[:, f * C:f * C + C], w[0:CK[c], c, f * P:f * P + P],
                                             ctxT[0:CK[c], c, 0:C], start=(c == 0), stop=(c == NC - 1))
                    last.then_inc(filled(now, (use, 0)), 1)
                return step

            def ctx_rows(use, w, at):
                def step(b, _):
                    ps = free(pe, now, b, (use, 0))
                    for c in range(NC):
                        last = pe.matmul(ps[:, 0:D], ctxT[0:CK[c], c, :], w[0:CK[c], c, at:at + D],
                                         start=(c == 0), stop=(c == NC - 1))
                    last.then_inc(filled(now, (use, 0)), 1)
                return step

            def scores(b, u):
                if u == 0:
                    pe.wait_ge(S["q_stacked"], n("q_stacked", b, PER["q_stacked"]))
                    pe.wait_ge(S["k_stacked"], n("k_stacked", b, PER["k_stacked"]))
                qb, h0, per = MAX_UNITS[u]
                w = (qb + 1) * P
                ps = free(pe, now, b, ("max", u))
                for i in range(2 * per):
                    e, m, at = i % 2, (h0 + i) // 2, (i // 2) * w
                    pe.matmul(ps[:, e, at:at + w], q_st[64 * e:64 * e + SA_K, m, qb * P:qb * P + P],
                              k_st[64 * e:64 * e + SA_K, m, 0:w], start=True, stop=False)
                    last = pe.matmul(ps[:, e, at + qb * P:at + w], ident_bf[:, :], mask_bf[:, :],
                                     start=False, stop=True)
                last.then_inc(filled(now, ("max", u)), 1)

            def scores2(b, t):
                if t == 0:
                    pe.wait_ge(S["q2_stacked"], n("q2_stacked", b, PER["q2_stacked"]))
                    pe.wait_ge(S["k2_stacked"], n("k2_stacked", b, PER["k2_stacked"]))
                ps = free(pe, now, b, ("max2", t))
                for m in range(NP):
                    at = (m % 4) * 2 * C
                    last = pe.matmul(ps[:, m // 4, at:at + 2 * C], q2_st[0:CA_K, m, t * P:t * P + P],
                                     k2_st[0:CA_K, m, :], start=True, stop=True)
                last.then_inc(filled(now, ("max2", t)), 1)

            def turn_max(use, ready):
                def step(b, _):
                    ps = free(pe, now, b, (use, 0))
                    pe.wait_ge(S[ready], n(ready, b, 1))
                    for t in range(NT):
                        last = pe.transpose(ps[0:2 * H, t * P:t * P + P],
                                            nm2[:, t, :, :].bitcast(f32).rearrange("p a h -> p (a h)"), ident[:, :])
                    last.then_inc(filled(now, (use, 0)), 1)
                return step

            def scores_T(b, st):
                g, kb = st // NT, st % NT
                if st == 0:
                    pe.wait_ge(S["max_stacked"], n("max_stacked", b, 64))
                for pr in range(2):
                    u = 2 * st + pr
                    ps = free(pe, now, b, ("st", u))
                    m = (HG * g + 2 * pr) // 2
                    for i in range(2):
                        pe.matmul(ps[:, i, 0:T - kb * P], k_st[64 * i:64 * i + SA_KM, m, kb * P:kb * P + P],
                                  q_st[64 * i:64 * i + SA_KM, m, kb * P:T], start=True, stop=False)
                    for i in range(2):
                        last = pe.matmul(ps[:, i, 0:P], ident_bf[:, :], maskT_bf[:, :], start=False, stop=True)
                    last.then_inc(filled(now, ("st", u)), 1)

            def weigh(b, st):
                g, kb = st // NT, st % NT
                if st == 0:
                    pe.wait_ge(S["v_done"], n("v_done", b, 2))
                ps = free(pe, now, b, ("pv", g)) if kb == 0 else acc[0]
                pe.wait_ge(S["exp_done"], n("exp_done", b, 2 * st + 2))
                for j in range(HG):
                    last = pe.matmul(ps[j * QW:j * QW + QW, kb * P:T], v_sa[:, kb, HG * g + j, :],
                                     probs[:, st % 2, j, kb * P:T], start=(kb == 0), stop=(kb == NT - 1))
                last.then_inc(S["pv_used"], 1)

            def scores2_T(b, u):
                if u == 0:
                    pe.wait_ge(S["max2_stacked"], n("max2_stacked", b, 64))
                ps = free(pe, now, b, ("st2", u))
                for i in range(2):
                    last = pe.matmul(ps[:, i, :], k2_st[0:CA_KM, 2 * u + i, :], q2_st[0:CA_KM, 2 * u + i, :],
                                     start=True, stop=True)
                last.then_inc(filled(now, ("st2", u)), 1)

            def weigh2(b, g):
                if g == 0:
                    pe.wait_ge(S["v2_done"], n("v2_done", b, 2))
                ps = free(pe, now, b, ("pv2", g))
                pe.wait_ge(S["exp2_done"], n("exp2_done", b, g + 1))
                for i in range(2):
                    last = pe.matmul(ps[i * 2 * QW:i * 2 * QW + 2 * QW, :], v_ca[:, 2 * g + i, :],
                                     probs2[:, 2 * g + i, :], start=True, stop=True)
                last.then_inc(filled(now, ("pv2", g)), 1)

            def project_out(use, w, src, done):
                def step(b, i):
                    ps = free(pe, now, b, (use, i))
                    for t in (2 * i, 2 * i + 1):
                        for q in range(NG // 2):
                            if t == 0:
                                pe.wait_ge(S[done], n(done, b, q + 1))
                            last = pe.matmul(ps[:, (t % 2) * D:(t % 2) * D + D], src[:, q, t * P:t * P + P],
                                             w[:, q, :], start=(q == 0), stop=(q == NG // 2 - 1))
                    last.then_inc(filled(now, (use, i)), 1)
                return step

            def hidden(b, f):
                ps = free(pe, now, b, ("ff1", f))
                first = True
                for kt in range(NF):
                    cols_f = slice(f * P, f * P + P)
                    if f == 0:
                        pe.wait_ge(S["h3_hi_done"], n("h3_hi_done", b, kt + 1))
                    for w in (wff1_hi, wff1_lo):
                        pe.matmul(ps[:, :], w[:, kt, cols_f], h3_hi[:, kt, :], start=first, stop=False)
                        first = False
                for kt in range(NF):
                    if f == 0:
                        pe.wait_ge(S["h3_lo_done"], n("h3_lo_done", b, kt + 1))
                    last = pe.matmul(ps[:, :], wff1_hi[:, kt, cols_f], h3_lo[:, kt, :], start=False,
                                     stop=(kt == NF - 1))
                last.then_inc(filled(now, ("ff1", f)), 1)

            def hidden_out(b, t):
                ps = free(pe, now, b, ("ff2", t))
                tokens = slice(t * P, t * P + P)
                for f in range(NFF):
                    if t == 0:
                        pe.wait_ge(S["gelu_hi"], n("gelu_hi", b, f + 1))
                    pe.matmul(ps[:, 0:D], gT_hi[:, f, tokens], wff2_hi[:, f, :], start=(f == 0), stop=False)
                    pe.matmul(ps[:, 0:D], gT_hi[:, f, tokens], wff2_lo[:, f, :], start=False, stop=False)
                    if t == 0:
                        pe.wait_ge(S["gelu_lo"], n("gelu_lo", b, f + 1))
                    last = pe.matmul(ps[:, 0:D], gT_lo[:, f, tokens], wff2_hi[:, f, :], start=False,
                                     stop=(f == NFF - 1))
                last.then_inc(filled(now, ("ff2", t)), 1)

            def prepare(b, _):
                if now.phase == "fill0":
                    pe.wait_ge(w_in, N_LOAD)
                    pe.wait_ge(prepared, N_PREPARED)

            def route_scores(b, _):
                ps = free(pe, now, b, ("route", 0))
                pe.wait_ge(S["xT_done"], n("xT_done", b, NF))
                pe.wait_ge(S["tokT_done"], n("tokT_done", b, NF))
                for t in range(NT):
                    for kt in range(NF):
                        last = pe.matmul(ps[:, t * C:t * C + C], xT[:, kt, t * P:t * P + P], tokT[:, kt, :],
                                         start=(kt == 0), stop=(kt == NF - 1))
                last.then_inc(filled(now, ("route", 0)), 1)

            def route_turn(b, _):
                ps = free(pe, now, b, ("routeT", 0))
                pe.wait_ge(S["rexp_done"], n("rexp_done", b, NT))
                for i in range(2):
                    last = pe.transpose(ps[:, i * P:i * P + P],
                                        turned[:, 0, 2 * i * C:2 * i * C + 2 * C], ident[:, :])
                last.then_inc(filled(now, ("routeT", 0)), 1)

            def route_tokens(b, _):
                pe.wait_ge(S["routeT_done"], n("routeT_done", b, 1))
                pe.wait_ge(S["tok_done"], n("tok_done", b, 1))
                for i in range(2):
                    ps = free(pe, now, b, ("routed", i))
                    rows = slice(i * C, i * C + C)
                    for t in (i, i + 2):
                        last = pe.matmul(ps[:, (t // 2) * D:(t // 2) * D + D], routeT[rows, t // 2, :], tok[rows, :],
                                         start=True, stop=True)
                    last.then_inc(filled(now, ("routed", i)), 1)

            def gate(use, w, first, first_ready, kts, starts=True, ends=True):
                def step(b, f):
                    ring, k, _, _ = PLACE[now.phase, (use, f)]
                    ps = free(pe, now, b, (use, f)) if starts else TILES[ring][k]
                    for kt in kts:
                        rhs, ready, c = ((first, first_ready, kt + 1) if kt < NF else (hT, "inn_done", kt - NF + 1))
                        if f == 0:
                            pe.wait_ge(S[ready], n(ready, b, c))
                        last = pe.matmul(ps[:, :], w[:, kt, f * P:f * P + P], rhs[:, kt % NF, :],
                                         start=(starts and kt == kts[0]), stop=(ends and kt == kts[-1]))
                    if ends:
                        last.then_inc(filled(now, (use, f)), 1)
                return step

            def new_turn(b, _):
                for i in range(2):
                    ps = free(pe, now, b, ("new", i))
                    if i == 0:
                        pe.wait_ge(S["new_done"], n("new_done", b, NF))
                    for t in (2 * i, 2 * i + 1):
                        for f in range(NF):
                            at = (t % 2) * D + f * P
                            last = pe.transpose(ps[:, at:at + P], cand[:, f, t * P:t * P + P], ident[:, :])
                    last.then_inc(filled(now, ("new", i)), 1)

            run(pe, now, {
                "ln1T": turn("ln1T", x_ln, "ln1_norm"), "ln2T": turn("ln2T", xh, "ln2_norm"),
                "ln3T": turn("ln3T", xh, "ln3_norm"), "psnT": turn("psnT", xh, "psn_norm"),
                "innT": turn("innT", xh, "inn_norm"), "xT": turn("xT", xs, "x3_done"),
                "q": project_T("q", wqkv, 0, hT_a, "h1"), "k": project_T("k", wqkv, D, hT_a, "h1"),
                "q2": project_T("q2", wq_ca, 0, hT, "h2"), "v": values, "ctxT": ctx_turn,
                "k2": ctx_features("k2", wkv_ca), "tokT": ctx_features("tokT", wtok),
                "v2": ctx_rows("v2", wkv_ca, D), "tok": ctx_rows("tok", wtok, 0),
                "max": scores, "max2": scores2, "negm": turn_max("negmT", "nm_lo_done"),
                "negm2": turn_max("negm2T", "nm2_lo_done"), "st": scores_T, "pv": weigh, "st2": scores2_T,
                "pv2": weigh2, 
                "proj": project_out("proj", wproj_sa, attT, "att_done"),
                "proj2": project_out("proj2", wproj_ca, att2T, "att2_done"),
                "prepare": prepare, "ff1": hidden, "ff2": hidden_out, "route": route_scores, "routeT": route_turn,
                "routed": route_tokens, "ra": gate("r", w_r, psnT, "psn_done", (0, 1), ends=False),
                "rb": gate("r", w_r, psnT, "psn_done", (2, 3), starts=False),
                "u": gate("u", w_u, psnT, "psn_done", (0, 1, 2, 3)),
                "n": gate("n", w_n, t_r, "rp_done", (2, 3, 0, 1)), "new": new_turn,
            })


_OUTS = [((16, 512, 256), 'float32')]


def kernel(**inputs):
    import numpy as _np
    import concourse.bacc as _bacc
    from concourse import mybir as _mybir
    from concourse.bass_utils import run_bass_kernel_spmd as _run

    names = ["x", "ctx_768"] + [f"L0_xattn_{w}" for w in (
        "Wqkv", "Wproj_sa", "bproj_sa", "g1", "b1", "Wq_ca", "Wkv_ca", "Wproj_ca", "bproj_ca", "g2", "b2", "Wff1",
        "bff1", "Wff2", "bff2", "g3", "b3")] + [f"L1_xattn_{w}" for w in (
            "W_proj", "b_proj", "g_state", "beta_state", "g_input", "beta_input", "g_out", "beta_out", "W_u", "b_u",
            "W_r", "b_r", "W_n", "b_n")]
    nc = _bacc.Bacc("TRN2", target_bir_lowering=False, num_devices=1)
    arrays, args = {}, []
    for name in names:
        a = _np.ascontiguousarray(inputs[name])
        arrays[f"in_{name}_dram"] = a
        args.append(nc.dram_tensor(f"in_{name}_dram", a.shape, _mybir.dt.from_np(a.dtype), kind="ExternalInput").ap())
    for i, (shape, dtype) in enumerate(_OUTS):
        dt = _mybir.dt.from_np(_np.dtype(dtype))
        args.append(nc.dram_tensor(f"out_{i}_dram", shape, dt, kind="ExternalOutput").ap())
    build(nc, *args)
    r = _run(nc, [arrays], core_ids=[0])
    return r.results[0]["out_0_dram"]
```
